# Optimizing a Trainium2 kernel written in Bass

```python
import numpy as np
import jax
import jax.numpy as jnp

def _softmax(x, axis=-1):
    return jax.nn.softmax(x, axis=axis)

def _gelu(x):
    return jax.nn.gelu(x, approximate=True)

def _silu(x):
    return jax.nn.silu(x)

def _sigmoid(x):
    return jax.nn.sigmoid(x)

def _layernorm(x, axis=-1, eps=1e-05):
    m = jnp.mean(x, axis=axis, keepdims=True)
    v = jnp.var(x, axis=axis, keepdims=True)
    return (x - m) / jnp.sqrt(v + eps)

def _scatter_add(tgt, idx, src, axis=0):
    return tgt.at[idx].add(src)

def _segment_sum(src, seg, n):
    return jax.ops.segment_sum(src, seg, n)
kernel_name = 'mk_cond_resid_d4_seqx_r8_aa66ef'

def setup_inputs(seed: int=0):
    np.random.seed(seed)
    _w = jnp.asarray

    def _rec_inputs():
        import jax
        import jax.numpy as jnp
        _rk = jax.random.key(seed)
        x = -0.000125 + 0.9999 * jax.random.normal(jax.random.fold_in(_rk, 1), (8, 128, 512), jnp.float32)
        _lenS = 128 - jax.random.randint(jax.random.fold_in(_rk, 7), (8,), 0, max(1, 128 // 4) + 1, jnp.int32)
        _lenS2 = 128 - jax.random.randint(jax.random.fold_in(_rk, 8), (8,), 0, max(1, 128 // 4) + 1, jnp.int32)
        itok_B_0_7 = jax.random.randint(jax.random.fold_in(_rk, 11), (8,), 0, 8, jnp.int32)
        itok_B_2_6 = jax.random.randint(jax.random.fold_in(_rk, 12), (8,), 2, 7, jnp.int32)
        itok_B_0_23 = jax.random.randint(jax.random.fold_in(_rk, 13), (8,), 0, 24, jnp.int32)
        itok_Bx16_0_63 = jax.random.randint(jax.random.fold_in(_rk, 14), (8, 16), 0, 64, jnp.int32)
        itok_B_207_1644 = jax.random.randint(jax.random.fold_in(_rk, 15), (8,), 207, 1645, jnp.int32)
        return (x, itok_B_0_7, itok_B_2_6, itok_B_0_23, itok_Bx16_0_63, itok_B_207_1644)
    x, itok_B_0_7, itok_B_2_6, itok_B_0_23, itok_Bx16_0_63, itok_B_207_1644 = _rec_inputs()

    def _L0_cond_setup():
        import jax, jax.numpy as jnp
        import numpy as np
        TOP_K = 2
        LANG_BIAS = 5.0
        SCALING = 32.0 / 16.0
        LANGUAGE_PAD_ID = -1
        key = jax.random.key(seed)
        ks = jax.random.split(key, 6)
        B, T, D, O, E, R = (4, 256, 512, 512, 8, 16)
        x = jax.random.normal(ks[0], (B, T, D), dtype=jnp.float32)
        language_ids = jax.random.randint(ks[1], (B,), 0, E).astype(jnp.int64)
        W = jax.random.normal(ks[2], (O, D), dtype=jnp.float32) * (1.0 / np.sqrt(D))
        Wr = jax.random.normal(ks[3], (E, D), dtype=jnp.float32) * (1.0 / np.sqrt(D))
        A = jax.random.normal(ks[4], (E, R, D), dtype=jnp.float32) * (1.0 / np.sqrt(D))
        Bm = jax.random.normal(ks[5], (O, R), dtype=jnp.float32) * 0.0
        Bm = jnp.broadcast_to(Bm, (E, O, R)) + jax.random.normal(ks[5], (E, O, R), dtype=jnp.float32) * 0.02
        return {'x': x, 'language_ids': language_ids, 'W': W, 'Wr': Wr, 'A': A, 'B': Bm}
    _L0_cond_all = _L0_cond_setup()
    _L0_cond_in = {k: v for k, v in _L0_cond_all.items() if k in ('W', 'Wr', 'A', 'B')}
    del _L0_cond_all

    def _L1_cond_setup():
        import jax, jax.numpy as jnp
        import numpy as np
        B, N, H, F = (4, 64, 512, 1376)
        L, R, RANK = (1, 16, 16)
        SCALE = 0.5
        key = jax.random.key(seed)
        ks = jax.random.split(key, 12)
        nrm = lambda k, shape, fan: jax.random.normal(k, shape, jnp.float32) * fan ** (-0.5)
        inp = {'x': jax.random.normal(ks[0], (B, N, H), jnp.float32), 'W_gate': nrm(ks[1], (F, H), H), 'W_up': nrm(ks[2], (F, H), H), 'W_down': nrm(ks[3], (H, F), F), 'A_gate': nrm(ks[4], (L, R, RANK, H), H), 'B_gate': nrm(ks[5], (L, R, F, RANK), RANK), 'A_up': nrm(ks[6], (L, R, RANK, H), H), 'B_up': nrm(ks[7], (L, R, F, RANK), RANK), 'A_down': nrm(ks[8], (L, R, RANK, F), F), 'B_down': nrm(ks[9], (L, R, H, RANK), RANK), 'lora_indices': jax.random.randint(ks[10], (B,), 0, R), 'layer_idx': 0}
        return inp
    _L1_cond_all = _L1_cond_setup()
    _L1_cond_in = {k: v for k, v in _L1_cond_all.items() if k in ('W_gate', 'W_up', 'W_down', 'A_gate', 'B_gate', 'A_up', 'B_up', 'A_down', 'B_down')}
    del _L1_cond_all

    def _L2_cond_setup():
        import jax, jax.numpy as jnp
        import numpy as np
        R = 16
        ALPHA = 32
        SCALING = ALPHA / R
        SLOTS = 32
        IN_F = 512
        OUT_F = 512
        B, T = (8, 128)
        key = jax.random.key(seed)
        k1, k2, k3, k4, k5, k6 = jax.random.split(key, 6)
        x = jax.random.normal(k1, (B, T, IN_F), dtype=jnp.float32)
        adapter_mapping = jax.random.randint(k2, (B,), 0, SLOTS, dtype=jnp.int32)
        W = jax.random.normal(k3, (OUT_F, IN_F), dtype=jnp.float32) * 0.02
        b = jax.random.normal(k4, (OUT_F,), dtype=jnp.float32) * 0.02
        lora_As = jax.random.normal(k5, (SLOTS, IN_F, R), dtype=jnp.float32) * 0.02
        lora_Bs = jax.random.normal(k6, (SLOTS, R, OUT_F), dtype=jnp.float32) * 0.02
        return {'x': x, 'adapter_mapping': adapter_mapping, 'W': W, 'b': b, 'lora_As': lora_As, 'lora_Bs': lora_Bs}
    _L2_cond_all = _L2_cond_setup()
    _L2_cond_in = {k: v for k, v in _L2_cond_all.items() if k in ('W', 'b', 'lora_As', 'lora_Bs')}
    del _L2_cond_all

    def _L3_cond_setup():
        import jax, jax.numpy as jnp
        import numpy as np
        B, S, HID = (4, 128, 512)
        D, HQ, HK = (128, 32, 8)
        PAGES, PSIZE, NPP = (64, 32, 16)
        THETA = 10000.0
        EPS = 1e-06
        SCALE = 1.0 / float(np.sqrt(D))

        def _rmsnorm(t, w):
            var = jnp.mean(t * t, axis=-1, keepdims=True)
            return t * jax.lax.rsqrt(var + EPS) * w

        def _rope(t, pos):
            inv_freq = 1.0 / THETA ** (jnp.arange(0, D, 2, dtype=jnp.float32) / D)
            freqs = pos[..., None].astype(jnp.float32) * inv_freq
            cos = jnp.cos(freqs)[:, :, None, :]
            sin = jnp.sin(freqs)[:, :, None, :]
            t1, t2 = (t[..., :D // 2], t[..., D // 2:])
            return jnp.concatenate([t1 * cos - t2 * sin, t2 * cos + t1 * sin], axis=-1)
        key = jax.random.key(seed)
        ks = jax.random.split(key, 10)
        x = jax.random.normal(ks[0], (B, S, HID), jnp.float32)
        Wq = jax.random.normal(ks[1], (HQ * D, HID), jnp.float32) * 0.02
        Wk = jax.random.normal(ks[2], (HK * D, HID), jnp.float32) * 0.02
        Wv = jax.random.normal(ks[3], (HK * D, HID), jnp.float32) * 0.02
        Wo = jax.random.normal(ks[4], (HID, HQ * D), jnp.float32) * 0.02
        q_norm_w = jax.random.uniform(ks[5], (D,), jnp.float32)
        k_norm_w = jax.random.uniform(ks[6], (D,), jnp.float32)
        k_cache = jax.random.normal(ks[7], (PAGES, PSIZE, HK, D), jnp.float32)
        v_cache = jax.random.normal(ks[8], (PAGES, PSIZE, HK, D), jnp.float32)
        block_table = jnp.arange(B * NPP, dtype=jnp.int32).reshape(B, NPP)
        cache_seqlens = jax.random.randint(ks[9], (B,), 0, 475).astype(jnp.int32)
        return dict(x=x, Wq=Wq, Wk=Wk, Wv=Wv, Wo=Wo, q_norm_w=q_norm_w, k_norm_w=k_norm_w, k_cache=k_cache, v_cache=v_cache, block_table=block_table, cache_seqlens=cache_seqlens)
    _L3_cond_all = _L3_cond_setup()
    _L3_cond_in = {k: v for k, v in _L3_cond_all.items() if k in ('Wq', 'Wk', 'Wv', 'Wo', 'q_norm_w', 'k_norm_w', 'k_cache', 'v_cache')}
    del _L3_cond_all
    return {'x': x, 'itok_B_0_7': itok_B_0_7, 'itok_B_2_6': itok_B_2_6, 'itok_B_0_23': itok_B_0_23, 'itok_Bx16_0_63': itok_Bx16_0_63, 'itok_B_207_1644': itok_B_207_1644, 'L0_cond_W': _L0_cond_in['W'], 'L0_cond_Wr': _L0_cond_in['Wr'], 'L0_cond_A': _L0_cond_in['A'], 'L0_cond_B': _L0_cond_in['B'], 'L1_cond_W_gate': _L1_cond_in['W_gate'], 'L1_cond_W_up': _L1_cond_in['W_up'], 'L1_cond_W_down': _L1_cond_in['W_down'], 'L1_cond_A_gate': _L1_cond_in['A_gate'], 'L1_cond_B_gate': _L1_cond_in['B_gate'], 'L1_cond_A_up': _L1_cond_in['A_up'], 'L1_cond_B_up': _L1_cond_in['B_up'], 'L1_cond_A_down': _L1_cond_in['A_down'], 'L1_cond_B_down': _L1_cond_in['B_down'], 'L2_cond_W': _L2_cond_in['W'], 'L2_cond_b': _L2_cond_in['b'], 'L2_cond_lora_As': _L2_cond_in['lora_As'], 'L2_cond_lora_Bs': _L2_cond_in['lora_Bs'], 'L3_cond_Wq': _L3_cond_in['Wq'], 'L3_cond_Wk': _L3_cond_in['Wk'], 'L3_cond_Wv': _L3_cond_in['Wv'], 'L3_cond_Wo': _L3_cond_in['Wo'], 'L3_cond_q_norm_w': _L3_cond_in['q_norm_w'], 'L3_cond_k_norm_w': _L3_cond_in['k_norm_w'], 'L3_cond_k_cache': _L3_cond_in['k_cache'], 'L3_cond_v_cache': _L3_cond_in['v_cache']}

def reference(x, itok_B_0_7, itok_B_2_6, itok_B_0_23, itok_Bx16_0_63, itok_B_207_1644, L0_cond_W, L0_cond_Wr, L0_cond_A, L0_cond_B, L1_cond_W_gate, L1_cond_W_up, L1_cond_W_down, L1_cond_A_gate, L1_cond_B_gate, L1_cond_A_up, L1_cond_B_up, L1_cond_A_down, L1_cond_B_down, L2_cond_W, L2_cond_b, L2_cond_lora_As, L2_cond_lora_Bs, L3_cond_Wq, L3_cond_Wk, L3_cond_Wv, L3_cond_Wo, L3_cond_q_norm_w, L3_cond_k_norm_w, L3_cond_k_cache, L3_cond_v_cache):
    import jax
    import jax.numpy as jnp

    def _L0_cond_ref(x, language_ids, W, Wr, A, B):
        import jax, jax.numpy as jnp
        import numpy as np
        TOP_K = 2
        LANG_BIAS = 5.0
        SCALING = 32.0 / 16.0
        LANGUAGE_PAD_ID = -1
        base = jnp.einsum('btd,od->bto', x, W)
        E = Wr.shape[0]
        logits = jnp.einsum('btd,ed->bte', x.astype(jnp.float32), Wr.astype(jnp.float32))
        expert_targets = language_ids
        valid = expert_targets >= 0
        tgt = jnp.where(valid, expert_targets, 0)
        bias = jax.nn.one_hot(tgt, E, dtype=logits.dtype) * LANG_BIAS
        bias = jnp.where(valid[:, None], bias, 0.0)
        logits = logits + bias[:, None, :]
        topw, topi = jax.lax.top_k(logits, TOP_K)
        weights = jax.nn.softmax(topw, axis=-1)
        gates = jnp.sum(jax.nn.one_hot(topi, E, dtype=weights.dtype) * weights[..., None], axis=-2)
        gates = gates.astype(x.dtype)
        h = jnp.einsum('btd,erd->bter', x, A)
        lora_out = jnp.einsum('bter,bte,eor->bto', h, gates, B)
        return base + SCALING * lora_out

    def _L1_cond_ref(x, W_gate, W_up, W_down, A_gate, B_gate, A_up, B_up, A_down, B_down, lora_indices, layer_idx):
        import jax, jax.numpy as jnp
        import numpy as np
        B, N, H, F = (4, 64, 512, 1376)
        L, R, RANK = (1, 16, 16)
        SCALE = 0.5

        def lora_add(base, inp, A, B):
            Ab = A[layer_idx][lora_indices]
            Bb = B[layer_idx][lora_indices]
            t = jnp.einsum('bri,bni->bnr', Ab, inp)
            return base + jnp.einsum('bor,bnr->bno', Bb, t) * SCALE
        gate = lora_add(jnp.einsum('bnh,fh->bnf', x, W_gate), x, A_gate, B_gate)
        up = lora_add(jnp.einsum('bnh,fh->bnf', x, W_up), x, A_up, B_up)
        act = jax.nn.silu(gate) * up
        down = lora_add(jnp.einsum('bnf,hf->bnh', act, W_down), act, A_down, B_down)
        return down

    def _L2_cond_ref(x, adapter_mapping, W, b, lora_As, lora_Bs):
        import jax, jax.numpy as jnp
        import numpy as np
        R = 16
        ALPHA = 32
        SCALING = ALPHA / R
        SLOTS = 32
        IN_F = 512
        OUT_F = 512
        B, T = (8, 128)
        base_out = jnp.einsum('bti,oi->bto', x, W) + b
        A = lora_As[adapter_mapping]
        Bm = lora_Bs[adapter_mapping]
        lora_h = jnp.einsum('bti,bir->btr', x, A)
        lora_out = jnp.einsum('btr,bro->bto', lora_h, Bm)
        return base_out + lora_out * SCALING

    def _L3_cond_ref(x, Wq, Wk, Wv, Wo, q_norm_w, k_norm_w, k_cache, v_cache, block_table, cache_seqlens):
        import jax, jax.numpy as jnp
        import numpy as np
        B, S, HID = (4, 128, 512)
        D, HQ, HK = (128, 32, 8)
        PAGES, PSIZE, NPP = (64, 32, 16)
        THETA = 10000.0
        EPS = 1e-06
        SCALE = 1.0 / float(np.sqrt(D))

        def _rmsnorm(t, w):
            var = jnp.mean(t * t, axis=-1, keepdims=True)
            return t * jax.lax.rsqrt(var + EPS) * w

        def _rope(t, pos):
            inv_freq = 1.0 / THETA ** (jnp.arange(0, D, 2, dtype=jnp.float32) / D)
            freqs = pos[..., None].astype(jnp.float32) * inv_freq
            cos = jnp.cos(freqs)[:, :, None, :]
            sin = jnp.sin(freqs)[:, :, None, :]
            t1, t2 = (t[..., :D // 2], t[..., D // 2:])
            return jnp.concatenate([t1 * cos - t2 * sin, t2 * cos + t1 * sin], axis=-1)
        bsz, seqlen, _ = x.shape
        q = jnp.einsum('bsd,ed->bse', x, Wq).reshape(bsz, seqlen, HQ, D)
        k = jnp.einsum('bsd,ed->bse', x, Wk).reshape(bsz, seqlen, HK, D)
        v = jnp.einsum('bsd,ed->bse', x, Wv).reshape(bsz, seqlen, HK, D)
        q = _rmsnorm(q, q_norm_w)
        k = _rmsnorm(k, k_norm_w)
        pos = cache_seqlens[:, None] + jnp.arange(seqlen)[None, :]
        q = _rope(q, pos)
        k = _rope(k, pos)
        L = NPP * PSIZE
        kc = k_cache[block_table].reshape(bsz, L, HK, D)
        vc = v_cache[block_table].reshape(bsz, L, HK, D)
        k_all = jnp.concatenate([kc, k], axis=1)
        v_all = jnp.concatenate([vc, v], axis=1)
        valid_c = jnp.arange(L)[None, :] < cache_seqlens[:, None]
        valid = jnp.concatenate([valid_c, jnp.ones((bsz, seqlen), dtype=bool)], axis=1)
        rep = HQ // HK
        k_all = jnp.repeat(k_all, rep, axis=2)
        v_all = jnp.repeat(v_all, rep, axis=2)
        scores = jnp.einsum('bqhd,bkhd->bhqk', q, k_all) * SCALE
        scores = jnp.where(valid[:, None, None, :], scores, -1e+30)
        probs = jax.nn.softmax(scores, axis=-1)
        o = jnp.einsum('bhqk,bkhd->bqhd', probs, v_all)
        o = o.reshape(bsz, seqlen, HQ * D)
        return jnp.einsum('bse,de->bsd', o, Wo)
    x = x + _L0_cond_ref(x, itok_B_0_7, L0_cond_W, L0_cond_Wr, L0_cond_A, L0_cond_B)
    x = x + _L1_cond_ref(x, L1_cond_W_gate, L1_cond_W_up, L1_cond_W_down, L1_cond_A_gate, L1_cond_B_gate, L1_cond_A_up, L1_cond_B_up, L1_cond_A_down, L1_cond_B_down, itok_B_2_6, 0)
    x = x + _L2_cond_ref(x, itok_B_0_23, L2_cond_W, L2_cond_b, L2_cond_lora_As, L2_cond_lora_Bs)
    x = x + _L3_cond_ref(x, L3_cond_Wq, L3_cond_Wk, L3_cond_Wv, L3_cond_Wo, L3_cond_q_norm_w, L3_cond_k_norm_w, L3_cond_k_cache, L3_cond_v_cache, itok_Bx16_0_63, itok_B_207_1644)
    return x

_drawn_inputs = setup_inputs


def setup_inputs(seed=0):
    import zlib

    import numpy as np

    out = dict(_drawn_inputs(seed))
    spreads = {}
    factors = {'L0_cond_Wr': 4.449,
     'L2_cond_b': 8.0,
     'L3_cond_Wq': 4.515,
     'L3_cond_Wk': 8.0,
     'L3_cond_Wv': 4.735,
     'L3_cond_q_norm_w': 7.874,
     'L3_cond_k_norm_w': 8.0,
     'L3_cond_k_cache': 4.808,
     'L3_cond_v_cache': 2.667}
    for name, (base, spread) in spreads.items():
        noise = np.random.default_rng([zlib.crc32(name.encode()), seed]).standard_normal(out[name].shape)
        drawn = base * np.exp(spread * noise) if base else spread * noise
        out[name] = jnp.asarray(drawn.astype(out[name].dtype))
    for name, factor in factors.items():
        out[name] = (out[name] * factor).astype(out[name].dtype)
    return out
```

```python
import concourse.bass as bass
from concourse import mybir
from contextlib import ExitStack
import numpy as np

P = 128
NB, T, D = 8, 128, 512
NT = NB * T
C = D // P
HALF = 512
E, R = 8, 16
F = 1376
FC = (F + P - 1) // P
FR = F - (FC - 1) * P
FG = F // R
HQ, HK, DH = 32, 8, 128
REP = HQ // HK
PAGES, PSIZE, NPP = 64, 32, 16
L = NPP * PSIZE
KC = L // P
KEYS = L + T
NGP = HK // 2
UNITS = 2 * NB
EPS = 1e-6
SCALE = 1.0 / float(np.sqrt(DH))
NEG = -1e30
TWO_PI = 2.0 * np.pi
ROUND = 1.5 * 2.0 ** 23
C1 = 6.28125
C2 = float(np.float32(TWO_PI - C1))
C3 = float(TWO_PI - C1 - np.float64(np.float32(TWO_PI - C1)))
K_ID, K_BM, K_IO, K_E, K_FR, K_P, K_END = 0, 128, 136, 648, 656, 720, 721


def constants():
    k = np.zeros((P, K_END), np.float32)
    k[:, K_ID:K_BM] = np.eye(P)
    k[:, K_BM:K_IO] = np.arange(P)[:, None] // R == np.arange(NB)[None]
    k[:, K_IO:K_E] = np.arange(L)[None]
    k[:, K_E:K_FR] = np.arange(E)[None]
    k[:, K_FR:K_P] = (np.float32(1.0) / np.power(np.float32(10000.0), np.arange(0, DH, 2, dtype=np.float32) / np.float32(DH)))[None]
    k[:, K_P] = np.arange(P)
    return k


fp32, i32, u32 = mybir.dt.float32, mybir.dt.int32, mybir.dt.uint32
ALU = mybir.AluOpType
ACT = mybir.ActivationFunctionType
AX = mybir.AxisListType


def build(nc, a, out):
    with ExitStack() as ctx:
        def sb(name, shape, dt=fp32):
            return ctx.enter_context(nc.sbuf_tensor(name, shape, dt))

        const = sb("const", [P, K_END])
        xT = sb("xT", [P, C, NT])
        ints = sb("ints", [P, 2, NB], i32)
        q_w = sb("q_w", [P, DH])
        k_w = sb("k_w", [P, DH])
        banks = ctx.enter_context(nc.psum_tensor("banks", [P, 8, 512], fp32))
        layers012(nc, a, const, xT, ints, q_w, k_w, banks)
        attention(nc, a, out, const, xT, ints, q_w, k_w, banks)


def layers012(nc, a, const, xT_b, ints, q_w, k_w, banks):
    ident = const[:, K_ID:K_BM]
    blockmask = const[:, K_BM:K_IO]

    def bank(n):
        return banks[:, n, :]

    with ExitStack() as part1:
        ctx = part1

        def sb(name, shape, dt=fp32, stack=ctx):
            return stack.enter_context(nc.sbuf_tensor(name, shape, dt))

        def sem(name):
            return ctx.enter_context(nc.semaphore(name))

        xT_a = sb("xT_a", [P, C, NT], stack=part1)
        RAW = 8
        raw = sb("raw", [P, RAW, C, P], stack=part1)
        w0T = sb("w0T", [P, C, D], stack=part1)
        w2T = sb("w2T", [P, C, D], stack=part1)
        wrT = sb("wrT", [P, C, E], stack=part1)
        wgT = sb("wgT", [P, C, F], stack=part1)
        wuT = sb("wuT", [P, C, F], stack=part1)
        wdT = sb("wdT", [P, FC, D], stack=part1)
        a0T = sb("a0T", [P, C, P], stack=part1)
        agT = sb("agT", [P, C, P], stack=part1)
        auT = sb("auT", [P, C, P], stack=part1)
        adT = sb("adT", [P, FC, P], stack=part1)
        a2T = sb("a2T", [P, C, P], stack=part1)
        b0T = sb("b0T", [P, D], stack=part1)
        bgT = sb("bgT", [P, F], stack=part1)
        buT = sb("buT", [P, F], stack=part1)
        bdT = sb("bdT", [P, D], stack=part1)
        b2R = sb("b2R", [P, D], stack=part1)
        bias2 = sb("bias2", [P, C], stack=part1)
        rank_act = sb("rank_act", [P, 2, HALF * 2], stack=part1)
        area = sb("area", [P, 2 * D + F + 2 * NB * 256 + D + 64], stack=part1)
        o = 0
        ag_raw = area[:, o:o + D]; o += D
        au_raw = area[:, o:o + D]; o += D
        ad_raw = area[:, o:o + F]; o += F
        bg_raw = area[:, o:o + NB * 256].rearrange("p (b s r) -> p b s r", b=NB, s=R); o += NB * 256
        bu_raw = area[:, o:o + NB * 256].rearrange("p (b s r) -> p b s r", b=NB, s=R); o += NB * 256
        bd_raw = area[:, o:o + D].rearrange("p (b s r) -> p b s r", b=NB, s=4)
        act_T = area[:, 0:FC * HALF].rearrange("p (f t) -> p f t", f=FC)
        silu = raw[:, 0:2, :, :].rearrange("p a c t -> p a (c t)")
        logit = sb("logit", [P, NB, E], stack=part1)
        top = sb("top", [P, NB, E], stack=part1)
        topi = sb("topi", [P, NB, E], u32, stack=part1)
        rt = sb("rt", [P, 6, NB, E], stack=part1)
        gate16 = rank_act[:, 1, :].rearrange("p (t e r) -> p t e r", t=NB, e=E)

        b0_sorted = wdT[:, 0, :].rearrange("p (s b r) -> p s b r", b=NB, r=R)
        bd_sorted = w2T[:, 0, :].rearrange("p (s b r) -> p s b r", b=NB, r=R)
        bg_sorted = wgT[:, :, :].rearrange("p c f -> p (c f)")[:, 0:NB * 256].rearrange("p (s b r) -> p s b r", b=NB, r=R)
        bu_sorted = wuT[:, :, :].rearrange("p c f -> p (c f)")[:, 0:NB * 256].rearrange("p (s b r) -> p s b r", b=NB, r=R)
        sorted_rows = {"b0": b0_sorted, "bd": bd_sorted, "bg": bg_sorted, "bu": bu_sorted}

        b0_in_order, b_in_order = sem("b0_in_order"), sem("b_in_order")
        consts_in, small_in = sem("consts_in"), sem("small_in")
        raw_in = [sem(f"raw_in{s}") for s in range(RAW)]
        gath_in = sem("gath_in")
        tr_filled = [sem("tr_filled0"), sem("tr_filled1")]
        tr_evac = [sem("tr_evac0"), sem("tr_evac1")]
        dve_step = sem("dve_step")
        router_in, router_exp, gates_ready = sem("router_in"), sem("router_exp"), sem("gates_ready")
        router_d = sem("router_d")
        gateT_filled, gateT_evac = sem("gateT_filled"), sem("gateT_evac")
        rank_filled, rank_evac = sem("rank_filled"), sem("rank_evac")
        lin_filled, lin_evac = sem("lin_filled"), sem("lin_evac")
        gu_filled, silu_done, gu_evac = sem("gu_filled"), sem("silu_done"), sem("gu_evac")

        def rows(src, n, m=P):
            return src[n * P:n * P + m, :]

        def blockwise(dst, n, m=P):
            return dst[:, :, n * P:n * P + m]

        groups = []
        for t in range(NB):
            groups.append(("x", t))
        for n in range(C):
            groups.append(("w0", n))
        groups += [("a0", 0), ("b0", 0), ("wr", 0)]
        END0 = len(groups)
        groups += [("ag", 0), ("au", 0)] + [("bg", n) for n in range(4)] + [("bu", n) for n in range(4)]
        for n in range(FC):
            groups += [("wg", n), ("wu", n)]
        for n in range(FC):
            groups.append(("wd", n))
        groups += [("ad", n) for n in range(3)] + [("bd", 0)]
        groups += [("w2", n) for n in range(C)]
        END1 = len(groups)
        ring = {}
        for g, (kind, n) in enumerate(groups):
            if kind not in ("ag", "au", "bg", "bu", "ad", "bd"):
                ring[g] = len(ring)
        ring_groups = {v: k for k, v in ring.items()}

        def fr(n):
            return P if n < FC - 1 else FR

        def load_of(g):
            kind, n = groups[g]
            s = raw[:, ring[g] % RAW, :, :]
            flat = s.rearrange("p c t -> p (c t)")
            if kind == "x":
                return flat, a["x"][n, :, :]
            if kind == "w0":
                return flat, rows(a["L0_cond_W"], n)
            if kind == "w2":
                return flat, rows(a["L2_cond_W"], n)
            if kind == "a0":
                return flat, a["L0_cond_A"].rearrange("e r d -> (e r) d")
            if kind == "b0":
                return s.rearrange("p c t -> p (c t)").rearrange("p (e k) -> p e k", e=E), \
                    a["L0_cond_B"].rearrange("e (g s) r -> g e (s r)", s=4)
            if kind == "wr":
                return flat[0:E, :], a["L0_cond_Wr"]
            if kind in ("wg", "wu"):
                return flat[0:fr(n), :], rows(a["L1_cond_W_gate" if kind == "wg" else "L1_cond_W_up"], n, fr(n))
            if kind == "wd":
                return s[:, :, 0:fr(n)], a["L1_cond_W_down"].rearrange("(c p) f -> p c f", p=P)[:, :, n * P:n * P + fr(n)]

        def transposes_of(g):
            kind, n = groups[g]
            b = banks[:, g % 2, :]
            if g in ring:
                s = raw[:, ring[g] % RAW, :, :]
            if kind in ("x", "w0", "w2", "a0", "wr", "wg", "wu", "ag", "au"):
                k = {"wr": E, "wg": fr(n), "wu": fr(n)}.get(kind, P)
                dst = {"x": xT_a, "w0": w0T, "w2": w2T, "a0": a0T, "wr": wrT, "wg": wgT, "wu": wuT, "ag": agT, "au": auT}[kind]
                src = {"ag": ag_raw, "au": au_raw}.get(kind)
                if src is None:
                    src = s.rearrange("p c t -> p (c t)")
                v = b.rearrange("p (c t) -> p c t", c=C)
                return [(src[0:k, c * P:(c + 1) * P], k, v[:, c, 0:k]) for c in range(C)], \
                    blockwise(dst, n, k), v[:, :, 0:k]
            if kind == "wd":
                m = fr(n)
                return [(s[:, c, 0:m], P, b[0:m, c * P:(c + 1) * P]) for c in range(C)], wdT[0:m, n, :], b[0:m, :]
            if kind == "ad":
                blocks = list(range(4 * n, min(4 * n + 4, FC)))
                full = [f for f in blocks if fr(f) == P]
                tr = [(ad_raw[:, f * P:f * P + fr(f)], P, b[0:fr(f), (f - 4 * n) * P:(f - 4 * n + 1) * P]) for f in blocks]
                return tr, adT[:, 4 * n:4 * n + len(full), :], b[:, 0:len(full) * P].rearrange("p (c t) -> p c t", t=P)
            if kind in ("b0", "bd"):
                s4 = sorted_rows[kind]
                dst = (bdT if kind == "bd" else b0T)[:, :].rearrange("p (g s) -> p s g", s=4)
                v = b.rearrange("p (s g) -> p s g", s=4)
                return [(s4[:, f, :, :], P, v[:, f, :]) for f in range(4)], dst, v
            if kind in ("bg", "bu"):
                s4 = sorted_rows[kind]
                dst = (bgT if kind == "bg" else buT)[:, :].rearrange("p (g s) -> p s g", s=R)[:, 4 * n:4 * n + 4, :]
                v = b[:, 0:4 * P].rearrange("p (s g) -> p s g", s=4)
                return [(s4[0:FG, 4 * n + f, :, :], FG, v[:, f, 0:FG]) for f in range(4)], dst, v[:, :, 0:FG]

        AD_TAIL = [g for g, (k, n) in enumerate(groups) if k == "ad" and 4 * n + 4 > FC - 1][0]

        GATHERED = 16 * (6 * NB + 2 * NB)
        block = ctx.enter_context(nc.Block())

        @block.sync
        def _(sp):
            sp.dma_start(const[:, :], a["shape_constants"]).then_inc(consts_in, 16)
            for k, g in sorted(ring_groups.items()):
                if k >= RAW:
                    prev = ring_groups[k - RAW]
                    sp.wait_ge(tr_filled[prev % 2], prev // 2 + 1)
                dst, src = load_of(g)
                sp.dma_start(dst, src).then_inc(raw_in[k % RAW], 16)

        @block.gpsimd
        def _(pool):
            for n, name in enumerate(("itok_B_0_7", "itok_B_207_1644")):
                pool.dma_start(ints[:, n, :], a[name].rearrange("(o b) -> o b", o=1).to_broadcast([P, NB])).then_inc(small_in, 16)
            pool.dma_start(q_w[:, :], a["L3_cond_q_norm_w"].rearrange("(o b) -> o b", o=1).to_broadcast([P, DH])).then_inc(small_in, 16)
            pool.dma_start(k_w[:, :], a["L3_cond_k_norm_w"].rearrange("(o b) -> o b", o=1).to_broadcast([P, DH])).then_inc(small_in, 16)
            pool.dma_start(bias2[:, :], a["L2_cond_b"].rearrange("(c p) -> p c", p=P), allow_slow_non_contiguous=True).then_inc(small_in, 16)
            idx = a["itok_B_2_6"].rearrange("(o b) -> o b", o=1)
            for b in range(NB):
                k = pool.value_load(idx[0:1, b:b + 1], min_val=0, max_val=15)
                rb = slice(R * b, R * b + R)

                def row(name):
                    return a[name][0][bass.ds(k, 1)].rearrange("o r d -> (o r) d")
                pool.dma_start(ag_raw[rb, :], row("L1_cond_A_gate")).then_inc(gath_in, 16)
                pool.dma_start(au_raw[rb, :], row("L1_cond_A_up")).then_inc(gath_in, 16)
                pool.dma_start(ad_raw[rb, :], row("L1_cond_A_down")).then_inc(gath_in, 16)
                pool.dma_start(bg_raw[0:FG, b, :, :], row("L1_cond_B_gate").rearrange("(g s) r -> g s r", s=R)).then_inc(gath_in, 16)
                pool.dma_start(bu_raw[0:FG, b, :, :], row("L1_cond_B_up").rearrange("(g s) r -> g s r", s=R)).then_inc(gath_in, 16)
                pool.dma_start(bd_raw[:, b, :, :], row("L1_cond_B_down").rearrange("(g s) r -> g s r", s=4)).then_inc(gath_in, 16)
            g0 = groups.index(("b0", 0))
            pool.wait_ge(raw_in[ring[g0] % RAW], 16 * (ring[g0] // RAW + 1))
            pool.tensor_copy(b0_sorted, raw[:, ring[g0] % RAW, :, :].rearrange("p c t -> p (c t)")
                             .rearrange("p (b s r) -> p s b r", b=NB, s=4)).then_inc(b0_in_order, 1)
            idx2 = a["itok_B_0_23"].rearrange("(o b) -> o b", o=1)
            for b in range(NB):
                k = pool.value_load(idx2[0:1, b:b + 1], min_val=0, max_val=31)
                pool.dma_start(a2T[:, :, R * b:R * b + R], a["L2_cond_lora_As"][bass.ds(k, 1)].rearrange("o (c p) r -> p (o c) r", p=P)).then_inc(gath_in, 16)
                pool.dma_start(b2R[R * b:R * b + R, :], a["L2_cond_lora_Bs"][bass.ds(k, 1)].rearrange("o r d -> (o r) d")).then_inc(gath_in, 16)
            pool.wait_ge(gath_in, GATHERED)
            pool.tensor_copy(bd_sorted, bd_raw.rearrange("p b s r -> p s b r"))
            pool.tensor_copy(bg_sorted[0:FG], bg_raw[0:FG].rearrange("p b s r -> p s b r"))
            pool.tensor_copy(bu_sorted[0:FG], bu_raw[0:FG].rearrange("p b s r -> p s b r")).then_inc(b_in_order, 1)

        @block.tensor
        def _(pe):
            pe.wait_ge(consts_in, 16)
            idt = ident
            done = {"lin": 0}

            def transpose_groups(lo, hi):
                for g in range(lo, hi):
                    if g in ring:
                        pe.wait_ge(raw_in[ring[g] % RAW], 16 * (ring[g] // RAW + 1))
                    elif g == END0:
                        pe.wait_ge(gath_in, GATHERED)
                        pe.wait_ge(b_in_order, 1)
                    if groups[g][0] == "b0":
                        pe.wait_ge(b0_in_order, 1)
                    if g >= 2:
                        pe.wait_ge(tr_evac[g % 2], g // 2)
                    tr, _, _ = transposes_of(g)
                    for src, k, dst in tr:
                        last = pe.transpose(dst, src, idt[0:k, 0:k])
                    last.then_inc(tr_filled[g % 2], 1)

            def all_copied(g):
                pe.wait_ge(tr_evac[0], (g + 1) // 2)
                pe.wait_ge(tr_evac[1], g // 2)

            def linear(wT, blocks, lhs_rank, x_of, rank_of, half):
                for n in range(C):
                    k = done["lin"]
                    if k >= 2:
                        pe.wait_ge(lin_evac, k - 1)
                    dst = bank(6 + k % 2)
                    for c, m in enumerate(blocks):
                        pe.matmul(dst, wT[0:m, c, n * P:(n + 1) * P], x_of(c, m, half), start=(c == 0), stop=False)
                    pe.matmul(dst, lhs_rank[:, n * P:(n + 1) * P], rank_of(half), start=False, stop=True).then_inc(lin_filled, 1)
                    done["lin"] += 1

            def rank_products(pairs, x, half):
                for n, w in enumerate(pairs):
                    for c in range(C):
                        last = pe.matmul(bank(2 + n), w[:, c, :], x[:, c, half * HALF:(half + 1) * HALF], start=(c == 0), stop=(c == C - 1))
                last.then_inc(rank_filled, 1)

            transpose_groups(0, END0)
            all_copied(END0)
            for t in range(NB):
                for c in range(C):
                    last = pe.matmul(bank(4)[:, t * E:(t + 1) * E], xT_a[:, c, t * T:(t + 1) * T], wrT[:, c, :], start=(c == 0), stop=(c == C - 1))
            last.then_inc(router_in, 1)
            for half in range(2):
                for c in range(C):
                    last = pe.matmul(bank(2 + half), a0T[:, c, :], xT_a[:, c, half * HALF:(half + 1) * HALF], start=(c == 0), stop=(c == C - 1))
            last.then_inc(rank_filled, 1)
            pe.wait_ge(gates_ready, 1)
            for t in range(NB):
                last = pe.transpose(bank(5 + t // 4)[:, (t % 4) * T:(t % 4 + 1) * T], gate16[:, t, :, :], idt)
            last.then_inc(gateT_filled, 1)
            transpose_groups(END0, END1)
            pe.wait_ge(rank_evac, 1)
            pe.wait_ge(gateT_evac, 1)
            for half in range(2):
                linear(w0T, [P] * C, b0T, lambda c, m, h: xT_a[:, c, h * HALF:(h + 1) * HALF],
                       lambda h: rank_act[:, 0, h * HALF:(h + 1) * HALF], half)
            all_copied(END1)
            fblocks = [fr(n) for n in range(FC)]
            n_gu = 0
            n_rank = 1
            for half in range(2):
                pe.wait_ge(lin_evac, C * (2 + half))
                hs = slice(half * HALF, (half + 1) * HALF)
                rank_products([agT, auT], xT_b, half)
                n_rank += 1
                pe.wait_ge(rank_evac, n_rank)
                for n in range(FC):
                    m = fr(n)
                    if n_gu >= 2:
                        pe.wait_ge(gu_evac, n_gu - 1)
                    for k, (w, bT) in enumerate(((wgT, bgT), (wuT, buT))):
                        dst = bank(2 + 2 * (n_gu % 2) + k)[0:m, :]
                        for c in range(C):
                            pe.matmul(dst, w[:, c, n * P:n * P + m], xT_b[:, c, hs], start=(c == 0), stop=False)
                        last = pe.matmul(dst, bT[:, n * P:n * P + m], rank_act[:, k, hs], start=False, stop=True)
                    last.then_inc(gu_filled, 1)
                    n_gu += 1
                pe.wait_ge(gu_evac, n_gu)
                for n in range(FC):
                    last = pe.matmul(bank(2), adT[0:fr(n), n, :], act_T[0:fr(n), n, :], start=(n == 0), stop=(n == FC - 1))
                last.then_inc(rank_filled, 1)
                n_rank += 1
                pe.wait_ge(rank_evac, n_rank)
                linear(wdT, fblocks, bdT, lambda c, m, h: act_T[0:m, c, :], lambda h: rank_act[:, 0, h * HALF:(h + 1) * HALF], half)
            pe.wait_ge(lin_evac, 4 * C)
            for half in range(2):
                rank_products([a2T], xT_a, half)
                n_rank += 1
                pe.wait_ge(rank_evac, n_rank)
                linear(w2T, [P] * C, b2R, lambda c, m, h: xT_a[:, c, h * HALF:(h + 1) * HALF],
                       lambda h: rank_act[:, 0, h * HALF:(h + 1) * HALF], half)

        def copy_out(eng, g):
            _, dst, src = transposes_of(g)
            eng.wait_ge(tr_filled[g % 2], g // 2 + 1)
            f = nc.scalar.copy if g % 2 == 0 else nc.vector.tensor_copy
            if g == AD_TAIL:
                f(dst, src)
                n = FC - 1
                dst, src = adT[0:FR, n, :], banks[0:FR, g % 2, (n % 4) * P:(n % 4 + 1) * P]
            f(dst, src).then_inc(tr_evac[g % 2], 1)

        @block.scalar
        def _(act):
            for g in range(0, END0, 2):
                copy_out(act, g)
            act.wait_ge(router_d, 1)
            nc.scalar.activation(rt[:, 0, :, 1], rt[:, 0, :, 0], ACT.Exp).then_inc(router_exp, 1)
            act.wait_ge(gateT_filled, 1)
            nc.scalar.mul(xT_b[:, 0, 0:HALF], bank(5), 2.0)
            nc.scalar.mul(xT_b[:, 0, HALF:], bank(6), 2.0).then_inc(gateT_evac, 1)
            for g in range(END0 + END0 % 2, END1, 2):
                copy_out(act, g)
            for n in range(2 * FC):
                m = fr(n % FC)
                act.wait_ge(gu_filled, n + 1)
                if n >= 2:
                    act.wait_ge(gu_evac, n - 1)
                nc.scalar.activation(silu[0:m, n % 2, :], bank(2 + 2 * (n % 2))[0:m, :], ACT.Silu).then_inc(silu_done, 1)

        @block.vector
        def _(dve):
            steps = [0]

            def link(ins):
                steps[0] += 1
                ins.then_inc(dve_step, 1)
                dve.wait_ge(dve_step, steps[0])

            for g in range(1, END0, 2):
                copy_out(dve, g)
            dve.wait_ge(small_in, 80)
            link(nc.vector.tensor_copy(rt[:, 5, :, 0], ints[:, 0, :]))
            e_index = const[:, K_E:K_FR].rearrange("p (o e) -> p o e", o=1).to_broadcast([P, NB, E])

            def per_tile(col):
                return col.to_broadcast([P, NB, E])
            link(nc.vector.tensor_tensor(rt[:, 1, :, :], e_index, per_tile(rt[:, 5, :, 0:1]), ALU.is_equal))
            dve.wait_ge(router_in, 1)
            link(nc.vector.scalar_tensor_tensor(logit[:, :, :], rt[:, 1, :, :], 5.0,
                                                bank(4)[:, 0:NB * E].rearrange("p (t e) -> p t e", t=NB), ALU.mult, ALU.add))
            for t in range(NB):
                last = nc.vector.max(top[:, t, :], logit[:, t, :])
            link(last)
            for t in range(NB):
                last = nc.vector.max_index(topi[:, t, :], top[:, t, :], logit[:, t, :])
            link(last)
            link(nc.vector.tensor_copy(rt[:, 5, :, 0:2], topi[:, :, 0:2]))
            nc.vector.tensor_tensor(rt[:, 0, :, 0], top[:, :, 1], top[:, :, 0], ALU.subtract).then_inc(router_d, 1)
            dve.wait_ge(router_exp, 1)
            link(nc.vector.tensor_scalar(rt[:, 0, :, 2], rt[:, 0, :, 1], 1.0, None, ALU.add))
            link(nc.vector.reciprocal(rt[:, 0, :, 3], rt[:, 0, :, 2]))
            link(nc.vector.tensor_tensor(rt[:, 0, :, 4], rt[:, 0, :, 1], rt[:, 0, :, 3], ALU.mult))
            for k in range(2):
                link(nc.vector.tensor_tensor(rt[:, 1 + k, :, :], e_index, per_tile(rt[:, 5, :, k:k + 1]), ALU.is_equal))
                link(nc.vector.tensor_tensor(rt[:, 3 + k, :, :], rt[:, 1 + k, :, :], per_tile(rt[:, 0, :, 3 + k:4 + k]), ALU.mult))
            link(nc.vector.tensor_tensor(rt[:, 1, :, :], rt[:, 3, :, :], rt[:, 4, :, :], ALU.add))
            nc.vector.tensor_copy(gate16.rearrange("p t e r -> p (t e) r"),
                                  rt[:, 1, :, :].rearrange("p t (e o) -> p (t e) o", o=1).to_broadcast([P, NB * E, R])).then_inc(gates_ready, 1)
            dve.wait_ge(rank_filled, 1)
            dve.wait_ge(gateT_evac, 1)
            nc.vector.tensor_tensor(rank_act[:, 0, 0:HALF], bank(2), xT_b[:, 0, 0:HALF], ALU.mult)
            nc.vector.tensor_tensor(rank_act[:, 0, HALF:], bank(3), xT_b[:, 0, HALF:], ALU.mult).then_inc(rank_evac, 1)
            for g in range(END0 + 1 - END0 % 2, END1, 2):
                copy_out(dve, g)

            def block_of(x, k):
                return x[:, k % C, (k // C % 2) * HALF:(k // C % 2 + 1) * HALF]

            def residual(k, dst, src):
                dve.wait_ge(lin_filled, k + 1)
                nc.vector.tensor_tensor(block_of(dst, k), bank(6 + k % 2), block_of(src, k), ALU.add).then_inc(lin_evac, 1)

            def own_rows(srcs, half, scale, n_rank):
                dve.wait_ge(rank_filled, n_rank)
                for k, src in enumerate(srcs):
                    for b in range(HALF // T):
                        t = half * HALF + b * T
                        last = nc.vector.tensor_scalar(rank_act[:, k, t:t + T], src[:, b * T:(b + 1) * T],
                                                       blockmask[:, t // T:t // T + 1], scale, ALU.mult, ALU.mult)
                last.then_inc(rank_evac, 1)

            for k in range(2 * C):
                residual(k, xT_b, xT_a)
            n_rank = 1
            n = 0
            for half in range(2):
                n_rank += 1
                own_rows([bank(2), bank(3)], half, 0.5, n_rank)
                for fc in range(FC):
                    m = fr(fc)
                    dve.wait_ge(silu_done, n + 1)
                    nc.vector.tensor_tensor(act_T[0:m, fc, :], silu[0:m, n % 2, :], bank(3 + 2 * (n % 2))[0:m, :], ALU.mult).then_inc(gu_evac, 1)
                    n += 1
                n_rank += 1
                own_rows([bank(2)], half, 0.5, n_rank)
                for k in range((2 + half) * C, (3 + half) * C):
                    residual(k, xT_a, xT_b)
            for half in range(2):
                n_rank += 1
                own_rows([bank(2)], half, 2.0, n_rank)
                for k in range((4 + half) * C, (5 + half) * C):
                    dve.wait_ge(lin_filled, k + 1)
                    nc.vector.scalar_tensor_tensor(block_of(xT_b, k), bank(6 + k % 2), bias2[:, k % C:k % C + 1], block_of(xT_a, k),
                                                   ALU.add, ALU.add).then_inc(lin_evac, 1)


def attention(nc, a, out, const, xT, ints, q_w, k_w, banks):
    ident = const[:, K_ID:K_BM]
    key_index = const[:, K_IO:K_E]

    def bank(n):
        return banks[:, n, :]

    QKV, OUT, SNEW = bank(0), bank(2), bank(5)
    flat01 = banks[:, 0:2, :].rearrange("p n c -> p (n c)")
    QK5 = flat01[:, 0:5 * DH].rearrange("p (h d) -> p h d", h=5)
    KV = bank(1)[:, 0:2 * DH]
    VN = bank(1)[:, DH:2 * DH]
    KTN = bank(1)[:, 2 * DH:3 * DH]

    with ExitStack() as ctx:
        def sb(name, shape, dt=fp32):
            return ctx.enter_context(nc.sbuf_tensor(name, shape, dt))

        acc = sb("acc", [P, NB, D])
        lens = sb("lens", [P, NB])
        pages = sb("pages", [1, NB * NPP], i32)
        tabs = sb("tabs", [P, NB, 4, DH])
        ang = sb("ang", [P, 4, NB * DH // 2])
        wq_raw = sb("wq_raw", [P, 8, D])
        wkv_raw = sb("wkv_raw", [P, 4, D])
        wo_raw = sb("wo_raw", [P, C, 2 * REP * DH])
        wqT = sb("wqT", [P, C, 2 * REP * DH])
        wkvT = sb("wkvT", [P, C, 2, 2 * DH])
        woT = sb("woT", [P, 2 * REP, D])
        xb = sb("xb", [P, C, T])
        tab = sb("tab", [P, 4, DH])
        len_b = sb("len_b", [P, 1])
        k_raw = sb("k_raw", [P, KC, 2, DH])
        v_raw = sb("v_raw", [P, KC, 2, DH])
        mask = sb("mask", [P, L])
        unused = sb("unused", [P, 1])
        sq = sb("sq", [P, 5, DH])
        ss = sb("ss", [P, 3, 5])
        half_power = sb("half_power", [P, 5])
        qn = sb("qn", [P, 5, DH])
        rope_a = sb("rope_a", [P, 5, DH])
        rope_b = sb("rope_b", [P, 5, DH])
        qr = sb("qr", [P, 5, DH])
        qT = [sb(f"qT{s}", [P, REP, T]) for s in range(2)]
        kT = [sb(f"kT{s}", [P, KEYS]) for s in range(2)]
        v_new = [sb(f"v_new{s}", [P, DH]) for s in range(2)]
        probs = [sb(f"probs{s}", [P, REP, KEYS]) for s in range(2)]
        stat = sb("stat", [P, 2, 4, REP])
        sums = sb("sums", [P, 2, 4, REP])
        pT = [sb(f"pT{s}", [P, REP, T]) for s in range(2)]
        inv_rows = sb("inv_rows", [P, REP, DH])
        invT = sb("invT", [P, REP, T])
        oT = sb("oT", [P, REP, T])

        per_unit = {}

        def sem(name, n=0):
            s = ctx.enter_context(nc.semaphore(name))
            if n:
                per_unit[name] = (s, n)
            return s

        pages_in, tabs_ready, ang_ready, sin_ready = sem("pages_in"), sem("tabs_ready"), sem("ang_ready"), sem("sin_ready")
        x_filled, x_evac = [sem("x_filled0"), sem("x_filled1")], [sem("x_evac0"), sem("x_evac1")]
        w_in = sem("w_in")
        wt_filled, wt_evac = [sem("wt_filled0"), sem("wt_filled1")], [sem("wt_evac0"), sem("wt_evac1")]
        row_in, k_in, v_in = sem("row_in"), sem("k_in"), sem("v_in")
        step = sem("step")
        pstep = sem("pstep")
        out_stored = sem("out_stored")
        proj_filled = sem("proj_filled", 1)
        squared = sem("squared", 1)
        ms_ready = sem("ms_ready", 1)
        inv_rms = sem("inv_rms", 1)
        qn_ready = sem("qn_ready", 1)
        roped = sem("roped", 1)
        ktc_filled, ktc_evac = sem("ktc_filled", 1), sem("ktc_evac", 1)
        qt_filled, qt_evac = sem("qt_filled", 1), sem("qt_evac", 1)
        ktn_filled, ktn_evac = sem("ktn_filled", 1), sem("ktn_evac", 1)
        snew_filled = sem("snew_filled", 1)
        s_filled = sem("s_filled", REP)
        masked = sem("masked", REP)
        nmax_ready = sem("nmax_ready", REP)
        exp_done = sem("exp_done", REP)
        pt_filled = [sem(f"pt_filled{c}", 1) for c in range(KC + 1)]
        pt_evac = [sem(f"pt_evac{c}", 1) for c in range(KC + 1)]
        pv_done = sem("pv_done", KC + 1)
        inv_ready = sem("inv_ready", 1)
        inv_filled, inv_evac = sem("inv_filled", 1), sem("inv_evac", 1)
        o_ready = sem("o_ready", 1)
        out_filled, out_evac = sem("out_filled", 1), sem("out_evac", 1)
        newmax, total, summed = sem("newmax", 1), sem("total", 2), sem("summed", 1)
        mask_ready = sem("mask_ready")

        count = {s.name: n for s, n in per_unit.values()}

        def wait(eng, s, u, n=None):
            k = count[s.name]
            eng.wait_ge(s, (u + 2) * k + (k if n is None else n))

        def before_first(eng, sems):
            for s in sems:
                eng.sem_inc(s, 2 * count[s.name])

        def row_count(u, n):
            return (u + 2) * (n // 2)

        def loops(eng, prepare, front, scores, tail, both, last_both):
            with eng.Fori(0, NGP) as g:
                prepare(g)
                u0 = g * UNITS
                front(u0, 0, 0, True)
                scores(u0, 0, 0)
                front(u0 + 1, 1, 0, False)
                with eng.Fori(0, NB - 1) as b:
                    u = u0 + 2 * b
                    both(u + 1, 1, b)
                    both(u + 2, 0, b + 1)
                last_both(u0 + UNITS - 1, 1, NB - 1)
                tail(u0 + UNITS - 1, 1, NB - 1, True)

        def weights_place(n):
            if n < 8:
                return wqT[:, :, n * P:(n + 1) * P]
            if n < 12:
                j, k = (n - 8) % 2, (n - 8) // 2
                return wkvT[:, :, j, k * DH:(k + 1) * DH]
            return woT[:, (n % 2) * REP:(n % 2 + 1) * REP, (n - 12) // 2 * P:((n - 12) // 2 + 1) * P]

        def pt_slot_free(eng, u, c):
            wait(eng, pv_done, u - 1) if c < 2 else wait(eng, pv_done, u, c - 1)

        block = ctx.enter_context(nc.Block())

        @block.sync
        def _(sp):
            sp.dma_start(pages[:, :], a["itok_Bx16_0_63"].rearrange("(o b) n -> o (b n)", o=1)).then_inc(pages_in, 16)
            sp.wait_ge(pages_in, 16)
            sp.wait_ge(tabs_ready, 2)
            wq = a["L3_cond_Wq"].rearrange("(g n p) d -> g p n d", g=NGP, p=P)
            wk = a["L3_cond_Wk"].rearrange("(g n p) d -> g p n d", g=NGP, p=P)
            wv = a["L3_cond_Wv"].rearrange("(g n p) d -> g p n d", g=NGP, p=P)
            wo = a["L3_cond_Wo"].rearrange("(o p) (g k) -> g p o k", p=P, g=NGP)

            def one(w, g):
                return w[bass.ds(g, 1)].rearrange("o p n d -> (o p) n d")
            with sp.Fori(0, NGP) as g:
                for par in range(2):
                    sp.wait_ge(wt_filled[par], g * 10 + 1)
                sp.dma_start(wq_raw[:, :, :], one(wq, g)).then_inc(w_in, 16)
                sp.dma_start(wkv_raw[:, 0:2, :], one(wk, g)).then_inc(w_in, 16)
                sp.dma_start(wkv_raw[:, 2:4, :], one(wv, g)).then_inc(w_in, 16)
                sp.dma_start(wo_raw[:, :, :], one(wo, g)).then_inc(w_in, 16)
                with sp.Fori(0, NB) as b:
                    u = g * UNITS + 2 * b
                    row_pages = [sp.value_load(pages[0:1, bass.ds(b * NPP + n, 1)], min_val=0, max_val=PAGES - 1) for n in range(NPP)]
                    wait(sp, proj_filled, u - 1)
                    sp.dma_start(xb[:, :, :], xT[:, :, bass.ds(b * T, T)]).then_inc(row_in, 16)
                    wait(sp, roped, u - 1)
                    table = tabs[:, bass.ds(b, 1), :, :].rearrange("p o k d -> p (o k) d")
                    sp.dma_start(tab[:, :, :], table).then_inc(row_in, 16)
                    wait(sp, masked, u - 1)
                    wait(sp, ktc_filled, u - 1)
                    sp.dma_start(len_b[:, :], lens[:, bass.ds(b, 1)]).then_inc(row_in, 16)
                    for n in range(NPP):
                        sp.dma_start(k_raw[PSIZE * (n % 4):PSIZE * (n % 4 + 1), n // 4, :, :],
                                     a["L3_cond_k_cache"][bass.ds(row_pages[n], 1), :, bass.ds(2 * g, 2), :].rearrange("o s h d -> (o s) h d")).then_inc(k_in, 16)
                    wait(sp, pv_done, u - 1)
                    for n in range(NPP):
                        sp.dma_start(v_raw[PSIZE * (n % 4):PSIZE * (n % 4 + 1), n // 4, :, :],
                                     a["L3_cond_v_cache"][bass.ds(row_pages[n], 1), :, bass.ds(2 * g, 2), :].rearrange("o s h d -> (o s) h d")).then_inc(v_in, 16)
            wait(sp, out_evac, NGP * UNITS - 1)
            sp.dma_start(out.rearrange("b t d -> t b d"), acc[:, :, :]).then_inc(out_stored, 16)
            sp.wait_ge(out_stored, 16)

        @block.tensor
        def _(pe):
            before_first(pe, [proj_filled, ktc_filled, qt_filled, ktn_filled, snew_filled, s_filled, *pt_filled, pv_done, inv_filled, out_filled])
            for s in wt_filled:
                pe.sem_inc(s, 1)
            for t in range(NB):
                if t >= 2:
                    pe.wait_ge(x_evac[t % 2], t // 2)
                for c in range(C):
                    last = pe.transpose(bank(6 + t % 2)[:, c * P:(c + 1) * P], xT[:, c, t * T:(t + 1) * T], ident)
                last.then_inc(x_filled[t % 2], 1)
            pe.wait_ge(x_evac[0], NB // 2)
            pe.wait_ge(x_evac[1], NB // 2)

            def prepare(g):
                pe.wait_ge(w_in, (g + 1) * 64)
                for n in range(20):
                    dst = bank(6 + n % 2)
                    if n < 2:
                        wait(pe, (pt_evac[KC], inv_evac)[n], g * UNITS - 1)
                    else:
                        pe.wait_ge(wt_evac[n % 2], g * 10 + n // 2)
                    for c in range(C):
                        if n < 8:
                            src = wq_raw[:, n, c * P:(c + 1) * P]
                        elif n < 12:
                            src = wkv_raw[:, n - 8, c * P:(c + 1) * P]
                        else:
                            src = wo_raw[:, (n - 12) // 2, ((n % 2) * C + c) * P:((n % 2) * C + c + 1) * P]
                        last = pe.transpose(dst[:, c * P:(c + 1) * P], src, ident)
                    last.then_inc(wt_filled[n % 2], 1)
                pe.wait_ge(wt_evac[0], (g + 1) * 10)
                pe.wait_ge(wt_evac[1], (g + 1) * 10)

            def project(u, j, b, first):
                if j == 0:
                    pe.wait_ge(row_in, row_count(u, 48))
                wait(pe, ktn_evac, u - 1)
                for c in range(C):
                    pe.matmul(QKV, xb[:, c, :], wqT[:, c, j * REP * DH:(j + 1) * REP * DH], start=(c == 0), stop=(c == C - 1))
                for c in range(C):
                    last = pe.matmul(KV, xb[:, c, :], wkvT[:, c, j, :], start=(c == 0), stop=(c == C - 1))
                last.then_inc(proj_filled, 1)

            def cached_keys(u, j, b):
                if j == 0:
                    pe.wait_ge(k_in, row_count(u, 16 * NPP))
                wait(pe, pt_evac[KC], u - 2)
                for c in range(KC):
                    last = pe.transpose(bank(6)[:, c * P:(c + 1) * P], k_raw[:, c, j, :], ident)
                last.then_inc(ktc_filled, 1)

            def queries(u):
                wait(pe, roped, u)
                wait(pe, inv_evac, u - 2)
                for h in range(REP):
                    last = pe.transpose(bank(7)[:, h * T:(h + 1) * T], qr[:, h, :], ident)
                last.then_inc(qt_filled, 1)
                wait(pe, qn_ready, u)
                pe.transpose(KTN, qr[:, REP, :], ident).then_inc(ktn_filled, 1)

            def front(u, j, b, first):
                project(u, j, b, first)
                cached_keys(u, j, b)
                queries(u)

            def scores(u, s, b):
                q, k = qT[s], kT[s]
                wait(pe, qt_evac, u)
                wait(pe, ktn_evac, u)
                wait(pe, ktc_evac, u)
                wait(pe, exp_done, u - 1)
                for h in range(REP):
                    last = pe.matmul(SNEW[:, h * T:(h + 1) * T], q[:, h, :], k[:, L:KEYS], start=True, stop=True)
                last.then_inc(snew_filled, 1)
                for h in range(REP):
                    if h < 2:
                        wait(pe, masked, u - 1, h + 3)
                    else:
                        wait(pe, masked, u, h - 1)
                    pe.matmul(bank(3 + h % 2), q[:, h, :], k[:, 0:L], start=True, stop=True).then_inc(s_filled, 1)

            def values(u, j, c):
                wait(pe, pt_evac[c], u)
                if c == 0:
                    wait(pe, out_evac, u - 1)
                v = v_raw[:, c, j, :] if c < KC else v_new[j][:, :]
                pe.matmul(OUT, v, pT[c % 2][:, :, :].rearrange("p h t -> p (h t)"), start=(c == 0), stop=(c == KC)).then_inc(pv_done, 1)

            def attend(u, j, last_unit):
                wait(pe, exp_done, u)
                if j == 0:
                    pe.wait_ge(v_in, row_count(u, 16 * NPP))
                for c in range(KC + 1):
                    if c == 0:
                        wait(pe, pt_evac[KC], u - 1) if last_unit else wait(pe, ktc_evac, u + 1)
                    elif c == 1:
                        wait(pe, inv_evac, u - 1) if last_unit else wait(pe, qt_evac, u + 1)
                    else:
                        wait(pe, pt_evac[c - 2], u)
                    for h in range(REP):
                        last = pe.transpose(bank(6 + c % 2)[:, h * T:(h + 1) * T], probs[j][:, h, c * P:(c + 1) * P], ident)
                    last.then_inc(pt_filled[c], 1)
                    if c >= 1:
                        values(u, j, c - 1)
                wait(pe, inv_ready, u)
                wait(pe, pt_evac[KC - 1], u)
                for h in range(REP):
                    last = pe.transpose(bank(7)[:, h * T:(h + 1) * T], inv_rows[:, h, :], ident)
                last.then_inc(inv_filled, 1)
                values(u, j, KC)

            def project_out(u, j):
                wait(pe, o_ready, u)
                for h in range(REP):
                    last = pe.matmul(OUT, oT[:, h, :], woT[:, j * REP + h, :], start=(h == 0), stop=(h == REP - 1))
                last.then_inc(out_filled, 1)

            def tail(u, j, b, last_unit):
                attend(u, j, last_unit)
                project_out(u, j)

            def both(u, j, b):
                scores(u, j, b)
                attend(u - 1, 1 - j, False)
                project(u + 1, 1 - j, b, False)
                cached_keys(u + 1, 1 - j, b)
                project_out(u - 1, 1 - j)
                queries(u + 1)

            def last_both(u, j, b):
                scores(u, j, b)
                tail(u - 1, 1 - j, b, True)

            loops(pe, prepare, front, scores, tail, both, last_both)

        @block.scalar
        def _(act):
            before_first(act, [squared, ktc_evac, exp_done, pt_evac[0], pt_evac[2], pt_evac[4]])
            act.wait_ge(ang_ready, 1)
            nc.scalar.activation(ang[:, 0:2, :], ang[:, 0:2, :], ACT.Sin).then_inc(sin_ready, 1)
            for t in range(0, NB, 2):
                act.wait_ge(x_filled[0], t // 2 + 1)
                nc.scalar.copy(acc[:, t, :], bank(6)).then_inc(x_evac[0], 1)

            def prepare(g):
                for n in range(0, 20, 2):
                    act.wait_ge(wt_filled[0], g * 10 + n // 2 + 2)
                    nc.scalar.copy(weights_place(n), bank(6).rearrange("p (c t) -> p c t", c=C)).then_inc(wt_evac[0], 1)

            def squares(u, j):
                wait(act, proj_filled, u)
                wait(act, pv_done, u - 2)
                nc.scalar.copy(v_new[j][:, :], VN)
                wait(act, ms_ready, u - 1)
                nc.scalar.activation(sq[:, :, :], QK5, ACT.Square).then_inc(squared, 1)

            def cached_keys(u, j):
                wait(act, ktc_filled, u)
                wait(act, s_filled, u - 2)
                nc.scalar.copy(kT[j][:, 0:L], bank(6)).then_inc(ktc_evac, 1)

            def exps(u, s, h):
                wait(act, nmax_ready, u, h + 1)
                p = probs[s]
                nc.scalar.activation(p[:, h, 0:L], p[:, h, 0:L], ACT.Exp, bias=stat[:, s, 2, h:h + 1], scale=SCALE,
                                     accum_out=sums[:, s, 0, h:h + 1])
                nc.scalar.activation(p[:, h, L:KEYS], SNEW[:, h * T:(h + 1) * T], ACT.Exp, bias=stat[:, s, 2, h:h + 1], scale=SCALE,
                                     accum_out=sums[:, s, 1, h:h + 1]).then_inc(exp_done, 1)

            def probs_out(u, c):
                wait(act, pt_filled[c], u)
                pt_slot_free(act, u, c)
                nc.scalar.copy(pT[c % 2][:, :, :].rearrange("p h t -> p (h t)"), bank(6)).then_inc(pt_evac[c], 1)

            def front(u, j, b, first):
                squares(u, j)
                cached_keys(u, j)

            def scores(u, s, b):
                for h in range(REP):
                    exps(u, s, h)

            def tail(u, j, b, last_unit):
                for c in (0, 2, 4):
                    probs_out(u, c)

            def last_both(u, j, b):
                exps(u, j, 0)
                exps(u, j, 1)
                probs_out(u - 1, 0)
                exps(u, j, 2)
                probs_out(u - 1, 2)
                exps(u, j, 3)
                probs_out(u - 1, 4)

            def both(u, j, b):
                last_both(u, j, b)
                squares(u + 1, 1 - j)
                cached_keys(u + 1, 1 - j)

            loops(act, prepare, front, scores, tail, both, last_both)

        @block.gpsimd
        def _(pool):
            before_first(pool, [inv_rms, roped])
            pool.memset(half_power[:, :], -0.5).then_inc(pstep, 1)
            pool.wait_ge(pstep, 1)

            def front(u, j, b, first):
                if j == 0:
                    pool.wait_ge(row_in, row_count(u, 48))
                wait(pool, ms_ready, u)
                wait(pool, qn_ready, u - 1)
                nc.gpsimd.tensor_tensor(ss[:, 2, :], ss[:, 1, :], half_power[:, :], ALU.pow).then_inc(inv_rms, 1)
                wait(pool, qn_ready, u)
                h = DH // 2
                nc.gpsimd.tensor_tensor(rope_a[:, 0:REP, :], qn[:, 0:REP, :], tab[:, 0:1, :].to_broadcast([P, REP, DH]), ALU.mult)
                nc.gpsimd.tensor_tensor(rope_a[:, REP, :], qn[:, REP, :], tab[:, 1, :], ALU.mult)
                for lo, of in ((0, h), (h, 0)):
                    nc.gpsimd.tensor_tensor(rope_b[:, 0:REP, lo:lo + h], qn[:, 0:REP, of:of + h], tab[:, 2:3, lo:lo + h].to_broadcast([P, REP, h]), ALU.mult)
                    last = nc.gpsimd.tensor_tensor(rope_b[:, REP, lo:lo + h], qn[:, REP, of:of + h], tab[:, 3, lo:lo + h], ALU.mult)
                last.then_inc(pstep, 1)
                pool.wait_ge(pstep, u + 2)
                wait(pool, ktn_filled, u - 1)
                nc.gpsimd.tensor_tensor(qr[:, :, :], rope_a[:, :, :], rope_b[:, :, :], ALU.add).then_inc(roped, 1)

            def nothing(*_):
                pass

            def both(u, j, b):
                front(u + 1, 1 - j, b, False)

            loops(pool, nothing, front, nothing, nothing, both, nothing)

        @block.vector
        def _(dve):
            before_first(dve, [ms_ready, qn_ready, qt_evac, ktn_evac, masked, nmax_ready, pt_evac[1], pt_evac[3], inv_ready, inv_evac, o_ready, out_evac, newmax, total, summed])
            n = [0]

            def link(ins):
                n[0] += 1
                ins.then_inc(step, 1)
                dve.wait_ge(step, n[0])
            link(nc.vector.tensor_copy(lens[:, :], ints[:, 1, :]))
            pos = ang[:, 3, 0:NB]
            link(nc.vector.tensor_scalar(pos, lens[:, :], const[:, K_P:K_P + 1], None, ALU.add))
            f = ang[:, 2, :].rearrange("p (b i) -> p b i", b=NB)
            link(nc.vector.tensor_tensor(f, pos.rearrange("p (b o) -> p b o", o=1).to_broadcast([P, NB, DH // 2]),
                                         const[:, K_FR:K_P].rearrange("p (o i) -> p o i", o=1).to_broadcast([P, NB, DH // 2]), ALU.mult))
            for k, shift in ((0, 0.0), (1, 0.25)):
                turns, r = ang[:, 3, :], ang[:, k, :]
                link(nc.vector.tensor_scalar(turns, ang[:, 2, :], 1.0 / TWO_PI, shift, ALU.mult, ALU.add))
                link(nc.vector.tensor_scalar(turns, turns, ROUND, None, ALU.add))
                link(nc.vector.tensor_scalar(turns, turns, -ROUND, None, ALU.add))
                link(nc.vector.scalar_tensor_tensor(r, turns, -C1, ang[:, 2, :], ALU.mult, ALU.add))
                link(nc.vector.scalar_tensor_tensor(r, turns, -C2, r, ALU.mult, ALU.add))
                link(nc.vector.scalar_tensor_tensor(r, turns, -C3, r, ALU.mult, ALU.add))
                link(nc.vector.tensor_scalar(r, r, TWO_PI * shift, None, ALU.add))
                last = nc.vector.tensor_scalar(r, r, 3.1415925, -3.1415925, ALU.min, ALU.max)
                if k == 0:
                    link(last)
            last.then_inc(ang_ready, 1)
            dve.wait_ge(sin_ready, 1)
            h = DH // 2

            def rows_of(x, lo):
                return x[:, lo:lo + h].rearrange("p (o i) -> p o i", o=1).to_broadcast([P, NB, h])
            sin, cos = (ang[:, k, :].rearrange("p (b i) -> p b i", b=NB) for k in range(2))
            for k, w in enumerate((q_w, k_w)):
                nc.vector.tensor_tensor(tabs[:, :, k, 0:h], cos, rows_of(w, 0), ALU.mult)
                nc.vector.tensor_tensor(tabs[:, :, k, h:DH], cos, rows_of(w, h), ALU.mult)
                nc.vector.scalar_tensor_tensor(tabs[:, :, 2 + k, 0:h], sin, -1.0, rows_of(w, h), ALU.mult, ALU.mult)
                nc.vector.tensor_tensor(tabs[:, :, 2 + k, h:DH], sin, rows_of(w, 0), ALU.mult).then_inc(tabs_ready, 1)
            for t in range(1, NB, 2):
                dve.wait_ge(x_filled[1], t // 2 + 1)
                nc.vector.tensor_copy(acc[:, t, :], bank(7)).then_inc(x_evac[1], 1)

            def prepare(g):
                for m in range(1, 20, 2):
                    dve.wait_ge(wt_filled[1], g * 10 + m // 2 + 2)
                    nc.vector.tensor_copy(weights_place(m), bank(7).rearrange("p (c t) -> p c t", c=C)).then_inc(wt_evac[1], 1)

            def row_mask(u):
                dve.wait_ge(row_in, row_count(u, 48))
                nc.vector.tensor_scalar(mask[:, :], key_index, len_b[:, 0:1], NEG, ALU.is_ge, ALU.mult).then_inc(mask_ready, 1)
                dve.wait_ge(mask_ready, (u + 2) // 2)

            def maxima(u, s):
                if s == 0:
                    row_mask(u)
                wait(dve, snew_filled, u)
                wait(dve, exp_done, u - 1)
                nc.vector.tensor_reduce(stat[:, s, 0, :], SNEW.rearrange("p (h k) -> p h k", h=REP), AX.X, ALU.max).then_inc(newmax, 1)
                wait(dve, newmax, u)
                wait(dve, pt_filled[KC], u - 2)
                for h in range(REP):
                    wait(dve, s_filled, u, h + 1)
                    nc.vector.memset(unused[:, :], 0.0)
                    nc.vector.tensor_tensor_reduce(out=probs[s][:, h, 0:L], in0=bank(3 + h % 2), in1=mask[:, :], scale=1.0,
                                                   scalar=stat[:, s, 0, h:h + 1], op0=ALU.add, op1=ALU.max,
                                                   accum_out=stat[:, s, 1, h:h + 1]).then_inc(masked, 1)
                    wait(dve, masked, u, h + 1)
                    nc.vector.tensor_scalar(stat[:, s, 2, h:h + 1], stat[:, s, 1, h:h + 1], -SCALE, None, ALU.mult).then_inc(nmax_ready, 1)

            def inverse_sums(u, s):
                wait(dve, exp_done, u)
                nc.vector.tensor_tensor(sums[:, s, 2, :], sums[:, s, 0, :], sums[:, s, 1, :], ALU.add).then_inc(total, 1)
                wait(dve, total, u, 1)
                nc.vector.reciprocal(sums[:, s, 3, :], sums[:, s, 2, :]).then_inc(total, 1)
                wait(dve, total, u, 2)
                wait(dve, inv_filled, u - 1)
                nc.vector.tensor_copy(inv_rows[:, :, :], sums[:, s, 3, :].rearrange("p (h o) -> p h o", o=1).to_broadcast([P, REP, DH])).then_inc(inv_ready, 1)

            def probs_out(u, c):
                wait(dve, pt_filled[c], u)
                pt_slot_free(dve, u, c)
                nc.vector.tensor_copy(pT[c % 2][:, :, :].rearrange("p h t -> p (h t)"), bank(7)).then_inc(pt_evac[c], 1)

            def normalise(u):
                wait(dve, inv_filled, u)
                nc.vector.tensor_copy(invT[:, :, :].rearrange("p h t -> p (h t)"), bank(7)).then_inc(inv_evac, 1)
                wait(dve, inv_evac, u)
                wait(dve, pv_done, u)
                wait(dve, out_filled, u - 1)
                nc.vector.tensor_tensor(oT[:, :, :].rearrange("p h t -> p (h t)"), OUT, invT[:, :, :].rearrange("p h t -> p (h t)"), ALU.mult).then_inc(o_ready, 1)

            def norms(u):
                wait(dve, squared, u)
                nc.vector.tensor_reduce(ss[:, 0, :], sq[:, :, :], AX.X, ALU.add).then_inc(summed, 1)
                wait(dve, summed, u)
                wait(dve, inv_rms, u - 1)
                nc.vector.tensor_scalar(ss[:, 1, :], ss[:, 0, :], 1.0 / DH, EPS, ALU.mult, ALU.add).then_inc(ms_ready, 1)
                wait(dve, inv_rms, u)
                wait(dve, roped, u - 1)
                nc.vector.tensor_tensor(qn[:, :, :], QK5, ss[:, 2, :].rearrange("p (h o) -> p h o", o=1).to_broadcast([P, 5, DH]), ALU.mult).then_inc(qn_ready, 1)

            def add_out(u, b):
                wait(dve, out_filled, u)
                wait(dve, out_evac, u - 1)
                o = acc[:, bass.ds(b, 1), :].rearrange("p o d -> p (o d)")
                nc.vector.tensor_tensor(o, OUT, o, ALU.add).then_inc(out_evac, 1)

            def queries_out(u, s):
                wait(dve, qt_filled, u)
                wait(dve, s_filled, u - 2)
                nc.vector.tensor_copy(qT[s][:, :, :].rearrange("p h t -> p (h t)"), bank(7)).then_inc(qt_evac, 1)
                wait(dve, ktn_filled, u)
                nc.vector.tensor_copy(kT[s][:, L:KEYS], KTN).then_inc(ktn_evac, 1)

            def front(u, j, b, first):
                norms(u)
                queries_out(u, j)

            def scores(u, s, b):
                maxima(u, s)

            def attend(u, s):
                inverse_sums(u, s)
                probs_out(u, 1)
                probs_out(u, 3)
                normalise(u)

            def tail(u, j, b, last_unit):
                attend(u, j)
                add_out(u, b)

            def both(u, j, b):
                maxima(u, j)
                attend(u - 1, 1 - j)
                norms(u + 1)
                add_out(u - 1, b if j == 1 else b - 1)
                queries_out(u + 1, 1 - j)

            def last_both(u, j, b):
                maxima(u, j)
                tail(u - 1, 1 - j, b, True)

            loops(dve, prepare, front, scores, tail, both, last_both)


_INS = ['x', 'itok_B_0_7', 'itok_B_2_6', 'itok_B_0_23', 'itok_Bx16_0_63', 'itok_B_207_1644', 'L0_cond_W', 'L0_cond_Wr', 'L0_cond_A',
        'L0_cond_B', 'L1_cond_W_gate', 'L1_cond_W_up', 'L1_cond_W_down', 'L1_cond_A_gate', 'L1_cond_B_gate', 'L1_cond_A_up',
        'L1_cond_B_up', 'L1_cond_A_down', 'L1_cond_B_down', 'L2_cond_W', 'L2_cond_b', 'L2_cond_lora_As', 'L2_cond_lora_Bs',
        'L3_cond_Wq', 'L3_cond_Wk', 'L3_cond_Wv', 'L3_cond_Wo', 'L3_cond_q_norm_w', 'L3_cond_k_norm_w', 'L3_cond_k_cache',
        'L3_cond_v_cache']


def kernel(**inputs):
    import numpy as _np
    import concourse.bacc as _bacc
    from concourse import mybir as _mybir
    from concourse.bass_utils import run_bass_kernel_spmd as _run

    nc = _bacc.Bacc("TRN2", target_bir_lowering=False, num_devices=1)
    arrays, args = {}, {}
    given = {name: _np.ascontiguousarray(inputs[name]) for name in _INS}
    given["shape_constants"] = constants()
    for name, x in given.items():
        arrays[f"in_{name}"] = x
        args[name] = nc.dram_tensor(f"in_{name}", x.shape, _mybir.dt.from_np(x.dtype), kind="ExternalInput").ap()
    out = nc.dram_tensor("out_0", (NB, T, D), _mybir.dt.float32, kind="ExternalOutput").ap()
    build(nc, args, out)
    r = _run(nc, [arrays], core_ids=[0])
    return r.results[0]["out_0"]
```

```python
import concourse.bass as bass
from concourse import mybir
from contextlib import ExitStack
import numpy as np

P = 128
NB, T, D = 8, 128, 512
NT = NB * T
C = D // P
HALF = 512
E, R = 8, 16
F = 1376
FC = (F + P - 1) // P
FR = F - (FC - 1) * P
FG = F // R
HQ, HK, DH = 32, 8, 128
REP = HQ // HK
PAGES, PSIZE, NPP = 64, 32, 16
L = NPP * PSIZE
KC = L // P
KEYS = L + T
NGP = HK // 2
UNITS = 2 * NB
EPS = 1e-6
SCALE = 1.0 / float(np.sqrt(DH))
NEG = -1e30
TWO_PI = 2.0 * np.pi
ROUND = 1.5 * 2.0 ** 23
C1 = 6.28125
C2 = float(np.float32(TWO_PI - C1))
C3 = float(TWO_PI - C1 - np.float64(np.float32(TWO_PI - C1)))
K_ID, K_BM, K_IO, K_E, K_FR, K_P, K_END = 0, 128, 136, 648, 656, 720, 721


def constants():
    k = np.zeros((P, K_END), np.float32)
    k[:, K_ID:K_BM] = np.eye(P)
    k[:, K_BM:K_IO] = np.arange(P)[:, None] // R == np.arange(NB)[None]
    k[:, K_IO:K_E] = np.arange(L)[None]
    k[:, K_E:K_FR] = np.arange(E)[None]
    k[:, K_FR:K_P] = (np.float32(1.0) / np.power(np.float32(10000.0), np.arange(0, DH, 2, dtype=np.float32) / np.float32(DH)))[None]
    k[:, K_P] = np.arange(P)
    return k


fp32, fp32r, i32, u32 = mybir.dt.float32, mybir.dt.float32r, mybir.dt.int32, mybir.dt.uint32
ALU = mybir.AluOpType
ACT = mybir.ActivationFunctionType
AX = mybir.AxisListType


def build(nc, a, out):
    with ExitStack() as ctx:
        def sb(name, shape, dt=fp32):
            return ctx.enter_context(nc.sbuf_tensor(name, shape, dt))

        const = sb("const", [P, K_END])
        ints = sb("ints", [P, 2, NB], i32)
        acc = sb("acc", [P, NB, D])
        lens = sb("lens", [P, NB])
        ident_r = sb("ident_r", [P, P], fp32r)
        x_scratch = nc.dram_tensor("x_scratch", (NB, P, 2, C, T), fp32, kind="Internal").ap()
        tab_scratch = nc.dram_tensor("tab_scratch", (NB, P, 4, DH), fp32, kind="Internal").ap()
        banks = ctx.enter_context(nc.psum_tensor("banks", [P, 8, 512], fp32))
        with ExitStack() as early:
            def early_sb(name, shape):
                return early.enter_context(nc.sbuf_tensor(name, shape, fp32))
            xT = early_sb("xT", [P, C, NT])
            q_w = early_sb("q_w", [P, DH])
            k_w = early_sb("k_w", [P, DH])
            layers012(nc, a, const, xT, acc, ints, q_w, k_w, banks)
            attention_setup(nc, const, xT, ints, q_w, k_w, banks, acc, lens, ident_r, x_scratch, tab_scratch)
        attention(nc, a, out, const, banks, acc, lens, ident_r, x_scratch, tab_scratch)


def layers012(nc, a, const, xT_b, acc, ints, q_w, k_w, banks):
    ident = const[:, K_ID:K_BM]
    blockmask = const[:, K_BM:K_IO]

    def bank(n):
        return banks[:, n, :]

    with ExitStack() as part1:
        ctx = part1

        def sb(name, shape, dt=fp32, stack=ctx):
            return stack.enter_context(nc.sbuf_tensor(name, shape, dt))

        def sem(name):
            return ctx.enter_context(nc.semaphore(name))

        xT_a = acc[:, :, :].rearrange("p b d -> p (b d)").rearrange("p (c t) -> p c t", c=C)
        RAW = 8
        raw = sb("raw", [P, RAW, C, P], stack=part1)
        w0T = sb("w0T", [P, C, D], stack=part1)
        w2T = sb("w2T", [P, C, D], stack=part1)
        wrT = sb("wrT", [P, C, E], stack=part1)
        wgT = sb("wgT", [P, C, F], stack=part1)
        wuT = sb("wuT", [P, C, F], stack=part1)
        wdT = sb("wdT", [P, FC, D], stack=part1)
        a0T = sb("a0T", [P, C, P], stack=part1)
        agT = sb("agT", [P, C, P], stack=part1)
        auT = sb("auT", [P, C, P], stack=part1)
        adT = sb("adT", [P, FC, P], stack=part1)
        a2T = sb("a2T", [P, C, P], stack=part1)
        b0T = sb("b0T", [P, D], stack=part1)
        bgT = sb("bgT", [P, F], stack=part1)
        buT = sb("buT", [P, F], stack=part1)
        bdT = sb("bdT", [P, D], stack=part1)
        b2R = sb("b2R", [P, D], stack=part1)
        bias2 = sb("bias2", [P, C], stack=part1)
        rank_act = sb("rank_act", [P, 2, HALF * 2], stack=part1)
        area = sb("area", [P, 2 * D + F + 2 * NB * 256 + D + 64], stack=part1)
        o = 0
        ag_raw = area[:, o:o + D]; o += D
        au_raw = area[:, o:o + D]; o += D
        ad_raw = area[:, o:o + F]; o += F
        bg_raw = area[:, o:o + NB * 256].rearrange("p (b s r) -> p b s r", b=NB, s=R); o += NB * 256
        bu_raw = area[:, o:o + NB * 256].rearrange("p (b s r) -> p b s r", b=NB, s=R); o += NB * 256
        bd_raw = area[:, o:o + D].rearrange("p (b s r) -> p b s r", b=NB, s=4)
        act_T = area[:, 0:FC * HALF].rearrange("p (f t) -> p f t", f=FC)
        silu = raw[:, 0:2, :, :].rearrange("p a c t -> p a (c t)")
        logit = sb("logit", [P, NB, E], stack=part1)
        top = sb("top", [P, NB, E], stack=part1)
        topi = sb("topi", [P, NB, E], u32, stack=part1)
        rt = sb("rt", [P, 6, NB, E], stack=part1)
        gate16 = rank_act[:, 1, :].rearrange("p (t e r) -> p t e r", t=NB, e=E)

        b0_sorted = wdT[:, 0, :].rearrange("p (s b r) -> p s b r", b=NB, r=R)
        bd_sorted = w2T[:, 0, :].rearrange("p (s b r) -> p s b r", b=NB, r=R)
        bg_sorted = wgT[:, :, :].rearrange("p c f -> p (c f)")[:, 0:NB * 256].rearrange("p (s b r) -> p s b r", b=NB, r=R)
        bu_sorted = wuT[:, :, :].rearrange("p c f -> p (c f)")[:, 0:NB * 256].rearrange("p (s b r) -> p s b r", b=NB, r=R)
        sorted_rows = {"b0": b0_sorted, "bd": bd_sorted, "bg": bg_sorted, "bu": bu_sorted}

        b0_in_order, b_in_order = sem("b0_in_order"), sem("b_in_order")
        consts_in, small_in = sem("consts_in"), sem("small_in")
        raw_in = [sem(f"raw_in{s}") for s in range(RAW)]
        gath_in = sem("gath_in")
        tr_filled = [sem("tr_filled0"), sem("tr_filled1")]
        tr_evac = [sem("tr_evac0"), sem("tr_evac1")]
        dve_step = sem("dve_step")
        router_in, router_exp, gates_ready = sem("router_in"), sem("router_exp"), sem("gates_ready")
        router_d = sem("router_d")
        gateT_filled, gateT_evac = sem("gateT_filled"), sem("gateT_evac")
        rank_filled, rank_evac = sem("rank_filled"), sem("rank_evac")
        lin_filled, lin_evac = sem("lin_filled"), sem("lin_evac")
        gu_filled, silu_done, gu_evac = sem("gu_filled"), sem("silu_done"), sem("gu_evac")

        def rows(src, n, m=P):
            return src[n * P:n * P + m, :]

        def blockwise(dst, n, m=P):
            return dst[:, :, n * P:n * P + m]

        groups = []
        for t in range(NB):
            groups.append(("x", t))
        for n in range(C):
            groups.append(("w0", n))
        groups += [("a0", 0), ("b0", 0), ("wr", 0)]
        END0 = len(groups)
        groups += [("ag", 0), ("au", 0)] + [("bg", n) for n in range(4)] + [("bu", n) for n in range(4)]
        for n in range(FC):
            groups += [("wg", n), ("wu", n)]
        for n in range(FC):
            groups.append(("wd", n))
        groups += [("ad", n) for n in range(3)] + [("bd", 0)]
        groups += [("w2", n) for n in range(C)]
        END1 = len(groups)
        ring = {}
        for g, (kind, n) in enumerate(groups):
            if kind not in ("ag", "au", "bg", "bu", "ad", "bd"):
                ring[g] = len(ring)
        ring_groups = {v: k for k, v in ring.items()}

        def fr(n):
            return P if n < FC - 1 else FR

        def load_of(g):
            kind, n = groups[g]
            s = raw[:, ring[g] % RAW, :, :]
            flat = s.rearrange("p c t -> p (c t)")
            if kind == "x":
                return flat, a["x"][n, :, :]
            if kind == "w0":
                return flat, rows(a["L0_cond_W"], n)
            if kind == "w2":
                return flat, rows(a["L2_cond_W"], n)
            if kind == "a0":
                return flat, a["L0_cond_A"].rearrange("e r d -> (e r) d")
            if kind == "b0":
                return s.rearrange("p c t -> p (c t)").rearrange("p (e k) -> p e k", e=E), \
                    a["L0_cond_B"].rearrange("e (g s) r -> g e (s r)", s=4)
            if kind == "wr":
                return flat[0:E, :], a["L0_cond_Wr"]
            if kind in ("wg", "wu"):
                return flat[0:fr(n), :], rows(a["L1_cond_W_gate" if kind == "wg" else "L1_cond_W_up"], n, fr(n))
            if kind == "wd":
                return s[:, :, 0:fr(n)], a["L1_cond_W_down"].rearrange("(c p) f -> p c f", p=P)[:, :, n * P:n * P + fr(n)]

        def transposes_of(g):
            kind, n = groups[g]
            b = banks[:, g % 2, :]
            if g in ring:
                s = raw[:, ring[g] % RAW, :, :]
            if kind in ("x", "w0", "w2", "a0", "wr", "wg", "wu", "ag", "au"):
                k = {"wr": E, "wg": fr(n), "wu": fr(n)}.get(kind, P)
                dst = {"x": xT_a, "w0": w0T, "w2": w2T, "a0": a0T, "wr": wrT, "wg": wgT, "wu": wuT, "ag": agT, "au": auT}[kind]
                src = {"ag": ag_raw, "au": au_raw}.get(kind)
                if src is None:
                    src = s.rearrange("p c t -> p (c t)")
                v = b.rearrange("p (c t) -> p c t", c=C)
                return [(src[0:k, c * P:(c + 1) * P], k, v[:, c, 0:k]) for c in range(C)], \
                    blockwise(dst, n, k), v[:, :, 0:k]
            if kind == "wd":
                m = fr(n)
                return [(s[:, c, 0:m], P, b[0:m, c * P:(c + 1) * P]) for c in range(C)], wdT[0:m, n, :], b[0:m, :]
            if kind == "ad":
                blocks = list(range(4 * n, min(4 * n + 4, FC)))
                full = [f for f in blocks if fr(f) == P]
                tr = [(ad_raw[:, f * P:f * P + fr(f)], P, b[0:fr(f), (f - 4 * n) * P:(f - 4 * n + 1) * P]) for f in blocks]
                return tr, adT[:, 4 * n:4 * n + len(full), :], b[:, 0:len(full) * P].rearrange("p (c t) -> p c t", t=P)
            if kind in ("b0", "bd"):
                s4 = sorted_rows[kind]
                dst = (bdT if kind == "bd" else b0T)[:, :].rearrange("p (g s) -> p s g", s=4)
                v = b.rearrange("p (s g) -> p s g", s=4)
                return [(s4[:, f, :, :], P, v[:, f, :]) for f in range(4)], dst, v
            if kind in ("bg", "bu"):
                s4 = sorted_rows[kind]
                dst = (bgT if kind == "bg" else buT)[:, :].rearrange("p (g s) -> p s g", s=R)[:, 4 * n:4 * n + 4, :]
                v = b[:, 0:4 * P].rearrange("p (s g) -> p s g", s=4)
                return [(s4[0:FG, 4 * n + f, :, :], FG, v[:, f, 0:FG]) for f in range(4)], dst, v[:, :, 0:FG]

        AD_TAIL = [g for g, (k, n) in enumerate(groups) if k == "ad" and 4 * n + 4 > FC - 1][0]

        GATHERED = 16 * (6 * NB + 2 * NB)
        block = ctx.enter_context(nc.Block())

        @block.sync
        def _(sp):
            sp.dma_start(const[:, :], a["shape_constants"]).then_inc(consts_in, 16)
            for k, g in sorted(ring_groups.items()):
                if k >= RAW:
                    prev = ring_groups[k - RAW]
                    sp.wait_ge(tr_filled[prev % 2], prev // 2 + 1)
                dst, src = load_of(g)
                sp.dma_start(dst, src).then_inc(raw_in[k % RAW], 16)

        @block.gpsimd
        def _(pool):
            for n, name in enumerate(("itok_B_0_7", "itok_B_207_1644")):
                pool.dma_start(ints[:, n, :], a[name].rearrange("(o b) -> o b", o=1).to_broadcast([P, NB])).then_inc(small_in, 16)
            pool.dma_start(q_w[:, :], a["L3_cond_q_norm_w"].rearrange("(o b) -> o b", o=1).to_broadcast([P, DH])).then_inc(small_in, 16)
            pool.dma_start(k_w[:, :], a["L3_cond_k_norm_w"].rearrange("(o b) -> o b", o=1).to_broadcast([P, DH])).then_inc(small_in, 16)
            pool.dma_start(bias2[:, :], a["L2_cond_b"].rearrange("(c p) -> p c", p=P), allow_slow_non_contiguous=True).then_inc(small_in, 16)
            idx = a["itok_B_2_6"].rearrange("(o b) -> o b", o=1)
            for b in range(NB):
                k = pool.value_load(idx[0:1, b:b + 1], min_val=0, max_val=15)
                rb = slice(R * b, R * b + R)

                def row(name):
                    return a[name][0][bass.ds(k, 1)].rearrange("o r d -> (o r) d")
                pool.dma_start(ag_raw[rb, :], row("L1_cond_A_gate")).then_inc(gath_in, 16)
                pool.dma_start(au_raw[rb, :], row("L1_cond_A_up")).then_inc(gath_in, 16)
                pool.dma_start(ad_raw[rb, :], row("L1_cond_A_down")).then_inc(gath_in, 16)
                pool.dma_start(bg_raw[0:FG, b, :, :], row("L1_cond_B_gate").rearrange("(g s) r -> g s r", s=R)).then_inc(gath_in, 16)
                pool.dma_start(bu_raw[0:FG, b, :, :], row("L1_cond_B_up").rearrange("(g s) r -> g s r", s=R)).then_inc(gath_in, 16)
                pool.dma_start(bd_raw[:, b, :, :], row("L1_cond_B_down").rearrange("(g s) r -> g s r", s=4)).then_inc(gath_in, 16)
            g0 = groups.index(("b0", 0))
            pool.wait_ge(raw_in[ring[g0] % RAW], 16 * (ring[g0] // RAW + 1))
            pool.tensor_copy(b0_sorted, raw[:, ring[g0] % RAW, :, :].rearrange("p c t -> p (c t)")
                             .rearrange("p (b s r) -> p s b r", b=NB, s=4)).then_inc(b0_in_order, 1)
            idx2 = a["itok_B_0_23"].rearrange("(o b) -> o b", o=1)
            for b in range(NB):
                k = pool.value_load(idx2[0:1, b:b + 1], min_val=0, max_val=31)
                pool.dma_start(a2T[:, :, R * b:R * b + R], a["L2_cond_lora_As"][bass.ds(k, 1)].rearrange("o (c p) r -> p (o c) r", p=P)).then_inc(gath_in, 16)
                pool.dma_start(b2R[R * b:R * b + R, :], a["L2_cond_lora_Bs"][bass.ds(k, 1)].rearrange("o r d -> (o r) d")).then_inc(gath_in, 16)
            pool.wait_ge(gath_in, GATHERED)
            pool.tensor_copy(bd_sorted, bd_raw.rearrange("p b s r -> p s b r"))
            pool.tensor_copy(bg_sorted[0:FG], bg_raw[0:FG].rearrange("p b s r -> p s b r"))
            pool.tensor_copy(bu_sorted[0:FG], bu_raw[0:FG].rearrange("p b s r -> p s b r")).then_inc(b_in_order, 1)

        @block.tensor
        def _(pe):
            pe.wait_ge(consts_in, 16)
            idt = ident
            done = {"lin": 0}

            def transpose_groups(lo, hi):
                for g in range(lo, hi):
                    if g in ring:
                        pe.wait_ge(raw_in[ring[g] % RAW], 16 * (ring[g] // RAW + 1))
                    elif g == END0:
                        pe.wait_ge(gath_in, GATHERED)
                        pe.wait_ge(b_in_order, 1)
                    if groups[g][0] == "b0":
                        pe.wait_ge(b0_in_order, 1)
                    if g >= 2:
                        pe.wait_ge(tr_evac[g % 2], g // 2)
                    tr, _, _ = transposes_of(g)
                    for src, k, dst in tr:
                        last = pe.transpose(dst, src, idt[0:k, 0:k])
                    last.then_inc(tr_filled[g % 2], 1)

            def all_copied(g):
                pe.wait_ge(tr_evac[0], (g + 1) // 2)
                pe.wait_ge(tr_evac[1], g // 2)

            def linear(wT, blocks, lhs_rank, x_of, rank_of, half):
                for n in range(C):
                    k = done["lin"]
                    if k >= 2:
                        pe.wait_ge(lin_evac, k - 1)
                    dst = bank(6 + k % 2)
                    for c, m in enumerate(blocks):
                        pe.matmul(dst, wT[0:m, c, n * P:(n + 1) * P], x_of(c, m, half), start=(c == 0), stop=False)
                    pe.matmul(dst, lhs_rank[:, n * P:(n + 1) * P], rank_of(half), start=False, stop=True).then_inc(lin_filled, 1)
                    done["lin"] += 1

            def rank_products(pairs, x, half):
                for n, w in enumerate(pairs):
                    for c in range(C):
                        last = pe.matmul(bank(2 + n), w[:, c, :], x[:, c, half * HALF:(half + 1) * HALF], start=(c == 0), stop=(c == C - 1))
                last.then_inc(rank_filled, 1)

            transpose_groups(0, END0)
            all_copied(END0)
            for t in range(NB):
                for c in range(C):
                    last = pe.matmul(bank(4)[:, t * E:(t + 1) * E], xT_a[:, c, t * T:(t + 1) * T], wrT[:, c, :], start=(c == 0), stop=(c == C - 1))
            last.then_inc(router_in, 1)
            for half in range(2):
                for c in range(C):
                    last = pe.matmul(bank(2 + half), a0T[:, c, :], xT_a[:, c, half * HALF:(half + 1) * HALF], start=(c == 0), stop=(c == C - 1))
            last.then_inc(rank_filled, 1)
            pe.wait_ge(gates_ready, 1)
            for t in range(NB):
                last = pe.transpose(bank(5 + t // 4)[:, (t % 4) * T:(t % 4 + 1) * T], gate16[:, t, :, :], idt)
            last.then_inc(gateT_filled, 1)
            transpose_groups(END0, END1)
            pe.wait_ge(rank_evac, 1)
            pe.wait_ge(gateT_evac, 1)
            for half in range(2):
                linear(w0T, [P] * C, b0T, lambda c, m, h: xT_a[:, c, h * HALF:(h + 1) * HALF],
                       lambda h: rank_act[:, 0, h * HALF:(h + 1) * HALF], half)
            all_copied(END1)
            fblocks = [fr(n) for n in range(FC)]
            n_gu = 0
            n_rank = 1
            for half in range(2):
                pe.wait_ge(lin_evac, C * (2 + half))
                hs = slice(half * HALF, (half + 1) * HALF)
                rank_products([agT, auT], xT_b, half)
                n_rank += 1
                pe.wait_ge(rank_evac, n_rank)
                for n in range(FC):
                    m = fr(n)
                    if n_gu >= 2:
                        pe.wait_ge(gu_evac, n_gu - 1)
                    for k, (w, bT) in enumerate(((wgT, bgT), (wuT, buT))):
                        dst = bank(2 + 2 * (n_gu % 2) + k)[0:m, :]
                        for c in range(C):
                            pe.matmul(dst, w[:, c, n * P:n * P + m], xT_b[:, c, hs], start=(c == 0), stop=False)
                        last = pe.matmul(dst, bT[:, n * P:n * P + m], rank_act[:, k, hs], start=False, stop=True)
                    last.then_inc(gu_filled, 1)
                    n_gu += 1
                pe.wait_ge(gu_evac, n_gu)
                for n in range(FC):
                    last = pe.matmul(bank(2), adT[0:fr(n), n, :], act_T[0:fr(n), n, :], start=(n == 0), stop=(n == FC - 1))
                last.then_inc(rank_filled, 1)
                n_rank += 1
                pe.wait_ge(rank_evac, n_rank)
                linear(wdT, fblocks, bdT, lambda c, m, h: act_T[0:m, c, :], lambda h: rank_act[:, 0, h * HALF:(h + 1) * HALF], half)
            pe.wait_ge(lin_evac, 4 * C)
            for half in range(2):
                rank_products([a2T], xT_a, half)
                n_rank += 1
                pe.wait_ge(rank_evac, n_rank)
                linear(w2T, [P] * C, b2R, lambda c, m, h: xT_a[:, c, h * HALF:(h + 1) * HALF],
                       lambda h: rank_act[:, 0, h * HALF:(h + 1) * HALF], half)

        def copy_out(eng, g):
            _, dst, src = transposes_of(g)
            eng.wait_ge(tr_filled[g % 2], g // 2 + 1)
            f = nc.scalar.copy if g % 2 == 0 else nc.vector.tensor_copy
            if g == AD_TAIL:
                f(dst, src)
                n = FC - 1
                dst, src = adT[0:FR, n, :], banks[0:FR, g % 2, (n % 4) * P:(n % 4 + 1) * P]
            f(dst, src).then_inc(tr_evac[g % 2], 1)

        @block.scalar
        def _(act):
            for g in range(0, END0, 2):
                copy_out(act, g)
            act.wait_ge(router_d, 1)
            nc.scalar.activation(rt[:, 0, :, 1], rt[:, 0, :, 0], ACT.Exp).then_inc(router_exp, 1)
            act.wait_ge(gateT_filled, 1)
            nc.scalar.mul(xT_b[:, 0, 0:HALF], bank(5), 2.0)
            nc.scalar.mul(xT_b[:, 0, HALF:], bank(6), 2.0).then_inc(gateT_evac, 1)
            for g in range(END0 + END0 % 2, END1, 2):
                copy_out(act, g)
            for n in range(2 * FC):
                m = fr(n % FC)
                act.wait_ge(gu_filled, n + 1)
                if n >= 2:
                    act.wait_ge(gu_evac, n - 1)
                nc.scalar.activation(silu[0:m, n % 2, :], bank(2 + 2 * (n % 2))[0:m, :], ACT.Silu).then_inc(silu_done, 1)

        @block.vector
        def _(dve):
            steps = [0]

            def link(ins):
                steps[0] += 1
                ins.then_inc(dve_step, 1)
                dve.wait_ge(dve_step, steps[0])

            for g in range(1, END0, 2):
                copy_out(dve, g)
            dve.wait_ge(small_in, 80)
            link(nc.vector.tensor_copy(rt[:, 5, :, 0], ints[:, 0, :]))
            e_index = const[:, K_E:K_FR].rearrange("p (o e) -> p o e", o=1).to_broadcast([P, NB, E])

            def per_tile(col):
                return col.to_broadcast([P, NB, E])
            link(nc.vector.tensor_tensor(rt[:, 1, :, :], e_index, per_tile(rt[:, 5, :, 0:1]), ALU.is_equal))
            dve.wait_ge(router_in, 1)
            link(nc.vector.scalar_tensor_tensor(logit[:, :, :], rt[:, 1, :, :], 5.0,
                                                bank(4)[:, 0:NB * E].rearrange("p (t e) -> p t e", t=NB), ALU.mult, ALU.add))
            for t in range(NB):
                last = nc.vector.max(top[:, t, :], logit[:, t, :])
            link(last)
            for t in range(NB):
                last = nc.vector.max_index(topi[:, t, :], top[:, t, :], logit[:, t, :])
            link(last)
            link(nc.vector.tensor_copy(rt[:, 5, :, 0:2], topi[:, :, 0:2]))
            nc.vector.tensor_tensor(rt[:, 0, :, 0], top[:, :, 1], top[:, :, 0], ALU.subtract).then_inc(router_d, 1)
            dve.wait_ge(router_exp, 1)
            link(nc.vector.tensor_scalar(rt[:, 0, :, 2], rt[:, 0, :, 1], 1.0, None, ALU.add))
            link(nc.vector.reciprocal(rt[:, 0, :, 3], rt[:, 0, :, 2]))
            link(nc.vector.tensor_tensor(rt[:, 0, :, 4], rt[:, 0, :, 1], rt[:, 0, :, 3], ALU.mult))
            for k in range(2):
                link(nc.vector.tensor_tensor(rt[:, 1 + k, :, :], e_index, per_tile(rt[:, 5, :, k:k + 1]), ALU.is_equal))
                link(nc.vector.tensor_tensor(rt[:, 3 + k, :, :], rt[:, 1 + k, :, :], per_tile(rt[:, 0, :, 3 + k:4 + k]), ALU.mult))
            link(nc.vector.tensor_tensor(rt[:, 1, :, :], rt[:, 3, :, :], rt[:, 4, :, :], ALU.add))
            nc.vector.tensor_copy(gate16.rearrange("p t e r -> p (t e) r"),
                                  rt[:, 1, :, :].rearrange("p t (e o) -> p (t e) o", o=1).to_broadcast([P, NB * E, R])).then_inc(gates_ready, 1)
            dve.wait_ge(rank_filled, 1)
            dve.wait_ge(gateT_evac, 1)
            nc.vector.tensor_tensor(rank_act[:, 0, 0:HALF], bank(2), xT_b[:, 0, 0:HALF], ALU.mult)
            nc.vector.tensor_tensor(rank_act[:, 0, HALF:], bank(3), xT_b[:, 0, HALF:], ALU.mult).then_inc(rank_evac, 1)
            for g in range(END0 + 1 - END0 % 2, END1, 2):
                copy_out(dve, g)

            def block_of(x, k):
                return x[:, k % C, (k // C % 2) * HALF:(k // C % 2 + 1) * HALF]

            def residual(k, dst, src):
                dve.wait_ge(lin_filled, k + 1)
                nc.vector.tensor_tensor(block_of(dst, k), bank(6 + k % 2), block_of(src, k), ALU.add).then_inc(lin_evac, 1)

            def own_rows(srcs, half, scale, n_rank):
                dve.wait_ge(rank_filled, n_rank)
                for k, src in enumerate(srcs):
                    for b in range(HALF // T):
                        t = half * HALF + b * T
                        last = nc.vector.tensor_scalar(rank_act[:, k, t:t + T], src[:, b * T:(b + 1) * T],
                                                       blockmask[:, t // T:t // T + 1], scale, ALU.mult, ALU.mult)
                last.then_inc(rank_evac, 1)

            for k in range(2 * C):
                residual(k, xT_b, xT_a)
            n_rank = 1
            n = 0
            for half in range(2):
                n_rank += 1
                own_rows([bank(2), bank(3)], half, 0.5, n_rank)
                for fc in range(FC):
                    m = fr(fc)
                    dve.wait_ge(silu_done, n + 1)
                    nc.vector.tensor_tensor(act_T[0:m, fc, :], silu[0:m, n % 2, :], bank(3 + 2 * (n % 2))[0:m, :], ALU.mult).then_inc(gu_evac, 1)
                    n += 1
                n_rank += 1
                own_rows([bank(2)], half, 0.5, n_rank)
                for k in range((2 + half) * C, (3 + half) * C):
                    residual(k, xT_a, xT_b)
            for half in range(2):
                n_rank += 1
                own_rows([bank(2)], half, 2.0, n_rank)
                for k in range((4 + half) * C, (5 + half) * C):
                    dve.wait_ge(lin_filled, k + 1)
                    nc.vector.scalar_tensor_tensor(block_of(xT_b, k), bank(6 + k % 2), bias2[:, k % C:k % C + 1], block_of(xT_a, k),
                                                   ALU.add, ALU.add).then_inc(lin_evac, 1)


def place_of_weights(n, wqT, wkvT, woT):
    if n < 8:
        return wqT[:, :, :, n * P:(n + 1) * P]
    if n < 12:
        j, k = (n - 8) % 2, (n - 8) // 2
        return wkvT[:, :, :, j, k * DH:(k + 1) * DH]
    return woT[:, :, (n % 2) * REP:(n % 2 + 1) * REP, (n - 12) // 2 * P:((n - 12) // 2 + 1) * P]


def attention_setup(nc, const, xT, ints, q_w, k_w, banks, acc, lens, ident_r, x_scratch, tab_scratch):
    ident = const[:, K_ID:K_BM]

    def bank(n):
        return banks[:, n, :]

    with ExitStack() as ctx:
        def sb(name, shape, dt=fp32):
            return ctx.enter_context(nc.sbuf_tensor(name, shape, dt))

        def sem(name):
            return ctx.enter_context(nc.semaphore(name))

        tabs = sb("tabs", [P, NB, 4, DH])
        ang = sb("ang", [P, 4, NB * DH // 2])
        xs = sb("xs", [P, 2, C, NT], fp32r)
        ang_ready, sin_ready, tabs_ready = sem("ang_ready"), sem("sin_ready"), sem("tabs_ready")
        hi_ready, split_ready = sem("hi_ready"), sem("split_ready")
        x_filled, x_evac = sem("x_filled"), sem("x_evac")
        step = sem("step")
        stored = sem("stored")

        block = ctx.enter_context(nc.Block())

        @block.sync
        def _(sp):
            sp.wait_ge(split_ready, 1)
            for b in range(NB):
                sp.dma_start(x_scratch[b], xs[:, :, :, b * T:(b + 1) * T].bitcast(fp32)).then_inc(stored, 16)
            sp.wait_ge(tabs_ready, 2)
            sp.dma_start(tab_scratch.rearrange("b p k d -> p b k d"), tabs[:, :, :, :]).then_inc(stored, 16)
            sp.wait_ge(stored, 16 * (NB + 1))

        @block.tensor
        def _(pe):
            for t in range(NB):
                for c in range(C):
                    last = pe.transpose(bank(t)[:, c * P:(c + 1) * P], xT[:, c, t * T:(t + 1) * T], ident)
                last.then_inc(x_filled, 1)

        @block.scalar
        def _(act):
            nc.scalar.copy(xs[:, 0, :, :], xT[:, :, :]).then_inc(hi_ready, 1)
            act.wait_ge(ang_ready, 1)
            nc.scalar.activation(ang[:, 0:2, :], ang[:, 0:2, :], ACT.Sin).then_inc(sin_ready, 1)
            for t in range(NB):
                act.wait_ge(x_filled, t + 1)
                nc.scalar.copy(acc[:, t, :], bank(t)).then_inc(x_evac, 1)

        @block.vector
        def _(dve):
            n = [0]

            def link(ins):
                n[0] += 1
                ins.then_inc(step, 1)
                dve.wait_ge(step, n[0])
            nc.vector.tensor_copy(ident_r[:, :], ident)
            link(nc.vector.tensor_copy(lens[:, :], ints[:, 1, :]))
            pos = ang[:, 3, 0:NB]
            link(nc.vector.tensor_scalar(pos, lens[:, :], const[:, K_P:K_P + 1], None, ALU.add))
            f = ang[:, 2, :].rearrange("p (b i) -> p b i", b=NB)
            link(nc.vector.tensor_tensor(f, pos.rearrange("p (b o) -> p b o", o=1).to_broadcast([P, NB, DH // 2]),
                                         const[:, K_FR:K_P].rearrange("p (o i) -> p o i", o=1).to_broadcast([P, NB, DH // 2]), ALU.mult))
            for k, shift in ((0, 0.0), (1, 0.25)):
                turns, r = ang[:, 3, :], ang[:, k, :]
                link(nc.vector.tensor_scalar(turns, ang[:, 2, :], 1.0 / TWO_PI, shift, ALU.mult, ALU.add))
                link(nc.vector.tensor_scalar(turns, turns, ROUND, None, ALU.add))
                link(nc.vector.tensor_scalar(turns, turns, -ROUND, None, ALU.add))
                link(nc.vector.scalar_tensor_tensor(r, turns, -C1, ang[:, 2, :], ALU.mult, ALU.add))
                link(nc.vector.scalar_tensor_tensor(r, turns, -C2, r, ALU.mult, ALU.add))
                link(nc.vector.scalar_tensor_tensor(r, turns, -C3, r, ALU.mult, ALU.add))
                link(nc.vector.tensor_scalar(r, r, TWO_PI * shift, None, ALU.add))
                last = nc.vector.tensor_scalar(r, r, 3.1415925, -3.1415925, ALU.min, ALU.max)
                if k == 0:
                    link(last)
            last.then_inc(ang_ready, 1)
            dve.wait_ge(hi_ready, 1)
            nc.vector.tensor_tensor(xs[:, 1, :, :], xT[:, :, :], xs[:, 0, :, :].bitcast(fp32), ALU.subtract).then_inc(split_ready, 1)
            dve.wait_ge(sin_ready, 1)
            h = DH // 2

            def rows_of(x, lo):
                return x[:, lo:lo + h].rearrange("p (o i) -> p o i", o=1).to_broadcast([P, NB, h])
            sin, cos = (ang[:, k, :].rearrange("p (b i) -> p b i", b=NB) for k in range(2))
            for k, w in enumerate((q_w, k_w)):
                nc.vector.tensor_tensor(tabs[:, :, k, 0:h], cos, rows_of(w, 0), ALU.mult)
                nc.vector.tensor_tensor(tabs[:, :, k, h:DH], cos, rows_of(w, h), ALU.mult)
                nc.vector.scalar_tensor_tensor(tabs[:, :, 2 + k, 0:h], sin, -1.0, rows_of(w, h), ALU.mult, ALU.mult)
                nc.vector.tensor_tensor(tabs[:, :, 2 + k, h:DH], sin, rows_of(w, 0), ALU.mult).then_inc(tabs_ready, 1)


def attention(nc, a, out, const, banks, acc, lens, ident_r, x_scratch, tab_scratch):
    ident = const[:, K_ID:K_BM]
    key_index = const[:, K_IO:K_E]

    def bank(n):
        return banks[:, n, :]

    QP, OUT, SNEW = bank(0), bank(2), bank(5)
    flat01 = banks[:, 0:2, :].rearrange("p n c -> p (n c)")
    QK5 = flat01[:, 0:5 * DH].rearrange("p (h d) -> p h d", h=5)
    KV = bank(1)[:, 0:2 * DH]
    VN = bank(1)[:, DH:2 * DH]
    KTN = bank(1)[:, 2 * DH:2 * DH + T]
    KTC, QT = bank(3), bank(4)
    PT = (bank(6), bank(7))

    with ExitStack() as ctx:
        def sb(name, shape, dt=fp32):
            return ctx.enter_context(nc.sbuf_tensor(name, shape, dt))

        RING = 10
        GROUPS, QKV_GROUPS = 20, 12
        pages = sb("pages", [1, NB * NPP], i32)
        w_raw = sb("w_raw", [P, RING, D])
        wqT = sb("wqT", [P, 2, C, 2 * REP * DH], fp32r)
        wkvT = sb("wkvT", [P, 2, C, 2, 2 * DH], fp32r)
        woT = sb("woT", [P, 2, 2 * REP, D], fp32r)
        xb = sb("xb", [P, 2, C, T], fp32r)
        tab = sb("tab", [P, 4, DH])
        len_b = sb("len_b", [P, 1])
        k_raw = sb("k_raw", [P, KC, 2, DH])
        v_raw = sb("v_raw", [P, KC, 2, DH])
        mask = sb("mask", [P, L])
        unused = sb("unused", [P, REP])
        ss = sb("ss", [P, 3, 5])
        half_power = sb("half_power", [P, 5])
        qn = sb("qn", [P, 5, DH])
        qr = sb("qr", [P, 5, DH])
        rope_b = sb("rope_b", [P, 5, DH])
        sq = rope_b
        qT = [sb(f"qT{s}", [P, 2, REP, T], fp32r) for s in range(2)]
        kT = [sb(f"kT{s}", [P, 2, KEYS], fp32r) for s in range(2)]
        v_new = [sb(f"v_new{s}", [P, DH]) for s in range(2)]
        v = [sb(f"v{s}", [P, 2, KC + 1, DH], fp32r) for s in range(2)]
        probs = [sb(f"probs{s}", [P, REP, KEYS]) for s in range(2)]
        stat = sb("stat", [P, 3, REP])
        sums = sb("sums", [P, 4, REP])
        pT = [sb(f"pT{s}", [P, 2, REP * T], fp32r) for s in range(2)]
        oT = sb("oT", [P, 2, REP * T], fp32r)

        count = {}

        def sem(name, n=0):
            s = ctx.enter_context(nc.semaphore(name))
            if n:
                count[s.name] = n
            return s

        pages_in, w_in = sem("pages_in"), [sem(f"w_in{n}") for n in range(RING)]
        wt_filled, wt_hi, wt_lo = sem("wt_filled"), sem("wt_hi"), sem("wt_lo")
        row_in, tab_in, len_in, k_in, v_in = sem("row_in"), sem("tab_in"), sem("len_in"), sem("k_in"), sem("v_in")
        mask_ready, power_set = sem("mask_ready"), sem("power_set")
        out_stored = sem("out_stored")
        proj_filled = sem("proj_filled", 1)
        squared = sem("squared", 1)
        summed, ms_ready = sem("summed", 1), sem("ms_ready", 1)
        inv_rms = sem("inv_rms", 1)
        qn_ready = sem("qn_ready", 1)
        crossed = sem("crossed", 1)
        rotated = sem("rotated", 1)
        v_hi, v_ready = sem("v_hi", 1), sem("v_ready", 1)
        ktc_filled, ktc_hi, ktc_evac = sem("ktc_filled", 1), sem("ktc_hi", 1), sem("ktc_evac", 1)
        qt_filled, qt_hi, qt_evac = sem("qt_filled", 1), sem("qt_hi", 1), sem("qt_evac", 1)
        snew_filled = sem("snew_filled", 1)
        s_filled = sem("s_filled", REP)
        newmax = sem("newmax", 2)
        masked = sem("masked", REP)
        exp_done = sem("exp_done", REP)
        total, inverse = sem("total", 1), sem("inverse", 1)
        scaled = sem("scaled", REP)
        pt_filled = sem("pt_filled", KC + 1)
        p_hi_evac, p_lo_evac = sem("p_hi_evac", KC + 1), sem("p_lo_evac", KC + 1)
        pv_done = sem("pv_done", KC + 1)
        o_hi, o_ready = sem("o_hi", 1), sem("o_ready", 1)
        out_filled, out_evac = sem("out_filled", 1), sem("out_evac", 1)

        def wait(eng, s, u, n=None):
            k = count[s.name]
            eng.wait_ge(s, (u + 2) * k + (k if n is None else n))

        def before_first(eng, sems):
            for s in sems:
                eng.sem_inc(s, 2 * count[s.name])

        def row_count(u, n):
            return (u + 2) * (n // 2)

        def loops(eng, prepare, front, unit, tail):
            def pair(g, nxt):
                u0 = g * UNITS
                front(u0, 0, g)
                unit(u0, 0, 0, False, False, True, None)
                unit(u0 + 1, 1, 0, True, False, True, None)
                with eng.Fori(0, NB - 2) as row:
                    b = row + 1
                    u = u0 + 2 * b
                    unit(u, 0, b, True, True, True, None)
                    unit(u + 1, 1, b, True, True, True, None)
                u = u0 + 2 * (NB - 1)
                unit(u, 0, NB - 1, True, True, True, None)
                unit(u + 1, 1, NB - 1, True, True, False, nxt)
                tail(u + 1, 1, NB - 1, nxt)

            prepare(0, range(QKV_GROUPS))
            with eng.Fori(0, NGP - 1) as g:
                pair(g, g + 1)
            pair(NGP - 1, None)

        def pt_slot_free(eng, u, c):
            if c < 2:
                wait(eng, pv_done, u - 1)
            else:
                wait(eng, pv_done, u, c - 1)

        def weight_bank(n):
            return bank(n % 2 if n < QKV_GROUPS else 6 + n % 2)

        def flat(x):
            return x.rearrange("p h t -> p (h t)")

        block = ctx.enter_context(nc.Block())

        @block.sync
        def _(sp):
            sp.dma_start(pages[:, :], a["itok_Bx16_0_63"].rearrange("(o b) n -> o (b n)", o=1)).then_inc(pages_in, 16)
            sp.wait_ge(pages_in, 16)
            wq = a["L3_cond_Wq"].rearrange("(g n p) d -> g n p d", g=NGP, p=P)
            wk = a["L3_cond_Wk"].rearrange("(g n p) d -> g n p d", g=NGP, p=P)
            wv = a["L3_cond_Wv"].rearrange("(g n p) d -> g n p d", g=NGP, p=P)
            wo = a["L3_cond_Wo"].rearrange("(o p) (g j k) -> g o j p k", p=P, g=NGP, j=2)
            cache = {"k": a["L3_cond_k_cache"], "v": a["L3_cond_v_cache"]}

            def load_weights(g, n):
                if n < 8:
                    src = wq[bass.ds(g, 1), n]
                elif n < 12:
                    src = (wk if n < 10 else wv)[bass.ds(g, 1), n % 2]
                else:
                    src = wo[bass.ds(g, 1), (n - 12) // 2, n % 2]
                sp.wait_ge(wt_filled, g * GROUPS + n + 1)
                sp.dma_start(w_raw[:, n % RING, :], src.rearrange("o p d -> (o p) d")).then_inc(w_in[n % RING], 16)

            def gather(dst, kind, g, page, s):
                for n in range(NPP):
                    sp.dma_start(dst[PSIZE * (n % 4):PSIZE * (n % 4 + 1), n // 4, :, :],
                                 cache[kind][bass.ds(page[n], 1), :, bass.ds(2 * g, 2), :].rearrange("o s h d -> (o s) h d")).then_inc(s, 16)

            def load_front(g, b):
                u = g * UNITS + 2 * b
                wait(sp, proj_filled, u - 1)
                sp.dma_start(xb[:, :, :, :].bitcast(fp32), x_scratch[bass.ds(b, 1)].rearrange("o p k c t -> (o p) k c t")).then_inc(row_in, 16)
                page = [sp.value_load(pages[0:1, bass.ds(b * NPP + n, 1)], min_val=0, max_val=PAGES - 1) for n in range(NPP)]
                wait(sp, crossed, u - 1)
                sp.dma_start(tab[:, :, :], tab_scratch[bass.ds(b, 1)].rearrange("o p k d -> (o p) k d")).then_inc(tab_in, 16)
                wait(sp, ktc_filled, u - 1)
                gather(k_raw, "k", g, page, k_in)
                sp.wait_ge(mask_ready, (u + 2) // 2)
                sp.dma_start(len_b[:, :], lens[:, bass.ds(b, 1)]).then_inc(len_in, 16)
                return page

            def load_values(g, b, page):
                wait(sp, v_ready, g * UNITS + 2 * b - 1)
                gather(v_raw, "v", g, page, v_in)

            with sp.Fori(0, NGP) as g:
                for n in range(RING):
                    load_weights(g, n)
                page = load_front(g, 0)
                for n in range(RING, GROUPS):
                    load_weights(g, n)
                load_values(g, 0, page)
                with sp.Fori(0, NB - 1) as row:
                    load_values(g, row + 1, load_front(g, row + 1))
            wait(sp, out_evac, NGP * UNITS - 1)
            sp.dma_start(out.rearrange("b t d -> t b d"), acc[:, :, :]).then_inc(out_stored, 16)
            sp.wait_ge(out_stored, 16)

        @block.tensor
        def _(pe):
            before_first(pe, [proj_filled, ktc_filled, qt_filled, snew_filled, s_filled, pt_filled, pv_done, out_filled])
            pe.sem_inc(wt_filled, RING)

            def product(dst, w, x, start, stop):
                pe.matmul(dst, w[0], x[0], start=start, stop=False)
                pe.matmul(dst, w[0], x[1], start=False, stop=False)
                return pe.matmul(dst, w[1], x[0], start=False, stop=stop)

            def halves(x, *at):
                return x[(slice(None), 0) + at], x[(slice(None), 1) + at]

            def prepare(g, groups):
                for n in groups:
                    pe.wait_ge(w_in[n % RING], (g * (GROUPS // RING) + n // RING + 1) * 16)
                    if n == 0:
                        wait(pe, qt_evac, g * UNITS - 1)
                    if n >= 2 and n not in (QKV_GROUPS, QKV_GROUPS + 1):
                        pe.wait_ge(wt_lo, g * GROUPS + n - 1)
                    for c in range(C):
                        last = pe.transpose(weight_bank(n)[:, c * P:(c + 1) * P], w_raw[:, n % RING, c * P:(c + 1) * P], ident)
                    last.then_inc(wt_filled, 1)

            def project_q(u, j):
                if j == 0:
                    pe.wait_ge(row_in, row_count(u, 16))
                wait(pe, qn_ready, u - 1)
                for c in range(C):
                    product(QP, halves(xb, c), halves(wqT, c, slice(j * REP * DH, (j + 1) * REP * DH)), c == 0, c == C - 1)

            def project_kv(u, j):
                wait(pe, qt_evac, u - 1)
                for c in range(C):
                    last = product(KV, halves(xb, c), halves(wkvT, c, j), c == 0, c == C - 1)
                last.then_inc(proj_filled, 1)

            def cached_keys(u, j):
                if j == 0:
                    pe.wait_ge(k_in, row_count(u, 16 * NPP))
                wait(pe, masked, u - 1, 3)
                for c in range(KC):
                    last = pe.transpose(KTC[:, c * P:(c + 1) * P], k_raw[:, c, j, :], ident)
                last.then_inc(ktc_filled, 1)

            def queries(u):
                wait(pe, rotated, u)
                wait(pe, masked, u - 1, 4)
                for h in range(REP):
                    pe.transpose(QT[:, h * T:(h + 1) * T], qr[:, h, :], ident)
                pe.transpose(KTN, qr[:, REP, :], ident).then_inc(qt_filled, 1)

            def new_scores(u, s):
                wait(pe, qt_evac, u)
                wait(pe, exp_done, u - 1)
                for h in range(REP):
                    last = product(SNEW[:, h * T:(h + 1) * T], halves(qT[s], h), halves(kT[s], slice(L, KEYS)), True, True)
                last.then_inc(snew_filled, 1)

            def scores(u, s, h):
                wait(pe, ktc_evac, u)
                if h >= 2:
                    wait(pe, masked, u, h - 1)
                product(bank(3 + h % 2), halves(qT[s], h), halves(kT[s], slice(0, L)), True, True).then_inc(s_filled, 1)

            def turn_probs(u, j, c):
                if c == 0:
                    wait(pe, scaled, u)
                if c >= 2:
                    wait(pe, p_lo_evac, u, c - 1)
                for h in range(REP):
                    last = pe.transpose(PT[c % 2][:, h * T:(h + 1) * T], probs[j][:, h, c * P:(c + 1) * P], ident)
                last.then_inc(pt_filled, 1)

            def values(u, j, c):
                if c == 0:
                    wait(pe, v_ready, u)
                    wait(pe, out_evac, u - 1)
                wait(pe, p_lo_evac, u, c + 1)
                product(OUT, halves(v[j], c), halves(pT[c % 2]), c == 0, c == KC).then_inc(pv_done, 1)

            def project_out(u, j):
                wait(pe, o_ready, u)
                for h in range(REP):
                    last = product(OUT, halves(oT, slice(h * T, (h + 1) * T)), halves(woT, j * REP + h), h == 0, h == REP - 1)
                last.then_inc(out_filled, 1)

            def front(u, j, g):
                pe.wait_ge(wt_lo, g * GROUPS + QKV_GROUPS)
                project_q(u, j)
                project_kv(u, j)
                cached_keys(u, j)
                prepare(g, range(QKV_GROUPS, GROUPS))
                queries(u)

            def tail(u, j, b, nxt):
                values(u - 1, 1 - j, KC)
                turn_probs(u, j, 0)
                if nxt is not None:
                    prepare(nxt, [6])
                project_out(u - 1, 1 - j)
                for c in range(1, KC + 1):
                    turn_probs(u, j, c)
                    if nxt is not None:
                        prepare(nxt, [6 + c])
                    values(u, j, c - 1)
                values(u, j, KC)
                if nxt is not None:
                    prepare(nxt, [11])
                project_out(u, j)

            def unit(u, j, b, attend_last, finish_last, follow, nxt):
                if follow:
                    project_q(u + 1, 1 - j)
                if nxt is not None:
                    prepare(nxt, [0, 1, 2])
                if finish_last:
                    values(u - 2, j, KC)
                if follow:
                    project_kv(u + 1, 1 - j)
                if nxt is not None:
                    prepare(nxt, [3])
                if attend_last and not finish_last:
                    pe.wait_ge(wt_lo, (u + 1) // UNITS * GROUPS + GROUPS)
                if attend_last:
                    turn_probs(u - 1, 1 - j, 0)
                new_scores(u, j)
                scores(u, j, 0)
                scores(u, j, 1)
                if finish_last:
                    project_out(u - 2, j)
                for c in range(1, KC + 1):
                    if attend_last:
                        turn_probs(u - 1, 1 - j, c)
                    if c < 3:
                        scores(u, j, 1 + c)
                    if attend_last:
                        values(u - 1, 1 - j, c - 1)
                    if c == 2 and follow:
                        cached_keys(u + 1, 1 - j)
                    if c == 3 and follow:
                        queries(u + 1)
                    if c in (2, 3) and nxt is not None:
                        prepare(nxt, [2 + c])

            loops(pe, prepare, front, unit, tail)

        @block.scalar
        def _(act):
            before_first(act, [squared, v_hi, ktc_hi, qt_hi, exp_done, p_hi_evac, o_hi])

            def prepare(g, groups):
                for n in groups:
                    act.wait_ge(wt_filled, g * GROUPS + n + 1 + RING)
                    nc.scalar.copy(place_of_weights(n, wqT, wkvT, woT)[:, 0], weight_bank(n).rearrange("p (c t) -> p c t", c=C)).then_inc(wt_hi, 1)

            def squares(u, j):
                wait(act, proj_filled, u)
                wait(act, v_ready, u - 2)
                nc.scalar.copy(v_new[j][:, :], VN)
                wait(act, rotated, u - 1)
                nc.scalar.activation(sq[:, :, :], QK5, ACT.Square).then_inc(squared, 1)

            def cached_keys(u, j):
                wait(act, ktc_filled, u)
                wait(act, s_filled, u - 2)
                nc.scalar.copy(kT[j][:, 0, 0:L], KTC).then_inc(ktc_hi, 1)

            def queries(u, j):
                wait(act, qt_filled, u)
                nc.scalar.copy(kT[j][:, 0, L:KEYS], KTN)
                nc.scalar.copy(flat(qT[j][:, 0, :, :]), QT).then_inc(qt_hi, 1)

            def split_values(u, j):
                if j == 0:
                    act.wait_ge(v_in, row_count(u, 16 * NPP))
                wait(act, pv_done, u - 2)
                wait(act, v_ready, u - 2)
                nc.scalar.copy(v[j][:, 0, 0:KC, :], v_raw[:, :, j, :])
                nc.scalar.copy(v[j][:, 0, KC, :], v_new[j][:, :]).then_inc(v_hi, 1)

            def exps(u, h, s):
                wait(act, masked, u, h + 1)
                nc.scalar.activation(probs[s][:, h, 0:L], probs[s][:, h, 0:L], ACT.Exp, bias=stat[:, 2, h:h + 1], scale=-1.0,
                                     accum_out=sums[:, 0, h:h + 1])
                nc.scalar.activation(probs[s][:, h, L:KEYS], SNEW[:, h * T:(h + 1) * T], ACT.Exp, bias=stat[:, 2, h:h + 1], scale=SCALE,
                                     accum_out=sums[:, 1, h:h + 1]).then_inc(exp_done, 1)

            def probs_out(u, c):
                wait(act, pt_filled, u, c + 1)
                pt_slot_free(act, u, c)
                nc.scalar.copy(pT[c % 2][:, 0, :], PT[c % 2]).then_inc(p_hi_evac, 1)

            def output(u):
                wait(act, pv_done, u)
                wait(act, out_filled, u - 1)
                nc.scalar.copy(oT[:, 0, :], OUT).then_inc(o_hi, 1)

            def front(u, j, g):
                squares(u, j)
                cached_keys(u, j)
                prepare(g, range(QKV_GROUPS, GROUPS))
                queries(u, j)

            def tail(u, j, b, nxt):
                output(u - 1)
                for c in range(KC + 1):
                    probs_out(u, c)
                    if nxt is not None:
                        prepare(nxt, [6 + c])
                output(u)
                if nxt is not None:
                    prepare(nxt, [11])

            def unit(u, j, b, attend_last, finish_last, follow, nxt):
                if nxt is not None:
                    prepare(nxt, [0, 1, 2])
                if finish_last:
                    output(u - 2)
                if nxt is not None:
                    prepare(nxt, [3])
                if follow:
                    squares(u + 1, 1 - j)
                if attend_last:
                    probs_out(u - 1, 0)
                exps(u, 0, j)
                for c in range(1, KC + 1):
                    if attend_last:
                        probs_out(u - 1, c)
                    if c < REP:
                        exps(u, c, j)
                    if c == 2 and follow:
                        cached_keys(u + 1, 1 - j)
                    if c == 3 and follow:
                        queries(u + 1, 1 - j)
                    if c in (2, 3) and nxt is not None:
                        prepare(nxt, [2 + c])
                split_values(u, j)

            loops(act, prepare, front, unit, tail)

        @block.gpsimd
        def _(pool):
            before_first(pool, [inv_rms, crossed, rotated, v_ready])
            pool.memset(half_power[:, :], -0.5).then_inc(power_set, 1)
            pool.wait_ge(power_set, 1)

            def front(u, j, g):
                if j == 0:
                    pool.wait_ge(tab_in, row_count(u, 16))
                wait(pool, ms_ready, u)
                wait(pool, qn_ready, u - 1)
                nc.gpsimd.tensor_tensor(ss[:, 2, :], ss[:, 1, :], half_power[:, :], ALU.pow).then_inc(inv_rms, 1)
                wait(pool, qn_ready, u)
                wait(pool, qt_filled, u - 1)
                h = DH // 2
                nc.gpsimd.tensor_tensor(qr[:, 0:REP, :], qn[:, 0:REP, :], tab[:, 0:1, :].to_broadcast([P, REP, DH]), ALU.mult)
                nc.gpsimd.tensor_tensor(qr[:, REP, :], qn[:, REP, :], tab[:, 1, :], ALU.mult)
                for lo, of in ((0, h), (h, 0)):
                    nc.gpsimd.tensor_tensor(rope_b[:, 0:REP, lo:lo + h], qn[:, 0:REP, of:of + h], tab[:, 2:3, lo:lo + h].to_broadcast([P, REP, h]), ALU.mult)
                    last = nc.gpsimd.tensor_tensor(rope_b[:, REP, lo:lo + h], qn[:, REP, of:of + h], tab[:, 3, lo:lo + h], ALU.mult)
                last.then_inc(crossed, 1)
                wait(pool, crossed, u)
                nc.gpsimd.tensor_tensor(qr[:, :, :], qr[:, :, :], rope_b[:, :, :], ALU.add).then_inc(rotated, 1)

            def split_values(u, j):
                wait(pool, v_hi, u)
                nc.gpsimd.tensor_tensor(v[j][:, 1, 0:KC, :], v_raw[:, :, j, :], v[j][:, 0, 0:KC, :].bitcast(fp32), ALU.subtract)
                nc.gpsimd.tensor_tensor(v[j][:, 1, KC, :], v_new[j][:, :], v[j][:, 0, KC, :].bitcast(fp32), ALU.subtract).then_inc(v_ready, 1)

            def nothing(*_):
                pass

            def unit(u, j, b, attend_last, finish_last, follow, nxt):
                if follow:
                    front(u + 1, 1 - j, None)
                split_values(u, j)

            loops(pool, nothing, front, unit, nothing)

        @block.vector
        def _(dve):
            dve.sem_inc(mask_ready, 1)
            before_first(dve, [summed, ms_ready, qn_ready, ktc_evac, newmax, masked, total, inverse,
                               scaled, p_lo_evac, qt_evac, o_ready, out_evac])

            def prepare(g, groups):
                for n in groups:
                    dve.wait_ge(wt_hi, g * GROUPS + n + 1)
                    w = place_of_weights(n, wqT, wkvT, woT)
                    nc.vector.tensor_tensor(w[:, 1], weight_bank(n).rearrange("p (c t) -> p c t", c=C), w[:, 0].bitcast(fp32), ALU.subtract).then_inc(wt_lo, 1)

            def mean_squares(u):
                wait(dve, squared, u)
                nc.vector.tensor_reduce(ss[:, 0, :], sq[:, :, :], AX.X, ALU.add).then_inc(summed, 1)
                wait(dve, summed, u)
                wait(dve, inv_rms, u - 1)
                nc.vector.tensor_scalar(ss[:, 1, :], ss[:, 0, :], 1.0 / DH, EPS, ALU.mult, ALU.add).then_inc(ms_ready, 1)

            def normed(u):
                wait(dve, inv_rms, u)
                wait(dve, rotated, u - 1)
                nc.vector.tensor_tensor(qn[:, :, :], QK5, ss[:, 2, :].rearrange("p (h o) -> p h o", o=1).to_broadcast([P, 5, DH]), ALU.mult).then_inc(qn_ready, 1)

            def row_mask(u):
                dve.wait_ge(len_in, row_count(u, 16))
                wait(dve, masked, u - 1)
                nc.vector.tensor_scalar(mask[:, :], key_index, len_b[:, 0:1], NEG, ALU.is_ge, ALU.mult).then_inc(mask_ready, 1)

            def new_maxima(u):
                wait(dve, snew_filled, u)
                wait(dve, exp_done, u - 1)
                nc.vector.tensor_reduce(stat[:, 0, :], SNEW.rearrange("p (h k) -> p h k", h=REP), AX.X, ALU.max).then_inc(newmax, 1)
                wait(dve, newmax, u, 1)
                nc.vector.tensor_scalar(stat[:, 1, :], stat[:, 0, :], -SCALE, None, ALU.mult).then_inc(newmax, 1)
                wait(dve, newmax, u, 2)

            def maxima(u, h, s):
                wait(dve, pt_filled, u - 2)
                wait(dve, s_filled, u, h + 1)
                nc.vector.memset(unused[:, h:h + 1], 0.0)
                nc.vector.tensor_tensor_reduce(out=probs[s][:, h, 0:L], in0=bank(3 + h % 2), in1=mask[:, :], scale=-SCALE,
                                               scalar=stat[:, 1, h:h + 1], op0=ALU.add, op1=ALU.min,
                                               accum_out=stat[:, 2, h:h + 1]).then_inc(masked, 1)

            def inverse_sums(u):
                wait(dve, exp_done, u)
                nc.vector.tensor_tensor(sums[:, 2, :], sums[:, 0, :], sums[:, 1, :], ALU.add).then_inc(total, 1)
                wait(dve, total, u)
                nc.vector.reciprocal(sums[:, 3, :], sums[:, 2, :]).then_inc(inverse, 1)

            def scale_probs(u, heads, s):
                wait(dve, inverse, u)
                for h in heads:
                    nc.vector.tensor_scalar(probs[s][:, h, :], probs[s][:, h, :], sums[:, 3, h:h + 1], None, ALU.mult).then_inc(scaled, 1)

            def probs_out(u, c):
                wait(dve, p_hi_evac, u, c + 1)
                nc.vector.tensor_tensor(pT[c % 2][:, 1, :], PT[c % 2], pT[c % 2][:, 0, :].bitcast(fp32), ALU.subtract).then_inc(p_lo_evac, 1)

            def queries(u, s):
                wait(dve, qt_hi, u)
                nc.vector.tensor_tensor(kT[s][:, 1, L:KEYS], KTN, kT[s][:, 0, L:KEYS].bitcast(fp32), ALU.subtract)
                nc.vector.tensor_tensor(flat(qT[s][:, 1, :, :]), QT, flat(qT[s][:, 0, :, :]).bitcast(fp32), ALU.subtract).then_inc(qt_evac, 1)

            def output(u):
                wait(dve, o_hi, u)
                nc.vector.tensor_tensor(oT[:, 1, :], OUT, oT[:, 0, :].bitcast(fp32), ALU.subtract).then_inc(o_ready, 1)

            def add_out(u, b):
                wait(dve, out_filled, u)
                wait(dve, out_evac, u - 1)
                o = acc[:, bass.ds(b, 1), :].rearrange("p o d -> p (o d)")
                nc.vector.tensor_tensor(o, OUT, o, ALU.add).then_inc(out_evac, 1)

            def cached_keys(u, s):
                wait(dve, ktc_hi, u)
                nc.vector.tensor_tensor(kT[s][:, 1, 0:L], KTC, kT[s][:, 0, 0:L].bitcast(fp32), ALU.subtract).then_inc(ktc_evac, 1)

            def front(u, j, g):
                row_mask(u)
                mean_squares(u)
                normed(u)
                cached_keys(u, j)
                prepare(g, range(QKV_GROUPS, GROUPS))
                queries(u, j)

            def tail(u, j, b, nxt):
                output(u - 1)
                for c in range(KC + 1):
                    probs_out(u, c)
                    if nxt is not None:
                        prepare(nxt, [6 + c])
                    if c == 0:
                        add_out(u - 1, b)
                output(u)
                if nxt is not None:
                    prepare(nxt, [11])
                add_out(u, b)

            def unit(u, j, b, attend_last, finish_last, follow, nxt):
                if nxt is not None:
                    prepare(nxt, [0, 1, 2])
                if finish_last:
                    output(u - 2)
                if nxt is not None:
                    prepare(nxt, [3])
                if follow:
                    mean_squares(u + 1)
                if attend_last:
                    probs_out(u - 1, 0)
                new_maxima(u)
                if j == 0:
                    dve.wait_ge(mask_ready, (u + 4) // 2)
                maxima(u, 0, j)
                if follow:
                    normed(u + 1)
                maxima(u, 1, j)
                if finish_last:
                    add_out(u - 2, b - 1)
                for c in range(1, KC + 1):
                    if attend_last:
                        probs_out(u - 1, c)
                    if c < 3:
                        maxima(u, 1 + c, j)
                    if c == 2 and follow:
                        cached_keys(u + 1, 1 - j)
                    if c in (2, 3) and nxt is not None:
                        prepare(nxt, [2 + c])
                    if c == 3:
                        if follow:
                            queries(u + 1, 1 - j)
                        inverse_sums(u)
                        scale_probs(u, (0, 1), j)
                scale_probs(u, (2, 3), j)
                if j == 1 and follow:
                    row_mask(u + 1)

            loops(dve, prepare, front, unit, tail)


_INS = ['x', 'itok_B_0_7', 'itok_B_2_6', 'itok_B_0_23', 'itok_Bx16_0_63', 'itok_B_207_1644', 'L0_cond_W', 'L0_cond_Wr', 'L0_cond_A',
        'L0_cond_B', 'L1_cond_W_gate', 'L1_cond_W_up', 'L1_cond_W_down', 'L1_cond_A_gate', 'L1_cond_B_gate', 'L1_cond_A_up',
        'L1_cond_B_up', 'L1_cond_A_down', 'L1_cond_B_down', 'L2_cond_W', 'L2_cond_b', 'L2_cond_lora_As', 'L2_cond_lora_Bs',
        'L3_cond_Wq', 'L3_cond_Wk', 'L3_cond_Wv', 'L3_cond_Wo', 'L3_cond_q_norm_w', 'L3_cond_k_norm_w', 'L3_cond_k_cache',
        'L3_cond_v_cache']


def kernel(**inputs):
    import numpy as _np
    import concourse.bacc as _bacc
    from concourse import mybir as _mybir
    from concourse.bass_utils import run_bass_kernel_spmd as _run

    nc = _bacc.Bacc("TRN2", target_bir_lowering=False, num_devices=1)
    arrays, args = {}, {}
    given = {name: _np.ascontiguousarray(inputs[name]) for name in _INS}
    given["shape_constants"] = constants()
    for name, x in given.items():
        arrays[f"in_{name}"] = x
        args[name] = nc.dram_tensor(f"in_{name}", x.shape, _mybir.dt.from_np(x.dtype), kind="ExternalInput").ap()
    out = nc.dram_tensor("out_0", (NB, T, D), _mybir.dt.float32, kind="ExternalOutput").ap()
    build(nc, args, out)
    r = _run(nc, [arrays], core_ids=[0])
    return r.results[0]["out_0"]
```

```python
import concourse.bass as bass
from concourse import mybir
from contextlib import ExitStack
import numpy as np

P = 128
NB, T, D = 8, 128, 512
NT = NB * T
C = D // P
HALF = 512
E, R = 8, 16
F = 1376
FC = (F + P - 1) // P
FR = F - (FC - 1) * P
FG = F // R
HQ, HK, DH = 32, 8, 128
REP = HQ // HK
PAGES, PSIZE, NPP = 64, 32, 16
L = NPP * PSIZE
KC = L // P
KEYS = L + T
NGP = HK // 2
UNITS = 2 * NB
EPS = 1e-6
SCALE = 1.0 / float(np.sqrt(DH))
NEG = -1e30
TWO_PI = 2.0 * np.pi
ROUND = 1.5 * 2.0 ** 23
C1 = 6.28125
C2 = float(np.float32(TWO_PI - C1))
C3 = float(TWO_PI - C1 - np.float64(np.float32(TWO_PI - C1)))
K_ID, K_BM, K_IO, K_E, K_FR, K_P, K_END = 0, 128, 136, 648, 656, 720, 721


def constants():
    k = np.zeros((P, K_END), np.float32)
    k[:, K_ID:K_BM] = np.eye(P)
    k[:, K_BM:K_IO] = np.arange(P)[:, None] // R == np.arange(NB)[None]
    k[:, K_IO:K_E] = np.arange(L)[None]
    k[:, K_E:K_FR] = np.arange(E)[None]
    k[:, K_FR:K_P] = (np.float32(1.0) / np.power(np.float32(10000.0), np.arange(0, DH, 2, dtype=np.float32) / np.float32(DH)))[None]
    k[:, K_P] = np.arange(P)
    return k


fp32, fp32r, i32, u32 = mybir.dt.float32, mybir.dt.float32r, mybir.dt.int32, mybir.dt.uint32
ALU = mybir.AluOpType
ACT = mybir.ActivationFunctionType
AX = mybir.AxisListType


def build(nc, a, out):
    with ExitStack() as ctx:
        def sb(name, shape, dt=fp32):
            return ctx.enter_context(nc.sbuf_tensor(name, shape, dt))

        const = sb("const", [P, K_END])
        ints = sb("ints", [P, 2, NB], i32)
        acc = sb("acc", [P, NB, D])
        lens = sb("lens", [P, NB])
        trig = sb("trig", [P, 2, NB, DH // 2])
        rope_w = sb("rope_w", [P, 2, 2, DH])
        x_scratch = nc.dram_tensor("x_scratch", (NB, P, C, T), fp32, kind="Internal").ap()
        banks = ctx.enter_context(nc.psum_tensor("banks", [P, 8, 512], fp32))
        with ExitStack() as early:
            def early_sb(name, shape):
                return early.enter_context(nc.sbuf_tensor(name, shape, fp32))
            xT = early_sb("xT", [P, C, NT])
            with ExitStack() as middle:
                shapes = {"w2T": [C, D], "wgT": [C, F], "wuT": [C, F], "wdT": [FC, D], "agT": [C, P], "auT": [C, P], "adT": [FC, P],
                          "a2T": [C, P], "bgT": [F], "buT": [F], "bdT": [D], "b2R": [D], "bias2": [C]}
                weights = [middle.enter_context(nc.sbuf_tensor(name, [P] + shape, fp32)) for name, shape in shapes.items()]
                layer0(nc, a, const, xT, acc, ints, rope_w, banks, weights)
                layers12(nc, const, xT, acc, banks, weights)
            attention_setup(nc, const, xT, ints, rope_w, trig, banks, acc, lens, x_scratch)
        attention(nc, a, out, const, banks, acc, lens, trig, rope_w, x_scratch)


def layer0(nc, a, const, xT_b, acc, ints, rope_w, banks, weights):
    w2T, wgT, wuT, wdT, agT, auT, adT, a2T, bgT, buT, bdT, b2R, bias2 = weights
    ident = const[:, K_ID:K_BM]

    def bank(n):
        return banks[:, n, :]

    with ExitStack() as ctx:
        def sb(name, shape, dt=fp32):
            return ctx.enter_context(nc.sbuf_tensor(name, shape, dt))

        def sem(name):
            return ctx.enter_context(nc.semaphore(name))

        xT_a = acc[:, :, :].rearrange("p b d -> p (b d)").rearrange("p (c t) -> p c t", c=C)
        RAW = 8
        raw = sb("raw", [P, RAW, C, P])
        w0T = sb("w0T", [P, C, D])
        wrT = sb("wrT", [P, C, E])
        a0T = sb("a0T", [P, C, P])
        b0T = sb("b0T", [P, D])
        rank_act = sb("rank_act", [P, 2, HALF * 2])
        area = sb("area", [P, 2 * D + F + 2 * NB * 256 + D + 64])
        o = 0
        ag_raw = area[:, o:o + D]; o += D
        au_raw = area[:, o:o + D]; o += D
        ad_raw = area[:, o:o + F]; o += F
        bg_raw = area[:, o:o + NB * 256].rearrange("p (b s r) -> p b s r", b=NB, s=R); o += NB * 256
        bu_raw = area[:, o:o + NB * 256].rearrange("p (b s r) -> p b s r", b=NB, s=R); o += NB * 256
        bd_raw = area[:, o:o + D].rearrange("p (b s r) -> p b s r", b=NB, s=4)
        logit = sb("logit", [P, NB, E])
        top = sb("top", [P, NB, E])
        topi = sb("topi", [P, NB, E], u32)
        rt = sb("rt", [P, 6, NB, E])
        gate16 = rank_act[:, 1, :].rearrange("p (t e r) -> p t e r", t=NB, e=E)

        flat_wdT = wdT[:, :, :].rearrange("p f d -> p (f d)")
        b0_sorted = flat_wdT[:, 0:D].rearrange("p (s b r) -> p s b r", b=NB, r=R)
        bd_sorted = flat_wdT[:, D:2 * D].rearrange("p (s b r) -> p s b r", b=NB, r=R)
        bg_sorted = flat_wdT[:, 2 * D:2 * D + NB * 256].rearrange("p (s b r) -> p s b r", b=NB, r=R)
        bu_sorted = flat_wdT[:, 2 * D + NB * 256:2 * D + 2 * NB * 256].rearrange("p (s b r) -> p s b r", b=NB, r=R)
        sorted_rows = {"b0": b0_sorted, "bd": bd_sorted, "bg": bg_sorted, "bu": bu_sorted}

        b0_in_order, b_in_order = sem("b0_in_order"), sem("b_in_order")
        consts_in, small_in = sem("consts_in"), sem("small_in")
        raw_in = [sem(f"raw_in{s}") for s in range(RAW)]
        gath_in, adapters2_in = sem("gath_in"), sem("adapters2_in")
        tr_filled = [sem("tr_filled0"), sem("tr_filled1")]
        tr_evac = [sem("tr_evac0"), sem("tr_evac1")]
        dve_step = sem("dve_step")
        router_in, router_exp, gates_ready = sem("router_in"), sem("router_exp"), sem("gates_ready")
        router_d = sem("router_d")
        gateT_filled, gateT_evac = sem("gateT_filled"), sem("gateT_evac")
        rank_filled, rank_evac = sem("rank_filled"), sem("rank_evac")
        lin_filled, lin_evac = sem("lin_filled"), sem("lin_evac")

        def rows(src, n, m=P):
            return src[n * P:n * P + m, :]

        def blockwise(dst, n, m=P):
            return dst[:, :, n * P:n * P + m]

        groups = []
        for t in range(NB):
            groups.append(("x", t))
        for n in range(C):
            groups.append(("w0", n))
        groups += [("a0", 0), ("wr", 0)]
        END0 = len(groups)
        for n in range(FC):
            groups += [("wg", n), ("wu", n)]
        groups += [("w2", n) for n in range(C)]
        groups.append(("b0", 0))
        GATHERS = len(groups)
        groups += [("ag", 0), ("au", 0)] + [("bg", n) for n in range(4)] + [("bu", n) for n in range(4)]
        groups += [("ad", n) for n in range(3)] + [("bd", 0)]
        for n in range(FC):
            groups.append(("wd", n))
        END1 = len(groups)
        ring = {}
        for g, (kind, n) in enumerate(groups):
            if kind not in ("ag", "au", "bg", "bu", "ad", "bd"):
                ring[g] = len(ring)
        ring_groups = {v: k for k, v in ring.items()}

        def fr(n):
            return P if n < FC - 1 else FR

        def load_of(g):
            kind, n = groups[g]
            s = raw[:, ring[g] % RAW, :, :]
            flat = s.rearrange("p c t -> p (c t)")
            if kind == "x":
                return flat, a["x"][n, :, :]
            if kind == "w0":
                return flat, rows(a["L0_cond_W"], n)
            if kind == "w2":
                return flat, rows(a["L2_cond_W"], n)
            if kind == "a0":
                return flat, a["L0_cond_A"].rearrange("e r d -> (e r) d")
            if kind == "b0":
                return s.rearrange("p c t -> p (c t)").rearrange("p (e k) -> p e k", e=E), \
                    a["L0_cond_B"].rearrange("e (g s) r -> g e (s r)", s=4)
            if kind == "wr":
                return flat[0:E, :], a["L0_cond_Wr"]
            if kind in ("wg", "wu"):
                return flat[0:fr(n), :], rows(a["L1_cond_W_gate" if kind == "wg" else "L1_cond_W_up"], n, fr(n))
            if kind == "wd":
                return s[:, :, 0:fr(n)], a["L1_cond_W_down"].rearrange("(c p) f -> p c f", p=P)[:, :, n * P:n * P + fr(n)]

        def transposes_of(g):
            kind, n = groups[g]
            b = banks[:, g % 2, :]
            if g in ring:
                s = raw[:, ring[g] % RAW, :, :]
            if kind in ("x", "w0", "w2", "a0", "wr", "wg", "wu", "ag", "au"):
                k = {"wr": E, "wg": fr(n), "wu": fr(n)}.get(kind, P)
                dst = {"x": xT_a, "w0": w0T, "w2": w2T, "a0": a0T, "wr": wrT, "wg": wgT, "wu": wuT, "ag": agT, "au": auT}[kind]
                src = {"ag": ag_raw, "au": au_raw}.get(kind)
                if src is None:
                    src = s.rearrange("p c t -> p (c t)")
                v = b.rearrange("p (c t) -> p c t", c=C)
                return [(src[0:k, c * P:(c + 1) * P], k, v[:, c, 0:k]) for c in range(C)], \
                    blockwise(dst, n, k), v[:, :, 0:k]
            if kind == "wd":
                m = fr(n)
                return [(s[:, c, 0:m], P, b[0:m, c * P:(c + 1) * P]) for c in range(C)], wdT[0:m, n, :], b[0:m, :]
            if kind == "ad":
                blocks = list(range(4 * n, min(4 * n + 4, FC)))
                full = [f for f in blocks if fr(f) == P]
                tr = [(ad_raw[:, f * P:f * P + fr(f)], P, b[0:fr(f), (f - 4 * n) * P:(f - 4 * n + 1) * P]) for f in blocks]
                return tr, adT[:, 4 * n:4 * n + len(full), :], b[:, 0:len(full) * P].rearrange("p (c t) -> p c t", t=P)
            if kind in ("b0", "bd"):
                s4 = sorted_rows[kind]
                dst = (bdT if kind == "bd" else b0T)[:, :].rearrange("p (g s) -> p s g", s=4)
                v = b.rearrange("p (s g) -> p s g", s=4)
                return [(s4[:, f, :, :], P, v[:, f, :]) for f in range(4)], dst, v
            if kind in ("bg", "bu"):
                s4 = sorted_rows[kind]
                dst = (bgT if kind == "bg" else buT)[:, :].rearrange("p (g s) -> p s g", s=R)[:, 4 * n:4 * n + 4, :]
                v = b[:, 0:4 * P].rearrange("p (s g) -> p s g", s=4)
                return [(s4[0:FG, 4 * n + f, :, :], FG, v[:, f, 0:FG]) for f in range(4)], dst, v[:, :, 0:FG]

        AD_TAIL = [g for g, (k, n) in enumerate(groups) if k == "ad" and 4 * n + 4 > FC - 1][0]

        GATHERED = 16 * 6 * NB
        block = ctx.enter_context(nc.Block())

        @block.sync
        def _(sp):
            sp.dma_start(const[:, :], a["shape_constants"]).then_inc(consts_in, 16)
            for k, g in sorted(ring_groups.items()):
                if k >= RAW:
                    prev = ring_groups[k - RAW]
                    sp.wait_ge(tr_filled[prev % 2], prev // 2 + 1)
                dst, src = load_of(g)
                sp.dma_start(dst, src).then_inc(raw_in[k % RAW], 16)

        @block.gpsimd
        def _(pool):
            for n, name in enumerate(("itok_B_0_7", "itok_B_207_1644")):
                pool.dma_start(ints[:, n, :], a[name].rearrange("(o b) -> o b", o=1).to_broadcast([P, NB])).then_inc(small_in, 16)
            pool.dma_start(rope_w[:, 0, 0, :], a["L3_cond_q_norm_w"].rearrange("(o b) -> o b", o=1).to_broadcast([P, DH])).then_inc(small_in, 16)
            pool.dma_start(rope_w[:, 0, 1, :], a["L3_cond_k_norm_w"].rearrange("(o b) -> o b", o=1).to_broadcast([P, DH])).then_inc(small_in, 16)
            pool.dma_start(bias2[:, :], a["L2_cond_b"].rearrange("(c p) -> p c", p=P), allow_slow_non_contiguous=True).then_inc(small_in, 16)
            idx = a["itok_B_2_6"].rearrange("(o b) -> o b", o=1)
            for b in range(NB):
                k = pool.value_load(idx[0:1, b:b + 1], min_val=0, max_val=15)
                rb = slice(R * b, R * b + R)

                def row(name):
                    return a[name][0][bass.ds(k, 1)].rearrange("o r d -> (o r) d")
                pool.dma_start(ag_raw[rb, :], row("L1_cond_A_gate")).then_inc(gath_in, 16)
                pool.dma_start(au_raw[rb, :], row("L1_cond_A_up")).then_inc(gath_in, 16)
                pool.dma_start(ad_raw[rb, :], row("L1_cond_A_down")).then_inc(gath_in, 16)
                pool.dma_start(bg_raw[0:FG, b, :, :], row("L1_cond_B_gate").rearrange("(g s) r -> g s r", s=R)).then_inc(gath_in, 16)
                pool.dma_start(bu_raw[0:FG, b, :, :], row("L1_cond_B_up").rearrange("(g s) r -> g s r", s=R)).then_inc(gath_in, 16)
                pool.dma_start(bd_raw[:, b, :, :], row("L1_cond_B_down").rearrange("(g s) r -> g s r", s=4)).then_inc(gath_in, 16)
            idx2 = a["itok_B_0_23"].rearrange("(o b) -> o b", o=1)
            for b in range(NB):
                k = pool.value_load(idx2[0:1, b:b + 1], min_val=0, max_val=31)
                pool.dma_start(a2T[:, :, R * b:R * b + R], a["L2_cond_lora_As"][bass.ds(k, 1)].rearrange("o (c p) r -> p (o c) r", p=P)).then_inc(adapters2_in, 16)
                pool.dma_start(b2R[R * b:R * b + R, :], a["L2_cond_lora_Bs"][bass.ds(k, 1)].rearrange("o r d -> (o r) d")).then_inc(adapters2_in, 16)

        @block.tensor
        def _(pe):
            pe.wait_ge(consts_in, 16)
            done = {"lin": 0}

            def transpose_groups(lo, hi):
                for g in range(lo, hi):
                    if g in ring:
                        pe.wait_ge(raw_in[ring[g] % RAW], 16 * (ring[g] // RAW + 1))
                    elif g == GATHERS:
                        pe.wait_ge(gath_in, GATHERED)
                        pe.wait_ge(b_in_order, 2)
                    if groups[g][0] == "b0":
                        pe.wait_ge(b0_in_order, 1)
                    if g >= 2:
                        pe.wait_ge(tr_evac[g % 2], g // 2)
                    tr, _, _ = transposes_of(g)
                    for src, k, dst in tr:
                        last = pe.transpose(dst, src, ident[0:k, 0:k])
                    last.then_inc(tr_filled[g % 2], 1)

            def all_copied(g):
                pe.wait_ge(tr_evac[0], (g + 1) // 2)
                pe.wait_ge(tr_evac[1], g // 2)

            def linear(wT, blocks, lhs_rank, x_of, rank_of, half):
                for n in range(C):
                    k = done["lin"]
                    if k >= 2:
                        pe.wait_ge(lin_evac, k - 1)
                    dst = bank(6 + k % 2)
                    for c, m in enumerate(blocks):
                        pe.matmul(dst, wT[0:m, c, n * P:(n + 1) * P], x_of(c, m, half), start=(c == 0), stop=False)
                    pe.matmul(dst, lhs_rank[:, n * P:(n + 1) * P], rank_of(half), start=False, stop=True).then_inc(lin_filled, 1)
                    done["lin"] += 1

            transpose_groups(0, END0)
            all_copied(END0)
            for t in range(NB):
                for c in range(C):
                    last = pe.matmul(bank(4)[:, t * E:(t + 1) * E], xT_a[:, c, t * T:(t + 1) * T], wrT[:, c, :], start=(c == 0), stop=(c == C - 1))
            last.then_inc(router_in, 1)
            for half in range(2):
                for c in range(C):
                    last = pe.matmul(bank(2 + half), a0T[:, c, :], xT_a[:, c, half * HALF:(half + 1) * HALF], start=(c == 0), stop=(c == C - 1))
            last.then_inc(rank_filled, 1)
            pe.wait_ge(gates_ready, 1)
            for t in range(NB):
                last = pe.transpose(bank(5 + t // 4)[:, (t % 4) * T:(t % 4 + 1) * T], gate16[:, t, :, :], ident)
            last.then_inc(gateT_filled, 1)
            transpose_groups(END0, END1)
            pe.wait_ge(rank_evac, 1)
            pe.wait_ge(gateT_evac, 1)
            for half in range(2):
                linear(w0T, [P] * C, b0T, lambda c, m, h: xT_a[:, c, h * HALF:(h + 1) * HALF],
                       lambda h: rank_act[:, 0, h * HALF:(h + 1) * HALF], half)
            all_copied(END1)
            pe.wait_ge(adapters2_in, 16 * 2 * NB)

        def copy_out(eng, g):
            _, dst, src = transposes_of(g)
            eng.wait_ge(tr_filled[g % 2], g // 2 + 1)
            f = nc.scalar.copy if g % 2 == 0 else nc.vector.tensor_copy
            if g == AD_TAIL:
                f(dst, src)
                n = FC - 1
                dst, src = adT[0:FR, n, :], banks[0:FR, g % 2, (n % 4) * P:(n % 4 + 1) * P]
            f(dst, src).then_inc(tr_evac[g % 2], 1)

        @block.scalar
        def _(act):
            for g in range(0, END0, 2):
                copy_out(act, g)
            act.wait_ge(router_d, 1)
            nc.scalar.activation(rt[:, 0, :, 1], rt[:, 0, :, 0], ACT.Exp).then_inc(router_exp, 1)
            act.wait_ge(gateT_filled, 1)
            nc.scalar.mul(xT_b[:, 0, 0:HALF], bank(5), 2.0)
            nc.scalar.mul(xT_b[:, 0, HALF:], bank(6), 2.0).then_inc(gateT_evac, 1)
            for g in range(END0 + END0 % 2, END1, 2):
                if g in (GATHERS - 1, GATHERS):
                    act.wait_ge(gath_in, GATHERED)
                    nc.scalar.copy(bg_sorted[0:FG], bg_raw[0:FG].rearrange("p b s r -> p s b r")).then_inc(b_in_order, 1)
                copy_out(act, g)

        @block.vector
        def _(dve):
            steps = [0]

            def link(ins):
                steps[0] += 1
                ins.then_inc(dve_step, 1)
                dve.wait_ge(dve_step, steps[0])

            for g in range(1, END0, 2):
                copy_out(dve, g)
            dve.wait_ge(small_in, 80)
            link(nc.vector.tensor_copy(rt[:, 5, :, 0], ints[:, 0, :]))
            e_index = const[:, K_E:K_FR].rearrange("p (o e) -> p o e", o=1).to_broadcast([P, NB, E])

            def per_tile(col):
                return col.to_broadcast([P, NB, E])
            link(nc.vector.tensor_tensor(rt[:, 1, :, :], e_index, per_tile(rt[:, 5, :, 0:1]), ALU.is_equal))
            dve.wait_ge(router_in, 1)
            link(nc.vector.scalar_tensor_tensor(logit[:, :, :], rt[:, 1, :, :], 5.0,
                                                bank(4)[:, 0:NB * E].rearrange("p (t e) -> p t e", t=NB), ALU.mult, ALU.add))
            for t in range(NB):
                last = nc.vector.max(top[:, t, :], logit[:, t, :])
            link(last)
            for t in range(NB):
                last = nc.vector.max_index(topi[:, t, :], top[:, t, :], logit[:, t, :])
            link(last)
            link(nc.vector.tensor_copy(rt[:, 5, :, 0:2], topi[:, :, 0:2]))
            nc.vector.tensor_tensor(rt[:, 0, :, 0], top[:, :, 1], top[:, :, 0], ALU.subtract).then_inc(router_d, 1)
            dve.wait_ge(router_exp, 1)
            link(nc.vector.tensor_scalar(rt[:, 0, :, 2], rt[:, 0, :, 1], 1.0, None, ALU.add))
            link(nc.vector.reciprocal(rt[:, 0, :, 3], rt[:, 0, :, 2]))
            link(nc.vector.tensor_tensor(rt[:, 0, :, 4], rt[:, 0, :, 1], rt[:, 0, :, 3], ALU.mult))
            for k in range(2):
                link(nc.vector.tensor_tensor(rt[:, 1 + k, :, :], e_index, per_tile(rt[:, 5, :, k:k + 1]), ALU.is_equal))
                link(nc.vector.tensor_tensor(rt[:, 3 + k, :, :], rt[:, 1 + k, :, :], per_tile(rt[:, 0, :, 3 + k:4 + k]), ALU.mult))
            link(nc.vector.tensor_tensor(rt[:, 1, :, :], rt[:, 3, :, :], rt[:, 4, :, :], ALU.add))
            nc.vector.tensor_copy(gate16.rearrange("p t e r -> p (t e) r"),
                                  rt[:, 1, :, :].rearrange("p t (e o) -> p (t e) o", o=1).to_broadcast([P, NB * E, R])).then_inc(gates_ready, 1)
            dve.wait_ge(rank_filled, 1)
            dve.wait_ge(gateT_evac, 1)
            nc.vector.tensor_tensor(rank_act[:, 0, 0:HALF], bank(2), xT_b[:, 0, 0:HALF], ALU.mult)
            nc.vector.tensor_tensor(rank_act[:, 0, HALF:], bank(3), xT_b[:, 0, HALF:], ALU.mult).then_inc(rank_evac, 1)
            for g in range(END0 + 1 - END0 % 2, END1, 2):
                if g in (GATHERS - 1, GATHERS):
                    k = ring[GATHERS - 1]
                    dve.wait_ge(raw_in[k % RAW], 16 * (k // RAW + 1))
                    nc.vector.tensor_copy(b0_sorted, raw[:, k % RAW, :, :].rearrange("p c t -> p (c t)")
                                          .rearrange("p (b s r) -> p s b r", b=NB, s=4)).then_inc(b0_in_order, 1)
                    dve.wait_ge(gath_in, GATHERED)
                    nc.vector.tensor_copy(bd_sorted, bd_raw.rearrange("p b s r -> p s b r"))
                    nc.vector.tensor_copy(bu_sorted[0:FG], bu_raw[0:FG].rearrange("p b s r -> p s b r")).then_inc(b_in_order, 1)
                copy_out(dve, g)

            def block_of(x, k):
                return x[:, k % C, (k // C % 2) * HALF:(k // C % 2 + 1) * HALF]

            def residual(k, dst, src):
                dve.wait_ge(lin_filled, k + 1)
                nc.vector.tensor_tensor(block_of(dst, k), bank(6 + k % 2), block_of(src, k), ALU.add).then_inc(lin_evac, 1)

            for k in range(2 * C):
                residual(k, xT_b, xT_a)


def layers12(nc, const, xT_b, acc, banks, weights):
    w2T, wgT, wuT, wdT, agT, auT, adT, a2T, bgT, buT, bdT, b2R, bias2 = weights
    blockmask = const[:, K_BM:K_IO]
    xT_a = acc[:, :, :].rearrange("p b d -> p (b d)").rearrange("p (c t) -> p c t", c=C)

    def bank(n):
        return banks[:, n, :]

    def rows_of(n):
        return P if n < FC - 1 else FR

    def tokens(half):
        return slice(half * HALF, (half + 1) * HALF)

    with ExitStack() as ctx:
        def sb(name, shape, dt=fp32):
            return ctx.enter_context(nc.sbuf_tensor(name, shape, dt))

        def sem(name):
            return ctx.enter_context(nc.semaphore(name))

        act_T = sb("act_T", [P, FC, HALF])
        rank_act = sb("rank_act1", [P, 2, HALF])
        xs = [sb(f"xs{half}", [P, 2, C, HALF], fp32r) for half in range(2)]
        w_split = [sb(f"w_split{s}", [P, 2, C, P], fp32r) for s in range(2)]

        x_hi, x_ready = sem("x1_hi"), sem("x1_ready")
        w_hi, w_ready, w_used = sem("w1_hi"), sem("w1_ready"), sem("w1_used")
        gu_filled, silu_done, gu_done = sem("gu_filled"), sem("silu_done"), sem("gu_done")
        d_hi, d_ready, d_used = sem("d_hi"), sem("d_ready"), sem("d_used")
        rank_filled, rank_evac = sem("rank1_filled"), sem("rank1_evac")
        lin_filled, lin_evac = sem("lin1_filled"), sem("lin1_evac")

        block = ctx.enter_context(nc.Block())

        @block.tensor
        def _(pe):
            n_rank = 0

            def product(dst, w, x, start):
                pe.matmul(dst, w[0], x[0], start=start, stop=False)
                pe.matmul(dst, w[0], x[1], start=False, stop=False)
                return pe.matmul(dst, w[1], x[0], start=False, stop=False)

            def rank_products(stacks, x, half):
                for n, w in enumerate(stacks):
                    for c in range(C):
                        last = pe.matmul(bank(2 + n), w[:, c, :], x[:, c, tokens(half)], start=(c == 0), stop=(c == C - 1))
                last.then_inc(rank_filled, 1)

            for half in range(2):
                rank_products([agT, auT], xT_b, half)
                n_rank += 1
                pe.wait_ge(rank_evac, n_rank)
                pe.wait_ge(x_ready, half + 1)
                for n in range(FC):
                    m, step = rows_of(n), half * FC + n
                    if n >= 2:
                        pe.wait_ge(gu_done, step - 1)
                    elif half:
                        pe.wait_ge(lin_evac, C)
                    for k, bT in enumerate((bgT, buT)):
                        dst = bank(2 + 2 * (n % 2) + k)[0:m, :]
                        pe.wait_ge(w_ready, 2 * step + k + 1)
                        for c in range(C):
                            last = product(dst, (w_split[k][:, 0, c, 0:m], w_split[k][:, 1, c, 0:m]),
                                           (xs[half][:, 0, c, :], xs[half][:, 1, c, :]), c == 0)
                        last.then_inc(w_used, 1)
                        last = pe.matmul(dst, bT[:, n * P:n * P + m], rank_act[:, k, :], start=False, stop=True)
                    last.then_inc(gu_filled, 1)
                pe.wait_ge(gu_done, (half + 1) * FC)
                for n in range(FC):
                    m, step, slot = rows_of(n), half * FC + n, 2 * (n % 2)
                    last = pe.matmul(bank(2), adT[0:m, n, :], act_T[0:m, n, :], start=(n == 0), stop=(n == FC - 1))
                    if n == FC - 1:
                        last.then_inc(rank_filled, 1)
                    pe.wait_ge(d_ready, step + 1)
                    for o in range(C):
                        last = product(bank(4 + o), [xs[half][0:m, h, slot + 1, o * P:(o + 1) * P] for h in range(2)],
                                       [xs[half][0:m, h, slot, :] for h in range(2)], n == 0)
                    last.then_inc(d_used, 1)
                n_rank += 1
                pe.wait_ge(rank_evac, n_rank)
                for o in range(C):
                    pe.matmul(bank(4 + o), bdT[:, o * P:(o + 1) * P], rank_act[:, 0, :], start=False, stop=True).then_inc(lin_filled, 1)
            pe.wait_ge(lin_evac, 2 * C)
            for half in range(2):
                rank_products([a2T], xT_a, half)
                n_rank += 1
                pe.wait_ge(rank_evac, n_rank)
                for o in range(C):
                    if half:
                        pe.wait_ge(lin_evac, 2 * C + o + 1)
                    for c in range(C):
                        pe.matmul(bank(4 + o), w2T[:, c, o * P:(o + 1) * P], xT_a[:, c, tokens(half)], start=(c == 0), stop=False)
                    pe.matmul(bank(4 + o), b2R[:, o * P:(o + 1) * P], rank_act[:, 0, :], start=False, stop=True).then_inc(lin_filled, 1)

        def weight_blocks():
            return [(n, k, rows_of(n), w[:, :, n * P:n * P + rows_of(n)]) for n in range(FC) for k, w in enumerate((wgT, wuT))]

        @block.scalar
        def _(act):
            def split_weights(half, i):
                n, k, m, w = weight_blocks()[i]
                done = half * 2 * FC + i
                if done >= 2:
                    act.wait_ge(w_used, done - 1)
                nc.scalar.copy(w_split[k][:, 0, :, 0:m], w).then_inc(w_hi, 1)

            for half in range(2):
                nc.scalar.copy(xs[half][:, 0, :, :], xT_b[:, :, tokens(half)]).then_inc(x_hi, 1)
                split_weights(half, 0)
                split_weights(half, 1)
                for n in range(FC):
                    m, step = rows_of(n), half * FC + n
                    if n + 1 < FC:
                        split_weights(half, 2 * n + 2)
                        split_weights(half, 2 * n + 3)
                    act.wait_ge(gu_filled, step + 1)
                    if half and n == 0:
                        act.wait_ge(d_used, FC)
                    nc.scalar.activation(act_T[0:m, n, :], bank(2 + 2 * (n % 2))[0:m, :], ACT.Silu).then_inc(silu_done, 1)
                for n in range(FC):
                    m, step, slot = rows_of(n), half * FC + n, 2 * (n % 2)
                    act.wait_ge(gu_done, half * FC + n + 1)
                    if n < 2:
                        act.wait_ge(gu_filled, (half + 1) * FC)
                    else:
                        act.wait_ge(d_used, step - 1)
                    nc.scalar.copy(xs[half][0:m, 0, slot, :], act_T[0:m, n, :])
                    nc.scalar.copy(xs[half][0:m, 0, slot + 1, :], wdT[0:m, n, :]).then_inc(d_hi, 1)

        @block.vector
        def _(dve):
            def own_rows(srcs, half, scale, n_rank):
                dve.wait_ge(rank_filled, n_rank)
                for k, src in enumerate(srcs):
                    for b in range(HALF // T):
                        row = half * (HALF // T) + b
                        last = nc.vector.tensor_scalar(rank_act[:, k, b * T:(b + 1) * T], src[:, b * T:(b + 1) * T],
                                                       blockmask[:, row:row + 1], scale, ALU.mult, ALU.mult)
                last.then_inc(rank_evac, 1)

            def low(hi_and_lo, src):
                return nc.vector.tensor_tensor(hi_and_lo[1], src, hi_and_lo[0].bitcast(fp32), ALU.subtract)

            def split_weights(half, i):
                n, k, m, w = weight_blocks()[i]
                dve.wait_ge(w_hi, half * 2 * FC + i + 1)
                low([w_split[k][:, h, :, 0:m] for h in range(2)], w).then_inc(w_ready, 1)

            n_rank = 0
            for half in range(2):
                dve.wait_ge(x_hi, half + 1)
                low([xs[half][:, h, :, :] for h in range(2)], xT_b[:, :, tokens(half)]).then_inc(x_ready, 1)
                split_weights(half, 0)
                split_weights(half, 1)
                n_rank += 1
                own_rows([bank(2), bank(3)], half, 0.5, n_rank)
                for n in range(FC):
                    m, step = rows_of(n), half * FC + n
                    if n + 1 < FC:
                        split_weights(half, 2 * n + 2)
                        split_weights(half, 2 * n + 3)
                    dve.wait_ge(silu_done, step + 1)
                    nc.vector.tensor_tensor(act_T[0:m, n, :], act_T[0:m, n, :], bank(3 + 2 * (n % 2))[0:m, :], ALU.mult).then_inc(gu_done, 1)
                for n in range(FC):
                    m, slot = rows_of(n), 2 * (n % 2)
                    dve.wait_ge(d_hi, half * FC + n + 1)
                    low([xs[half][0:m, h, slot, :] for h in range(2)], act_T[0:m, n, :])
                    low([xs[half][0:m, h, slot + 1, :] for h in range(2)], wdT[0:m, n, :]).then_inc(d_ready, 1)
                n_rank += 1
                own_rows([bank(2)], half, 0.5, n_rank)
                for o in range(C):
                    dve.wait_ge(lin_filled, half * C + o + 1)
                    nc.vector.tensor_tensor(xT_a[:, o, tokens(half)], bank(4 + o), xT_b[:, o, tokens(half)], ALU.add).then_inc(lin_evac, 1)
            for half in range(2):
                n_rank += 1
                own_rows([bank(2)], half, 2.0, n_rank)
                for o in range(C):
                    dve.wait_ge(lin_filled, (2 + half) * C + o + 1)
                    nc.vector.scalar_tensor_tensor(xT_b[:, o, tokens(half)], bank(4 + o), bias2[:, o:o + 1], xT_a[:, o, tokens(half)],
                                                   ALU.add, ALU.add).then_inc(lin_evac, 1)


def place_of_weights(n, wqT, wkvT, woT):
    if n < 8:
        return wqT[:, :, :, n * P:(n + 1) * P]
    if n < 12:
        j, k = (n - 8) % 2, (n - 8) // 2
        return wkvT[:, :, :, j, k * DH:(k + 1) * DH]
    return woT[:, :, (n % 2) * REP:(n % 2 + 1) * REP, (n - 12) // 2 * P:((n - 12) // 2 + 1) * P]


def attention_setup(nc, const, xT, ints, rope_w, trig, banks, acc, lens, x_scratch):
    ident = const[:, K_ID:K_BM]

    def bank(n):
        return banks[:, n, :]

    with ExitStack() as ctx:
        def sb(name, shape, dt=fp32):
            return ctx.enter_context(nc.sbuf_tensor(name, shape, dt))

        def sem(name):
            return ctx.enter_context(nc.semaphore(name))

        angle = sb("angle", [P, NB, DH // 2])
        turns = sb("turns", [P, NB, DH // 2])
        pos = sb("pos", [P, NB])
        reduced = sem("reduced")
        x_filled, x_evac = sem("x_filled"), sem("x_evac")
        step = sem("step")
        stored = sem("stored")

        block = ctx.enter_context(nc.Block())

        @block.sync
        def _(sp):
            for b in range(NB):
                sp.dma_start(x_scratch[b], xT[:, :, b * T:(b + 1) * T]).then_inc(stored, 16)
            sp.wait_ge(stored, 16 * NB)

        @block.tensor
        def _(pe):
            for t in range(NB):
                for c in range(C):
                    last = pe.transpose(bank(t)[:, c * P:(c + 1) * P], xT[:, c, t * T:(t + 1) * T], ident)
                last.then_inc(x_filled, 1)

        @block.scalar
        def _(act):
            for t in range(NB):
                act.wait_ge(x_filled, t + 1)
                nc.scalar.copy(acc[:, t, :], bank(t)).then_inc(x_evac, 1)
            for k in range(2):
                act.wait_ge(reduced, k + 1)
                nc.scalar.activation(trig[:, k, :, :], trig[:, k, :, :], ACT.Sin)

        @block.gpsimd
        def _(pool):
            h = DH // 2
            pool.tensor_scalar(rope_w[:, 1, :, 0:h], rope_w[:, 0, :, h:DH], -1.0, None, ALU.mult)
            pool.tensor_copy(rope_w[:, 1, :, h:DH], rope_w[:, 0, :, 0:h])

        @block.vector
        def _(dve):
            n = [0]

            def link(ins):
                n[0] += 1
                ins.then_inc(step, 1)
                dve.wait_ge(step, n[0])
            link(nc.vector.tensor_copy(lens[:, :], ints[:, 1, :]))
            link(nc.vector.tensor_scalar(pos[:, :], lens[:, :], const[:, K_P:K_P + 1], None, ALU.add))
            link(nc.vector.tensor_tensor(angle[:, :, :], pos[:, :].rearrange("p (b o) -> p b o", o=1).to_broadcast([P, NB, DH // 2]),
                                         const[:, K_FR:K_P].rearrange("p (o i) -> p o i", o=1).to_broadcast([P, NB, DH // 2]), ALU.mult))
            for k, shift in ((0, 0.0), (1, 0.25)):
                r = trig[:, k, :, :]
                link(nc.vector.tensor_scalar(turns[:, :, :], angle[:, :, :], 1.0 / TWO_PI, shift, ALU.mult, ALU.add))
                link(nc.vector.tensor_scalar(turns[:, :, :], turns[:, :, :], ROUND, None, ALU.add))
                link(nc.vector.tensor_scalar(turns[:, :, :], turns[:, :, :], -ROUND, None, ALU.add))
                link(nc.vector.scalar_tensor_tensor(r, turns[:, :, :], -C1, angle[:, :, :], ALU.mult, ALU.add))
                link(nc.vector.scalar_tensor_tensor(r, turns[:, :, :], -C2, r, ALU.mult, ALU.add))
                link(nc.vector.scalar_tensor_tensor(r, turns[:, :, :], -C3, r, ALU.mult, ALU.add))
                link(nc.vector.tensor_scalar(r, r, TWO_PI * shift, None, ALU.add))
                nc.vector.tensor_scalar(r, r, 3.1415925, -3.1415925, ALU.min, ALU.max).then_inc(reduced, 1)


def attention(nc, a, out, const, banks, acc, lens, trig, rope_w, x_scratch):
    ident = const[:, K_ID:K_BM]
    key_index = const[:, K_IO:K_E]

    def bank(n):
        return banks[:, n, :]

    QP, OUT, SNEW = bank(0), bank(2), bank(5)
    flat01 = banks[:, 0:2, :].rearrange("p n c -> p (n c)")
    QK5 = flat01[:, 0:5 * DH].rearrange("p (h d) -> p h d", h=5)
    KV = bank(1)[:, 0:2 * DH]
    VN = bank(1)[:, DH:2 * DH]
    KTN = bank(1)[:, 2 * DH:2 * DH + T]
    KTC, QT = bank(3), bank(4)
    PT = (bank(6), bank(7))

    with ExitStack() as ctx:
        def sb(name, shape, dt=fp32):
            return ctx.enter_context(nc.sbuf_tensor(name, shape, dt))

        RING = 5
        GROUPS, QKV_GROUPS = 20, 12
        OUT_GROUPS = range(QKV_GROUPS, GROUPS)
        pages = sb("pages", [1, NB * NPP], i32)
        w_raw = sb("w_raw", [P, RING, D])
        wqT = sb("wqT", [P, 2, C, 2 * REP * DH], fp32r)
        wkvT = sb("wkvT", [P, 2, C, 2, 2 * DH], fp32r)
        woT = sb("woT", [P, 2, 2 * REP, D], fp32r)
        x_raw = sb("x_raw", [P, C, T])
        xb = sb("xb", [P, 2, C, T], fp32r)
        tab = sb("tab", [P, 4, DH])
        len_b = sb("len_b", [P, 1])
        k_raw = sb("k_raw", [P, KC, 2, DH])
        v_raw = sb("v_raw", [P, KC, 2, DH])
        mask = sb("mask", [P, L])
        unused = sb("unused", [P, REP])
        ss = sb("ss", [P, 3, 5])
        half_power = sb("half_power", [P, 5])
        qn = sb("qn", [P, 5, DH])
        qr = sb("qr", [P, 5, DH])
        rope_b = sb("rope_b", [P, 5, DH])
        sq = rope_b
        qT = [sb(f"qT{s}", [P, 2, REP, T], fp32r) for s in range(2)]
        kT = [sb(f"kT{s}", [P, 2, KEYS], fp32r) for s in range(2)]
        v_new = [sb(f"v_new{s}", [P, DH]) for s in range(2)]
        v = [sb(f"v{s}", [P, 2, KC + 1, DH], fp32r) for s in range(2)]
        probs = [sb(f"probs{s}", [P, REP, KEYS]) for s in range(2)]
        stat = sb("stat", [P, 3, REP])
        sums = sb("sums", [P, 4, REP])
        pT = [sb(f"pT{s}", [P, 2, REP * T], fp32r) for s in range(2)]
        oT = sb("oT", [P, 2, REP * T], fp32r)

        count = {}

        def sem(name, n=0):
            s = ctx.enter_context(nc.semaphore(name))
            if n:
                count[s.name] = n
            return s

        pages_in, w_in = sem("pages_in"), [sem(f"w_in{n}") for n in range(RING)]
        wt_filled, wt_hi, wt_lo = sem("wt_filled"), sem("wt_hi"), sem("wt_lo")
        x_in, len_in, k_in, v_in = sem("x_in"), sem("len_in"), sem("k_in"), sem("v_in")
        x_hi, x_ready = sem("x_hi"), sem("x_ready")
        tab_ready, mask_ready = sem("tab_ready"), sem("mask_ready")
        power_set = sem("power_set")
        out_stored = sem("out_stored")
        proj_filled = sem("proj_filled", 1)
        squared = sem("squared", 1)
        summed, ms_ready = sem("summed", 1), sem("ms_ready", 1)
        inv_rms = sem("inv_rms", 1)
        qn_ready = sem("qn_ready", 1)
        crossed = sem("crossed", 1)
        rotated = sem("rotated", 1)
        v_hi, v_ready = sem("v_hi", 1), sem("v_ready", 1)
        ktc_filled, ktc_hi, ktc_evac = sem("ktc_filled", 1), sem("ktc_hi", 1), sem("ktc_evac", 1)
        qt_filled, qt_hi, qt_evac = sem("qt_filled", 1), sem("qt_hi", 1), sem("qt_evac", 1)
        snew_filled = sem("snew_filled", 1)
        s_filled = sem("s_filled", REP)
        newmax = sem("newmax", 2)
        masked = sem("masked", REP)
        exp_done = sem("exp_done", REP)
        total, inverse = sem("total", 1), sem("inverse", 1)
        scaled = sem("scaled", REP)
        pt_filled = sem("pt_filled", KC + 1)
        p_hi_evac, p_lo_evac = sem("p_hi_evac", KC + 1), sem("p_lo_evac", KC + 1)
        pv_done = sem("pv_done", KC + 1)
        o_hi, o_ready = sem("o_hi", 1), sem("o_ready", 1)
        out_filled, out_evac = sem("out_filled", 1), sem("out_evac", 1)

        def wait(eng, s, u, n=None):
            k = count[s.name]
            eng.wait_ge(s, (u + 2) * k + (k if n is None else n))

        def before_first(eng, sems):
            for s in sems:
                eng.sem_inc(s, 2 * count[s.name])

        def wait_row(eng, s, u):
            eng.wait_ge(s, (u + 4) // 2)

        def next_of(b):
            return 0 if isinstance(b, int) and b == NB - 1 else b + 1

        def row_count(u, n):
            return (u + 2) * (n // 2)

        def loops(eng, start, front, unit, tail):
            def pair(g, nxt):
                u0 = g * UNITS
                front(u0, 0, g, nxt)
                unit(u0, 0, 0, False, False, True, True, None)
                unit(u0 + 1, 1, 0, True, False, True, True, None)
                with eng.Fori(0, NB - 2) as row:
                    b = row + 1
                    u = u0 + 2 * b
                    unit(u, 0, b, True, True, True, True, None)
                    unit(u + 1, 1, b, True, True, True, True, None)
                u = u0 + 2 * (NB - 1)
                unit(u, 0, NB - 1, True, True, True, nxt is not None, None)
                unit(u + 1, 1, NB - 1, True, True, False, nxt is not None, nxt)
                tail(u + 1, 1, NB - 1, nxt)

            start()
            with eng.Fori(0, NGP - 1) as g:
                pair(g, g + 1)
            pair(NGP - 1, None)

        def pt_slot_free(eng, u, c):
            if c < 2:
                wait(eng, pv_done, u - 1)
            else:
                wait(eng, pv_done, u, c - 1)

        def weight_bank(n):
            return bank(n % 2 if n < QKV_GROUPS else 6 + n % 2)

        def flat(x):
            return x.rearrange("p h t -> p (h t)")

        block = ctx.enter_context(nc.Block())

        @block.sync
        def _(sp):
            sp.dma_start(pages[:, :], a["itok_Bx16_0_63"].rearrange("(o b) n -> o (b n)", o=1)).then_inc(pages_in, 16)
            sp.wait_ge(pages_in, 16)
            cache = {"k": a["L3_cond_k_cache"], "v": a["L3_cond_v_cache"]}

            def gather(dst, kind, g, page, s):
                for n in range(NPP):
                    sp.dma_start(dst[PSIZE * (n % 4):PSIZE * (n % 4 + 1), n // 4, :, :],
                                 cache[kind][bass.ds(page[n], 1), :, bass.ds(2 * g, 2), :].rearrange("o s h d -> (o s) h d")).then_inc(s, 16)

            def load_front(g, b):
                u = g * UNITS + 2 * b
                page = [sp.value_load(pages[0:1, bass.ds(b * NPP + n, 1)], min_val=0, max_val=PAGES - 1) for n in range(NPP)]
                wait(sp, ktc_filled, u - 1)
                gather(k_raw, "k", g, page, k_in)
                wait_row(sp, mask_ready, u - 2)
                sp.dma_start(len_b[:, :], lens[:, bass.ds(b, 1)]).then_inc(len_in, 16)
                return page

            def load_values(g, b, page):
                wait(sp, v_ready, g * UNITS + 2 * b - 1)
                gather(v_raw, "v", g, page, v_in)

            with sp.Fori(0, NGP) as g:
                with sp.Fori(0, NB) as b:
                    load_values(g, b, load_front(g, b))
            wait(sp, out_evac, NGP * UNITS - 1)
            sp.dma_start(out.rearrange("b t d -> t b d"), acc[:, :, :]).then_inc(out_stored, 16)
            sp.wait_ge(out_stored, 16)

        @block.tensor
        def _(pe):
            before_first(pe, [proj_filled, ktc_filled, qt_filled, snew_filled, s_filled, pt_filled, pv_done, out_filled])
            pe.sem_inc(wt_filled, RING)

            def product(dst, w, x, start, stop):
                pe.matmul(dst, w[0], x[0], start=start, stop=False)
                pe.matmul(dst, w[0], x[1], start=False, stop=False)
                return pe.matmul(dst, w[1], x[0], start=False, stop=stop)

            def halves(x, *at):
                return x[(slice(None), 0) + at], x[(slice(None), 1) + at]

            def prepare(g, groups):
                for n in groups:
                    pe.wait_ge(w_in[n % RING], (g * (GROUPS // RING) + n // RING + 1) * 16)
                    if n == 0:
                        wait(pe, qt_evac, g * UNITS - 1)
                    if n >= 2 and n not in (QKV_GROUPS, QKV_GROUPS + 1):
                        pe.wait_ge(wt_lo, g * GROUPS + n - 1)
                    for c in range(C):
                        last = pe.transpose(weight_bank(n)[:, c * P:(c + 1) * P], w_raw[:, n % RING, c * P:(c + 1) * P], ident)
                    last.then_inc(wt_filled, 1)

            def project_q(u, j):
                if j == 0:
                    wait_row(pe, x_ready, u)
                wait(pe, qn_ready, u - 1)
                for c in range(C):
                    product(QP, halves(xb, c), halves(wqT, c, slice(j * REP * DH, (j + 1) * REP * DH)), c == 0, c == C - 1)

            def project_kv(u, j):
                wait(pe, qt_evac, u - 1)
                for c in range(C):
                    last = product(KV, halves(xb, c), halves(wkvT, c, j), c == 0, c == C - 1)
                last.then_inc(proj_filled, 1)

            def cached_keys(u, j):
                if j == 0:
                    pe.wait_ge(k_in, row_count(u, 16 * NPP))
                wait(pe, masked, u - 1, 3)
                for c in range(KC):
                    last = pe.transpose(KTC[:, c * P:(c + 1) * P], k_raw[:, c, j, :], ident)
                last.then_inc(ktc_filled, 1)

            def queries(u):
                wait(pe, rotated, u)
                wait(pe, masked, u - 1, 4)
                for h in range(REP):
                    pe.transpose(QT[:, h * T:(h + 1) * T], qr[:, h, :], ident)
                pe.transpose(KTN, qr[:, REP, :], ident).then_inc(qt_filled, 1)

            def new_scores(u, s):
                wait(pe, qt_evac, u)
                wait(pe, exp_done, u - 1)
                for h in range(REP):
                    last = product(SNEW[:, h * T:(h + 1) * T], halves(qT[s], h), halves(kT[s], slice(L, KEYS)), True, True)
                last.then_inc(snew_filled, 1)

            def scores(u, s, h):
                wait(pe, ktc_evac, u)
                if h >= 2:
                    wait(pe, masked, u, h - 1)
                product(bank(3 + h % 2), halves(qT[s], h), halves(kT[s], slice(0, L)), True, True).then_inc(s_filled, 1)

            def turn_probs(u, j, c):
                if c == 0:
                    wait(pe, scaled, u)
                if c >= 2:
                    wait(pe, p_lo_evac, u, c - 1)
                for h in range(REP):
                    last = pe.transpose(PT[c % 2][:, h * T:(h + 1) * T], probs[j][:, h, c * P:(c + 1) * P], ident)
                last.then_inc(pt_filled, 1)

            def values(u, j, c):
                if c == 0:
                    wait(pe, v_ready, u)
                    wait(pe, out_evac, u - 1)
                wait(pe, p_lo_evac, u, c + 1)
                product(OUT, halves(v[j], c), halves(pT[c % 2]), c == 0, c == KC).then_inc(pv_done, 1)

            def project_out(u, j):
                wait(pe, o_ready, u)
                for h in range(REP):
                    last = product(OUT, halves(oT, slice(h * T, (h + 1) * T)), halves(woT, j * REP + h), h == 0, h == REP - 1)
                last.then_inc(out_filled, 1)

            def front(u, j, g, nxt):
                prepare(g, OUT_GROUPS[0:2])
                pe.wait_ge(wt_lo, g * GROUPS + QKV_GROUPS)
                project_q(u, j)
                project_kv(u, j)
                cached_keys(u, j)
                prepare(g, OUT_GROUPS[2:])
                queries(u)

            def tail(u, j, b, nxt):
                values(u - 1, 1 - j, KC)
                turn_probs(u, j, 0)
                if nxt is not None:
                    prepare(nxt, [6])
                project_out(u - 1, 1 - j)
                for c in range(1, KC + 1):
                    turn_probs(u, j, c)
                    if nxt is not None:
                        prepare(nxt, [6 + c])
                    values(u, j, c - 1)
                values(u, j, KC)
                if nxt is not None:
                    prepare(nxt, [11])
                project_out(u, j)

            def unit(u, j, b, attend_last, finish_last, follow, next_row, nxt):
                if follow:
                    project_q(u + 1, 1 - j)
                if nxt is not None:
                    prepare(nxt, [0, 1, 2])
                if finish_last:
                    values(u - 2, j, KC)
                if follow:
                    project_kv(u + 1, 1 - j)
                if nxt is not None:
                    prepare(nxt, [3])
                if attend_last and not finish_last:
                    pe.wait_ge(wt_lo, (u + 1) // UNITS * GROUPS + GROUPS)
                if attend_last:
                    turn_probs(u - 1, 1 - j, 0)
                new_scores(u, j)
                scores(u, j, 0)
                scores(u, j, 1)
                if finish_last:
                    project_out(u - 2, j)
                for c in range(1, KC + 1):
                    if attend_last:
                        turn_probs(u - 1, 1 - j, c)
                    if c < 3:
                        scores(u, j, 1 + c)
                    if attend_last:
                        values(u - 1, 1 - j, c - 1)
                    if c == 2 and follow:
                        cached_keys(u + 1, 1 - j)
                    if c == 3 and follow:
                        queries(u + 1)
                    if c in (2, 3) and nxt is not None:
                        prepare(nxt, [2 + c])

            def start():
                prepare(0, range(QKV_GROUPS))

            loops(pe, start, front, unit, tail)

        @block.scalar
        def _(act):
            act.sem_inc(x_hi, 1)
            before_first(act, [squared, v_hi, ktc_hi, qt_hi, exp_done, p_hi_evac, o_hi])

            wq = a["L3_cond_Wq"].rearrange("(g n p) d -> g n p d", g=NGP, p=P)
            wk = a["L3_cond_Wk"].rearrange("(g n p) d -> g n p d", g=NGP, p=P)
            wv = a["L3_cond_Wv"].rearrange("(g n p) d -> g n p d", g=NGP, p=P)
            wo = a["L3_cond_Wo"].rearrange("(o p) (g j k) -> g o j p k", p=P, g=NGP, j=2)

            def load_weights(g, n):
                if n < 8:
                    src = wq[bass.ds(g, 1), n]
                elif n < QKV_GROUPS:
                    src = (wk if n < 10 else wv)[bass.ds(g, 1), n % 2]
                else:
                    src = wo[bass.ds(g, 1), (n - QKV_GROUPS) // 2, n % 2]
                act.dma_start(w_raw[:, n % RING, :], src.rearrange("o p d -> (o p) d")).then_inc(w_in[n % RING], 16)

            def prepare(g, groups, nxt=None):
                for n in groups:
                    act.wait_ge(wt_filled, g * GROUPS + n + 1 + RING)
                    nc.scalar.copy(place_of_weights(n, wqT, wkvT, woT)[:, 0], weight_bank(n).rearrange("p (c t) -> p c t", c=C)).then_inc(wt_hi, 1)
                    if n + RING < GROUPS:
                        load_weights(g, n + RING)
                    elif nxt is not None:
                        load_weights(nxt, n + RING - GROUPS)

            def load_x(b):
                act.dma_start(x_raw[:, :, :], x_scratch[bass.ds(b, 1)].rearrange("o p c t -> (o p) c t")).then_inc(x_in, 16)

            def split_x(u):
                act.wait_ge(x_in, row_count(u, 16))
                wait(act, proj_filled, u - 1)
                nc.scalar.copy(xb[:, 0, :, :], x_raw[:, :, :]).then_inc(x_hi, 1)

            def start():
                for n in range(RING):
                    load_weights(0, n)
                load_x(0)
                split_x(0)
                prepare(0, range(QKV_GROUPS))

            def squares(u, j):
                wait(act, proj_filled, u)
                wait(act, v_ready, u - 2)
                nc.scalar.copy(v_new[j][:, :], VN)
                wait(act, rotated, u - 1)
                nc.scalar.activation(sq[:, :, :], QK5, ACT.Square).then_inc(squared, 1)

            def cached_keys(u, j):
                wait(act, ktc_filled, u)
                wait(act, s_filled, u - 2)
                nc.scalar.copy(kT[j][:, 0, 0:L], KTC).then_inc(ktc_hi, 1)

            def queries(u, j):
                wait(act, qt_filled, u)
                nc.scalar.copy(kT[j][:, 0, L:KEYS], KTN)
                nc.scalar.copy(flat(qT[j][:, 0, :, :]), QT).then_inc(qt_hi, 1)

            def split_values(u, j):
                if j == 0:
                    act.wait_ge(v_in, row_count(u, 16 * NPP))
                wait(act, pv_done, u - 2)
                wait(act, v_ready, u - 2)
                nc.scalar.copy(v[j][:, 0, 0:KC, :], v_raw[:, :, j, :])
                nc.scalar.copy(v[j][:, 0, KC, :], v_new[j][:, :]).then_inc(v_hi, 1)

            def exps(u, h, s):
                wait(act, masked, u, h + 1)
                nc.scalar.activation(probs[s][:, h, 0:L], probs[s][:, h, 0:L], ACT.Exp, bias=stat[:, 2, h:h + 1], scale=-1.0,
                                     accum_out=sums[:, 0, h:h + 1])
                nc.scalar.activation(probs[s][:, h, L:KEYS], SNEW[:, h * T:(h + 1) * T], ACT.Exp, bias=stat[:, 2, h:h + 1], scale=SCALE,
                                     accum_out=sums[:, 1, h:h + 1]).then_inc(exp_done, 1)

            def probs_out(u, c):
                wait(act, pt_filled, u, c + 1)
                pt_slot_free(act, u, c)
                nc.scalar.copy(pT[c % 2][:, 0, :], PT[c % 2]).then_inc(p_hi_evac, 1)

            def output(u):
                wait(act, pv_done, u)
                wait(act, out_filled, u - 1)
                nc.scalar.copy(oT[:, 0, :], OUT).then_inc(o_hi, 1)

            def front(u, j, g, nxt):
                prepare(g, OUT_GROUPS[0:2], nxt)
                squares(u, j)
                cached_keys(u, j)
                prepare(g, OUT_GROUPS[2:], nxt)
                queries(u, j)

            def tail(u, j, b, nxt):
                output(u - 1)
                for c in range(KC + 1):
                    probs_out(u, c)
                    if nxt is not None:
                        prepare(nxt, [6 + c])
                output(u)
                if nxt is not None:
                    prepare(nxt, [11])

            def unit(u, j, b, attend_last, finish_last, follow, next_row, nxt):
                if j == 0 and next_row:
                    load_x(next_of(b))
                if nxt is not None:
                    prepare(nxt, [0, 1, 2])
                if finish_last:
                    output(u - 2)
                if nxt is not None:
                    prepare(nxt, [3])
                if follow:
                    squares(u + 1, 1 - j)
                if attend_last:
                    probs_out(u - 1, 0)
                exps(u, 0, j)
                for c in range(1, KC + 1):
                    if attend_last:
                        probs_out(u - 1, c)
                    if c == 3 and j == 0 and next_row:
                        split_x(u + 2)
                    if c < REP:
                        exps(u, c, j)
                    if c == 2 and follow:
                        cached_keys(u + 1, 1 - j)
                    if c == 3 and follow:
                        queries(u + 1, 1 - j)
                    if c in (2, 3) and nxt is not None:
                        prepare(nxt, [2 + c])
                split_values(u, j)

            loops(act, start, front, unit, tail)

        @block.gpsimd
        def _(pool):
            pool.sem_inc(tab_ready, 1)
            before_first(pool, [inv_rms, crossed, rotated, v_ready])
            pool.memset(half_power[:, :], -0.5).then_inc(power_set, 1)
            pool.wait_ge(power_set, 1)

            def table(u, b):
                wait(pool, crossed, u - 1)
                for k, of in ((0, 1), (1, 0)):
                    part = trig[:, of, bass.ds(b, 1), :].to_broadcast([P, 4, DH // 2])
                    last = nc.gpsimd.tensor_tensor(tab[:, 2 * k:2 * k + 2, :].rearrange("p k (s i) -> p (k s) i", s=2), part,
                                                   rope_w[:, k, :, :].rearrange("p k (s i) -> p (k s) i", s=2), ALU.mult)
                last.then_inc(tab_ready, 1)

            def front(u, j, g=None, nxt=None):
                if j == 0:
                    wait_row(pool, tab_ready, u)
                wait(pool, ms_ready, u)
                wait(pool, qn_ready, u - 1)
                nc.gpsimd.tensor_tensor(ss[:, 2, :], ss[:, 1, :], half_power[:, :], ALU.pow).then_inc(inv_rms, 1)
                wait(pool, qn_ready, u)
                wait(pool, qt_filled, u - 1)
                h = DH // 2
                nc.gpsimd.tensor_tensor(qr[:, 0:REP, :], qn[:, 0:REP, :], tab[:, 0:1, :].to_broadcast([P, REP, DH]), ALU.mult)
                nc.gpsimd.tensor_tensor(qr[:, REP, :], qn[:, REP, :], tab[:, 1, :], ALU.mult)
                for lo, of in ((0, h), (h, 0)):
                    nc.gpsimd.tensor_tensor(rope_b[:, 0:REP, lo:lo + h], qn[:, 0:REP, of:of + h], tab[:, 2:3, lo:lo + h].to_broadcast([P, REP, h]), ALU.mult)
                    last = nc.gpsimd.tensor_tensor(rope_b[:, REP, lo:lo + h], qn[:, REP, of:of + h], tab[:, 3, lo:lo + h], ALU.mult)
                last.then_inc(crossed, 1)
                wait(pool, crossed, u)
                nc.gpsimd.tensor_tensor(qr[:, :, :], qr[:, :, :], rope_b[:, :, :], ALU.add).then_inc(rotated, 1)

            def split_values(u, j):
                wait(pool, v_hi, u)
                nc.gpsimd.tensor_tensor(v[j][:, 1, 0:KC, :], v_raw[:, :, j, :], v[j][:, 0, 0:KC, :].bitcast(fp32), ALU.subtract)
                nc.gpsimd.tensor_tensor(v[j][:, 1, KC, :], v_new[j][:, :], v[j][:, 0, KC, :].bitcast(fp32), ALU.subtract).then_inc(v_ready, 1)

            def nothing(*_):
                pass

            def unit(u, j, b, attend_last, finish_last, follow, next_row, nxt):
                if follow:
                    front(u + 1, 1 - j)
                split_values(u, j)
                if j == 0 and next_row:
                    table(u + 2, next_of(b))

            def start():
                table(0, 0)

            loops(pool, start, front, unit, nothing)

        @block.vector
        def _(dve):
            dve.sem_inc(mask_ready, 1)
            dve.sem_inc(x_ready, 1)
            before_first(dve, [summed, ms_ready, qn_ready, ktc_evac, newmax, masked, total, inverse,
                               scaled, p_lo_evac, qt_evac, o_ready, out_evac])

            def prepare(g, groups):
                for n in groups:
                    dve.wait_ge(wt_hi, g * GROUPS + n + 1)
                    w = place_of_weights(n, wqT, wkvT, woT)
                    nc.vector.tensor_tensor(w[:, 1], weight_bank(n).rearrange("p (c t) -> p c t", c=C), w[:, 0].bitcast(fp32), ALU.subtract).then_inc(wt_lo, 1)

            def mean_squares(u):
                wait(dve, squared, u)
                nc.vector.tensor_reduce(ss[:, 0, :], sq[:, :, :], AX.X, ALU.add).then_inc(summed, 1)
                wait(dve, summed, u)
                wait(dve, inv_rms, u - 1)
                nc.vector.tensor_scalar(ss[:, 1, :], ss[:, 0, :], 1.0 / DH, EPS, ALU.mult, ALU.add).then_inc(ms_ready, 1)

            def normed(u):
                wait(dve, inv_rms, u)
                wait(dve, rotated, u - 1)
                nc.vector.tensor_tensor(qn[:, :, :], QK5, ss[:, 2, :].rearrange("p (h o) -> p h o", o=1).to_broadcast([P, 5, DH]), ALU.mult).then_inc(qn_ready, 1)

            def row_mask(u):
                dve.wait_ge(len_in, row_count(u, 16))
                wait(dve, masked, u - 1)
                nc.vector.tensor_scalar(mask[:, :], key_index, len_b[:, 0:1], NEG, ALU.is_ge, ALU.mult).then_inc(mask_ready, 1)

            def new_maxima(u):
                wait(dve, snew_filled, u)
                wait(dve, exp_done, u - 1)
                nc.vector.tensor_reduce(stat[:, 0, :], SNEW.rearrange("p (h k) -> p h k", h=REP), AX.X, ALU.max).then_inc(newmax, 1)
                wait(dve, newmax, u, 1)
                nc.vector.tensor_scalar(stat[:, 1, :], stat[:, 0, :], -SCALE, None, ALU.mult).then_inc(newmax, 1)
                wait(dve, newmax, u, 2)

            def maxima(u, h, s):
                wait(dve, pt_filled, u - 2)
                wait(dve, s_filled, u, h + 1)
                nc.vector.memset(unused[:, h:h + 1], 0.0)
                nc.vector.tensor_tensor_reduce(out=probs[s][:, h, 0:L], in0=bank(3 + h % 2), in1=mask[:, :], scale=-SCALE,
                                               scalar=stat[:, 1, h:h + 1], op0=ALU.add, op1=ALU.min,
                                               accum_out=stat[:, 2, h:h + 1]).then_inc(masked, 1)

            def inverse_sums(u):
                wait(dve, exp_done, u)
                nc.vector.tensor_tensor(sums[:, 2, :], sums[:, 0, :], sums[:, 1, :], ALU.add).then_inc(total, 1)
                wait(dve, total, u)
                nc.vector.reciprocal(sums[:, 3, :], sums[:, 2, :]).then_inc(inverse, 1)

            def scale_probs(u, heads, s):
                wait(dve, inverse, u)
                for h in heads:
                    nc.vector.tensor_scalar(probs[s][:, h, :], probs[s][:, h, :], sums[:, 3, h:h + 1], None, ALU.mult).then_inc(scaled, 1)

            def probs_out(u, c):
                wait(dve, p_hi_evac, u, c + 1)
                nc.vector.tensor_tensor(pT[c % 2][:, 1, :], PT[c % 2], pT[c % 2][:, 0, :].bitcast(fp32), ALU.subtract).then_inc(p_lo_evac, 1)

            def queries(u, s):
                wait(dve, qt_hi, u)
                nc.vector.tensor_tensor(kT[s][:, 1, L:KEYS], KTN, kT[s][:, 0, L:KEYS].bitcast(fp32), ALU.subtract)
                nc.vector.tensor_tensor(flat(qT[s][:, 1, :, :]), QT, flat(qT[s][:, 0, :, :]).bitcast(fp32), ALU.subtract).then_inc(qt_evac, 1)

            def output(u):
                wait(dve, o_hi, u)
                nc.vector.tensor_tensor(oT[:, 1, :], OUT, oT[:, 0, :].bitcast(fp32), ALU.subtract).then_inc(o_ready, 1)

            def add_out(u, b):
                wait(dve, out_filled, u)
                wait(dve, out_evac, u - 1)
                o = acc[:, bass.ds(b, 1), :].rearrange("p o d -> p (o d)")
                nc.vector.tensor_tensor(o, OUT, o, ALU.add).then_inc(out_evac, 1)

            def cached_keys(u, s):
                wait(dve, ktc_hi, u)
                nc.vector.tensor_tensor(kT[s][:, 1, 0:L], KTC, kT[s][:, 0, 0:L].bitcast(fp32), ALU.subtract).then_inc(ktc_evac, 1)

            def front(u, j, g, nxt):
                row_mask(u)
                prepare(g, OUT_GROUPS[0:2])
                mean_squares(u)
                cached_keys(u, j)
                prepare(g, OUT_GROUPS[2:3])
                normed(u)
                prepare(g, OUT_GROUPS[3:])
                queries(u, j)

            def tail(u, j, b, nxt):
                output(u - 1)
                for c in range(KC + 1):
                    probs_out(u, c)
                    if nxt is not None:
                        prepare(nxt, [6 + c])
                    if c == 0:
                        add_out(u - 1, b)
                output(u)
                if nxt is not None:
                    prepare(nxt, [11])
                add_out(u, b)

            def unit(u, j, b, attend_last, finish_last, follow, next_row, nxt):
                if nxt is not None:
                    prepare(nxt, [0, 1, 2])
                if finish_last:
                    output(u - 2)
                if nxt is not None:
                    prepare(nxt, [3])
                if follow:
                    mean_squares(u + 1)
                if attend_last:
                    probs_out(u - 1, 0)
                new_maxima(u)
                if j == 0:
                    wait_row(dve, mask_ready, u)
                maxima(u, 0, j)
                if follow:
                    normed(u + 1)
                if finish_last:
                    add_out(u - 2, b - 1)
                maxima(u, 1, j)
                for c in range(1, KC + 1):
                    if attend_last:
                        probs_out(u - 1, c)
                    if c == 3 and j == 0 and next_row:
                        split_x(u + 2)
                    if c < 3:
                        maxima(u, 1 + c, j)
                    if c == 2 and follow:
                        cached_keys(u + 1, 1 - j)
                    if c in (2, 3) and nxt is not None:
                        prepare(nxt, [2 + c])
                    if c == 3 and follow:
                        queries(u + 1, 1 - j)
                inverse_sums(u)
                scale_probs(u, range(REP), j)
                if j == 1 and follow:
                    row_mask(u + 1)

            def split_x(u):
                wait_row(dve, x_hi, u)
                nc.vector.tensor_tensor(xb[:, 1, :, :], x_raw[:, :, :], xb[:, 0, :, :].bitcast(fp32), ALU.subtract).then_inc(x_ready, 1)

            def start():
                split_x(0)
                prepare(0, range(QKV_GROUPS))

            loops(dve, start, front, unit, tail)


_INS = ['x', 'itok_B_0_7', 'itok_B_2_6', 'itok_B_0_23', 'itok_Bx16_0_63', 'itok_B_207_1644', 'L0_cond_W', 'L0_cond_Wr', 'L0_cond_A',
        'L0_cond_B', 'L1_cond_W_gate', 'L1_cond_W_up', 'L1_cond_W_down', 'L1_cond_A_gate', 'L1_cond_B_gate', 'L1_cond_A_up',
        'L1_cond_B_up', 'L1_cond_A_down', 'L1_cond_B_down', 'L2_cond_W', 'L2_cond_b', 'L2_cond_lora_As', 'L2_cond_lora_Bs',
        'L3_cond_Wq', 'L3_cond_Wk', 'L3_cond_Wv', 'L3_cond_Wo', 'L3_cond_q_norm_w', 'L3_cond_k_norm_w', 'L3_cond_k_cache',
        'L3_cond_v_cache']


def kernel(**inputs):
    import numpy as _np
    import concourse.bacc as _bacc
    from concourse import mybir as _mybir
    from concourse.bass_utils import run_bass_kernel_spmd as _run

    nc = _bacc.Bacc("TRN2", target_bir_lowering=False, num_devices=1)
    arrays, args = {}, {}
    given = {name: _np.ascontiguousarray(inputs[name]) for name in _INS}
    given["shape_constants"] = constants()
    for name, x in given.items():
        arrays[f"in_{name}"] = x
        args[name] = nc.dram_tensor(f"in_{name}", x.shape, _mybir.dt.from_np(x.dtype), kind="ExternalInput").ap()
    out = nc.dram_tensor("out_0", (NB, T, D), _mybir.dt.float32, kind="ExternalOutput").ap()
    build(nc, args, out)
    r = _run(nc, [arrays], core_ids=[0])
    return r.results[0]["out_0"]
```
